# Optimizing a Trainium2 kernel written in Bass

```python
import numpy as np
import jax
import jax.numpy as jnp

def _softmax(x, axis=-1):
    return jax.nn.softmax(x, axis=axis)

def _gelu(x):
    return jax.nn.gelu(x, approximate=True)

def _silu(x):
    return jax.nn.silu(x)

def _sigmoid(x):
    return jax.nn.sigmoid(x)

def _layernorm(x, axis=-1, eps=1e-05):
    m = jnp.mean(x, axis=axis, keepdims=True)
    v = jnp.var(x, axis=axis, keepdims=True)
    return (x - m) / jnp.sqrt(v + eps)

def _scatter_add(tgt, idx, src, axis=0):
    return tgt.at[idx].add(src)

def _segment_sum(src, seg, n):
    return jax.ops.segment_sum(src, seg, n)
kernel_name = 'mk_xattn_seq_d4_seqx_r8_2d69d7'

def setup_inputs(seed: int=0):
    np.random.seed(seed)
    _w = jnp.asarray

    def _rec_inputs():
        import jax
        import jax.numpy as jnp
        _rk = jax.random.key(seed)
        x = 7.22e-05 + 1 * jax.random.normal(jax.random.fold_in(_rk, 1), (4, 512, 128), jnp.float32)
        _lenS = 512 - jax.random.randint(jax.random.fold_in(_rk, 7), (4,), 0, max(1, 512 // 4) + 1, jnp.int32)
        _lenS2 = 154 - jax.random.randint(jax.random.fold_in(_rk, 8), (4,), 0, max(1, 154 // 4) + 1, jnp.int32)
        _ctx_1024P = jax.random.normal(jax.random.fold_in(_rk, 11), (4, 16, 128), jnp.float32)
        _ctx_1024c = jax.random.dirichlet(jax.random.fold_in(_rk, 511), 0.3 * jnp.ones((16,), jnp.float32), (4, 154))
        _ctx_1024t = jnp.einsum('bsk,bkd->bsd', _ctx_1024c, _ctx_1024P)
        _ctx_1024t = _ctx_1024t * jax.lax.rsqrt(jnp.mean(jnp.square(_ctx_1024t)) + 1e-12) * 0.953939
        ctx_1024 = 4.13588e-05 + 0.999923 * (_ctx_1024t + 0.3 * jax.random.normal(jax.random.fold_in(_rk, 611), (4, 154, 128), jnp.float32))
        itok_BxS2_4_31999 = jax.random.randint(jax.random.fold_in(_rk, 12), (4, 154), 4, 4000, jnp.int32)
        _ctxb_2048x64P = jax.random.normal(jax.random.fold_in(_rk, 13), (4, 16, 64), jnp.float32)
        _ctxb_2048x64c = jax.random.dirichlet(jax.random.fold_in(_rk, 513), 0.3 * jnp.ones((16,), jnp.float32), (4, 154))
        _ctxb_2048x64t = jnp.einsum('bsk,bkd->bsd', _ctxb_2048x64c, _ctxb_2048x64P)
        _ctxb_2048x64t = _ctxb_2048x64t * jax.lax.rsqrt(jnp.mean(jnp.square(_ctxb_2048x64t)) + 1e-12) * 0.953939
        ctxb_2048x64 = 0.50053 + 0.288505 * (_ctxb_2048x64t + 0.3 * jax.random.normal(jax.random.fold_in(_rk, 613), (4, 154, 64), jnp.float32))
        return (x, ctx_1024, itok_BxS2_4_31999, ctxb_2048x64)
    x, ctx_1024, itok_BxS2_4_31999, ctxb_2048x64 = _rec_inputs()

    def _L0_xattn_setup():
        import jax, jax.numpy as jnp
        import numpy as np
        BATCH, T, H, S, P, NH = (4, 256, 128, 64, 64, 8)
        HD = H // NH

        def _layernorm(x, g, b):
            mu = jnp.mean(x, axis=-1, keepdims=True)
            var = jnp.mean((x - mu) ** 2, axis=-1, keepdims=True)
            return (x - mu) * jax.lax.rsqrt(var + 1e-05) * g + b

        def _mha(q_in, kv_in, W_qkv, b_qkv, W_o, b_o):
            Wq, Wk, Wv = jnp.split(W_qkv, 3, axis=0)
            bq, bk, bv = jnp.split(b_qkv, 3, axis=0)

            def heads(x, W, b):
                y = x @ W.T + b
                return y.reshape(y.shape[0], y.shape[1], NH, HD).transpose(0, 2, 1, 3)
            q, k, v = (heads(q_in, Wq, bq), heads(kv_in, Wk, bk), heads(kv_in, Wv, bv))
            scores = jnp.einsum('bhqd,bhkd->bhqk', q, k) * (1.0 / np.sqrt(HD))
            attn = jax.nn.softmax(scores, axis=-1)
            out = jnp.einsum('bhqk,bhkd->bhqd', attn, v)
            out = out.transpose(0, 2, 1, 3).reshape(q_in.shape)
            return out @ W_o.T + b_o
        key = jax.random.key(seed)
        ks = jax.random.split(key, 16)
        sH = 1.0 / np.sqrt(H)
        d = {}
        d['builder_state'] = jax.random.normal(ks[0], (BATCH, T, H), jnp.float32)
        d['base_state'] = jax.random.normal(ks[1], (BATCH, T, H), jnp.float32)
        d['input_ids'] = jax.random.randint(ks[2], (BATCH, T), 0, 4000)
        d['program_probs'] = jax.random.uniform(ks[3], (BATCH, T, P), jnp.float32)
        d['A'] = jax.random.normal(ks[4], (S, S), jnp.float32) * (0.5 / np.sqrt(S))
        d['Bmat'] = jax.random.normal(ks[5], (H, S), jnp.float32) * sH
        d['Cmat'] = jax.random.normal(ks[6], (S, H), jnp.float32) * (1.0 / np.sqrt(S))
        d['W_in'] = jax.random.normal(ks[7], (H, H), jnp.float32) * sH
        d['b_in'] = jnp.zeros((H,), jnp.float32)
        d['W_qkv'] = jax.random.normal(ks[8], (3 * H, H), jnp.float32) * sH
        d['b_qkv'] = jnp.zeros((3 * H,), jnp.float32)
        d['W_o'] = jax.random.normal(ks[9], (H, H), jnp.float32) * sH
        d['b_o'] = jnp.zeros((H,), jnp.float32)
        d['W_prog'] = jax.random.normal(ks[10], (H, P), jnp.float32) * (1.0 / np.sqrt(P))
        d['b_prog'] = jnp.zeros((H,), jnp.float32)
        d['g1'] = jnp.ones((H,), jnp.float32)
        d['beta1'] = jnp.zeros((H,), jnp.float32)
        d['g2'] = jnp.ones((H,), jnp.float32)
        d['beta2'] = jnp.zeros((H,), jnp.float32)
        return d
    _L0_xattn_all = _L0_xattn_setup()
    _L0_xattn_in = {k: v for k, v in _L0_xattn_all.items() if k in ('A', 'Bmat', 'Cmat', 'W_in', 'b_in', 'W_qkv', 'b_qkv', 'W_o', 'b_o', 'W_prog', 'b_prog', 'g1', 'beta1', 'g2', 'beta2')}
    del _L0_xattn_all

    def _L1_xattn_setup():
        import jax, jax.numpy as jnp
        import numpy as np
        D_MODEL = 128
        N_HEADS = 16
        D_K = D_MODEL // N_HEADS
        LN_EPS = 1e-05

        def _attention(query, key_value, W_qkv, b_qkv, W_o, b_o, ln_gamma, ln_beta):
            B, Sq, _ = query.shape
            Skv = key_value.shape[1]
            Wq, Wk, Wv = (W_qkv[:D_MODEL], W_qkv[D_MODEL:2 * D_MODEL], W_qkv[2 * D_MODEL:])
            bq, bk, bv = (b_qkv[:D_MODEL], b_qkv[D_MODEL:2 * D_MODEL], b_qkv[2 * D_MODEL:])
            Q = (query @ Wq.T + bq).reshape(B, Sq, N_HEADS, D_K).transpose(0, 2, 1, 3)
            K = (key_value @ Wk.T + bk).reshape(B, Skv, N_HEADS, D_K).transpose(0, 2, 1, 3)
            V = (key_value @ Wv.T + bv).reshape(B, Skv, N_HEADS, D_K).transpose(0, 2, 1, 3)
            scores = jnp.einsum('bhqd,bhkd->bhqk', Q.astype(jnp.float32), K.astype(jnp.float32))
            scores = scores / np.sqrt(D_K)
            attn = jax.nn.softmax(scores, axis=-1)
            context = jnp.einsum('bhqk,bhkd->bhqd', attn, V.astype(jnp.float32)).astype(query.dtype)
            context = context.transpose(0, 2, 1, 3).reshape(B, Sq, D_MODEL)
            output = context @ W_o.T + b_o
            x = output + query
            mu = jnp.mean(x, axis=-1, keepdims=True)
            var = jnp.mean(jnp.square(x - mu), axis=-1, keepdims=True)
            return (x - mu) / jnp.sqrt(var + LN_EPS) * ln_gamma + ln_beta
        key = jax.random.key(seed)
        ks = jax.random.split(key, 8)
        B, Sq, Skv = (2, 256, 256)
        scale = 1.0 / np.sqrt(D_MODEL)
        return {'query': jax.random.normal(ks[0], (B, Sq, D_MODEL), dtype=jnp.float32), 'key_value': jax.random.normal(ks[1], (B, Skv, D_MODEL), dtype=jnp.float32), 'W_qkv': jax.random.normal(ks[2], (3 * D_MODEL, D_MODEL), dtype=jnp.float32) * scale, 'b_qkv': jax.random.normal(ks[3], (3 * D_MODEL,), dtype=jnp.float32) * 0.01, 'W_o': jax.random.normal(ks[4], (D_MODEL, D_MODEL), dtype=jnp.float32) * scale, 'b_o': jax.random.normal(ks[5], (D_MODEL,), dtype=jnp.float32) * 0.01, 'ln_gamma': jnp.ones((D_MODEL,), dtype=jnp.float32), 'ln_beta': jnp.zeros((D_MODEL,), dtype=jnp.float32)}
    _L1_xattn_all = _L1_xattn_setup()
    _L1_xattn_in = {k: v for k, v in _L1_xattn_all.items() if k in ('W_qkv', 'b_qkv', 'W_o', 'b_o', 'ln_gamma', 'ln_beta')}
    del _L1_xattn_all

    def _L2_xattn_setup():
        import jax, jax.numpy as jnp
        import numpy as np
        DIM = 128
        HEADS = 16
        HEAD_DIM = DIM // HEADS
        HIDDEN = int(DIM * 4.0)
        SCALE = HEAD_DIM ** (-0.5)
        EPS = 1e-05

        def _ln(x, g, b):
            m = jnp.mean(x, axis=-1, keepdims=True)
            v = jnp.mean((x - m) ** 2, axis=-1, keepdims=True)
            return (x - m) * jax.lax.rsqrt(v + EPS) * g + b

        def _split_heads(t, B, N):
            return t.reshape(B, N, HEADS, HEAD_DIM).transpose(0, 2, 1, 3)
        key = jax.random.key(seed)
        ks = jax.random.split(key, 16)
        B, Nt, Ni = (4, 128, 72)
        s = lambda fan_in: 1.0 / np.sqrt(fan_in)
        return {'x': jax.random.normal(ks[0], (B, Nt, DIM), jnp.float32), 'encoder_hidden_state': jax.random.normal(ks[1], (B, Ni, DIM), jnp.float32), 'ln1_g': jnp.ones((DIM,), jnp.float32), 'ln1_b': jnp.zeros((DIM,), jnp.float32), 'w_qkv': jax.random.uniform(ks[2], (3 * DIM, DIM), jnp.float32, -s(DIM), s(DIM)), 'w_prj1': jax.random.uniform(ks[3], (DIM, DIM), jnp.float32, -s(DIM), s(DIM)), 'b_prj1': jnp.zeros((DIM,), jnp.float32), 'ln2_g': jnp.ones((DIM,), jnp.float32), 'ln2_b': jnp.zeros((DIM,), jnp.float32), 'w_q': jax.random.uniform(ks[4], (DIM, DIM), jnp.float32, -s(DIM), s(DIM)), 'w_kv': jax.random.uniform(ks[5], (2 * DIM, DIM), jnp.float32, -s(DIM), s(DIM)), 'w_prj2': jax.random.uniform(ks[6], (DIM, DIM), jnp.float32, -s(DIM), s(DIM)), 'b_prj2': jnp.zeros((DIM,), jnp.float32), 'ln3_g': jnp.ones((DIM,), jnp.float32), 'ln3_b': jnp.zeros((DIM,), jnp.float32), 'w_fc1': jax.random.uniform(ks[7], (HIDDEN, DIM), jnp.float32, -s(DIM), s(DIM)), 'b_fc1': jnp.zeros((HIDDEN,), jnp.float32), 'w_fc2': jax.random.uniform(ks[8], (DIM, HIDDEN), jnp.float32, -s(HIDDEN), s(HIDDEN)), 'b_fc2': jnp.zeros((DIM,), jnp.float32)}
    _L2_xattn_all = _L2_xattn_setup()
    _L2_xattn_in = {k: v for k, v in _L2_xattn_all.items() if k in ('ln1_g', 'ln1_b', 'w_qkv', 'w_prj1', 'b_prj1', 'ln2_g', 'ln2_b', 'w_q', 'w_kv', 'w_prj2', 'b_prj2', 'ln3_g', 'ln3_b', 'w_fc1', 'b_fc1', 'w_fc2', 'b_fc2')}
    del _L2_xattn_all

    def _L3_xattn_setup():
        import jax, jax.numpy as jnp
        import numpy as np
        B, T, E = (4, 256, 128)
        H, HS = (16, 64)
        EPS = 1e-05

        def _layernorm(x, g, b):
            mu = jnp.mean(x, axis=-1, keepdims=True)
            var = jnp.mean(jnp.square(x - mu), axis=-1, keepdims=True)
            return (x - mu) * jax.lax.rsqrt(var + EPS) * g + b
        key = jax.random.key(seed)
        ks = jax.random.split(key, 8)
        q = jax.random.normal(ks[0], (B, T, E), dtype=jnp.float32)
        s_in = 1.0 / np.sqrt(E)
        s_o = 1.0 / np.sqrt(H * HS)
        return {'q': q, 'kv': q, 'ln_g': jnp.ones((E,), jnp.float32), 'ln_b': jnp.zeros((E,), jnp.float32), 'wq': jax.random.uniform(ks[1], (E, H * HS), jnp.float32, -s_in, s_in), 'bq': jax.random.uniform(ks[2], (H * HS,), jnp.float32, -s_in, s_in), 'wkv': jax.random.uniform(ks[3], (E, 2 * H * HS), jnp.float32, -s_in, s_in), 'bkv': jax.random.uniform(ks[4], (2 * H * HS,), jnp.float32, -s_in, s_in), 'wo': jax.random.uniform(ks[5], (H * HS, E), jnp.float32, -s_o, s_o), 'bo': jax.random.uniform(ks[6], (E,), jnp.float32, -s_o, s_o)}
    _L3_xattn_all = _L3_xattn_setup()
    _L3_xattn_in = {k: v for k, v in _L3_xattn_all.items() if k in ('ln_g', 'ln_b', 'wq', 'bq', 'wkv', 'bkv', 'wo', 'bo')}
    del _L3_xattn_all
    return {'x': x, 'ctx_1024': ctx_1024, 'itok_BxS2_4_31999': itok_BxS2_4_31999, 'ctxb_2048x64': ctxb_2048x64, 'L0_xattn_A': _L0_xattn_in['A'], 'L0_xattn_Bmat': _L0_xattn_in['Bmat'], 'L0_xattn_Cmat': _L0_xattn_in['Cmat'], 'L0_xattn_W_in': _L0_xattn_in['W_in'], 'L0_xattn_b_in': _L0_xattn_in['b_in'], 'L0_xattn_W_qkv': _L0_xattn_in['W_qkv'], 'L0_xattn_b_qkv': _L0_xattn_in['b_qkv'], 'L0_xattn_W_o': _L0_xattn_in['W_o'], 'L0_xattn_b_o': _L0_xattn_in['b_o'], 'L0_xattn_W_prog': _L0_xattn_in['W_prog'], 'L0_xattn_b_prog': _L0_xattn_in['b_prog'], 'L0_xattn_g1': _L0_xattn_in['g1'], 'L0_xattn_beta1': _L0_xattn_in['beta1'], 'L0_xattn_g2': _L0_xattn_in['g2'], 'L0_xattn_beta2': _L0_xattn_in['beta2'], 'L1_xattn_W_qkv': _L1_xattn_in['W_qkv'], 'L1_xattn_b_qkv': _L1_xattn_in['b_qkv'], 'L1_xattn_W_o': _L1_xattn_in['W_o'], 'L1_xattn_b_o': _L1_xattn_in['b_o'], 'L1_xattn_ln_gamma': _L1_xattn_in['ln_gamma'], 'L1_xattn_ln_beta': _L1_xattn_in['ln_beta'], 'L2_xattn_ln1_g': _L2_xattn_in['ln1_g'], 'L2_xattn_ln1_b': _L2_xattn_in['ln1_b'], 'L2_xattn_w_qkv': _L2_xattn_in['w_qkv'], 'L2_xattn_w_prj1': _L2_xattn_in['w_prj1'], 'L2_xattn_b_prj1': _L2_xattn_in['b_prj1'], 'L2_xattn_ln2_g': _L2_xattn_in['ln2_g'], 'L2_xattn_ln2_b': _L2_xattn_in['ln2_b'], 'L2_xattn_w_q': _L2_xattn_in['w_q'], 'L2_xattn_w_kv': _L2_xattn_in['w_kv'], 'L2_xattn_w_prj2': _L2_xattn_in['w_prj2'], 'L2_xattn_b_prj2': _L2_xattn_in['b_prj2'], 'L2_xattn_ln3_g': _L2_xattn_in['ln3_g'], 'L2_xattn_ln3_b': _L2_xattn_in['ln3_b'], 'L2_xattn_w_fc1': _L2_xattn_in['w_fc1'], 'L2_xattn_b_fc1': _L2_xattn_in['b_fc1'], 'L2_xattn_w_fc2': _L2_xattn_in['w_fc2'], 'L2_xattn_b_fc2': _L2_xattn_in['b_fc2'], 'L3_xattn_ln_g': _L3_xattn_in['ln_g'], 'L3_xattn_ln_b': _L3_xattn_in['ln_b'], 'L3_xattn_wq': _L3_xattn_in['wq'], 'L3_xattn_bq': _L3_xattn_in['bq'], 'L3_xattn_wkv': _L3_xattn_in['wkv'], 'L3_xattn_bkv': _L3_xattn_in['bkv'], 'L3_xattn_wo': _L3_xattn_in['wo'], 'L3_xattn_bo': _L3_xattn_in['bo']}

def reference(x, ctx_1024, itok_BxS2_4_31999, ctxb_2048x64, L0_xattn_A, L0_xattn_Bmat, L0_xattn_Cmat, L0_xattn_W_in, L0_xattn_b_in, L0_xattn_W_qkv, L0_xattn_b_qkv, L0_xattn_W_o, L0_xattn_b_o, L0_xattn_W_prog, L0_xattn_b_prog, L0_xattn_g1, L0_xattn_beta1, L0_xattn_g2, L0_xattn_beta2, L1_xattn_W_qkv, L1_xattn_b_qkv, L1_xattn_W_o, L1_xattn_b_o, L1_xattn_ln_gamma, L1_xattn_ln_beta, L2_xattn_ln1_g, L2_xattn_ln1_b, L2_xattn_w_qkv, L2_xattn_w_prj1, L2_xattn_b_prj1, L2_xattn_ln2_g, L2_xattn_ln2_b, L2_xattn_w_q, L2_xattn_w_kv, L2_xattn_w_prj2, L2_xattn_b_prj2, L2_xattn_ln3_g, L2_xattn_ln3_b, L2_xattn_w_fc1, L2_xattn_b_fc1, L2_xattn_w_fc2, L2_xattn_b_fc2, L3_xattn_ln_g, L3_xattn_ln_b, L3_xattn_wq, L3_xattn_bq, L3_xattn_wkv, L3_xattn_bkv, L3_xattn_wo, L3_xattn_bo):
    import jax
    import jax.numpy as jnp

    def _L0_xattn_ref(builder_state, base_state, input_ids, program_probs, A, Bmat, Cmat, W_in, b_in, W_qkv, b_qkv, W_o, b_o, W_prog, b_prog, g1, beta1, g2, beta2):
        import jax, jax.numpy as jnp
        import numpy as np
        BATCH, T, H, S, P, NH = (4, 256, 128, 64, 64, 8)
        HD = H // NH

        def _layernorm(x, g, b):
            mu = jnp.mean(x, axis=-1, keepdims=True)
            var = jnp.mean((x - mu) ** 2, axis=-1, keepdims=True)
            return (x - mu) * jax.lax.rsqrt(var + 1e-05) * g + b

        def _mha(q_in, kv_in, W_qkv, b_qkv, W_o, b_o):
            Wq, Wk, Wv = jnp.split(W_qkv, 3, axis=0)
            bq, bk, bv = jnp.split(b_qkv, 3, axis=0)

            def heads(x, W, b):
                y = x @ W.T + b
                return y.reshape(y.shape[0], y.shape[1], NH, HD).transpose(0, 2, 1, 3)
            q, k, v = (heads(q_in, Wq, bq), heads(kv_in, Wk, bk), heads(kv_in, Wv, bv))
            scores = jnp.einsum('bhqd,bhkd->bhqk', q, k) * (1.0 / np.sqrt(HD))
            attn = jax.nn.softmax(scores, axis=-1)
            out = jnp.einsum('bhqk,bhkd->bhqd', attn, v)
            out = out.transpose(0, 2, 1, 3).reshape(q_in.shape)
            return out @ W_o.T + b_o
        residual = builder_state
        x = _layernorm(builder_state, g1, beta1)
        base_n = _layernorm(base_state, g1, beta1)
        x = residual + _mha(x, base_n, W_qkv, b_qkv, W_o, b_o)
        residual = x
        xn = _layernorm(x, g2, beta2)
        U = (xn @ W_in.T + b_in) @ Bmat

        def step(s, u_t):
            s = jax.nn.silu(s @ A.T) + u_t
            return (s, s)
        _, states = jax.lax.scan(step, jnp.zeros((builder_state.shape[0], S), U.dtype), U.transpose(1, 0, 2))
        ssm_out = jnp.einsum('tbs,sh->bth', states, Cmat)
        x = residual + ssm_out
        mod = program_probs.mean(axis=1) @ W_prog.T + b_prog
        return x + mod[:, None, :]

    def _L1_xattn_ref(query, key_value, W_qkv, b_qkv, W_o, b_o, ln_gamma, ln_beta):
        import jax, jax.numpy as jnp
        import numpy as np
        D_MODEL = 128
        N_HEADS = 16
        D_K = D_MODEL // N_HEADS
        LN_EPS = 1e-05

        def _attention(query, key_value, W_qkv, b_qkv, W_o, b_o, ln_gamma, ln_beta):
            B, Sq, _ = query.shape
            Skv = key_value.shape[1]
            Wq, Wk, Wv = (W_qkv[:D_MODEL], W_qkv[D_MODEL:2 * D_MODEL], W_qkv[2 * D_MODEL:])
            bq, bk, bv = (b_qkv[:D_MODEL], b_qkv[D_MODEL:2 * D_MODEL], b_qkv[2 * D_MODEL:])
            Q = (query @ Wq.T + bq).reshape(B, Sq, N_HEADS, D_K).transpose(0, 2, 1, 3)
            K = (key_value @ Wk.T + bk).reshape(B, Skv, N_HEADS, D_K).transpose(0, 2, 1, 3)
            V = (key_value @ Wv.T + bv).reshape(B, Skv, N_HEADS, D_K).transpose(0, 2, 1, 3)
            scores = jnp.einsum('bhqd,bhkd->bhqk', Q.astype(jnp.float32), K.astype(jnp.float32))
            scores = scores / np.sqrt(D_K)
            attn = jax.nn.softmax(scores, axis=-1)
            context = jnp.einsum('bhqk,bhkd->bhqd', attn, V.astype(jnp.float32)).astype(query.dtype)
            context = context.transpose(0, 2, 1, 3).reshape(B, Sq, D_MODEL)
            output = context @ W_o.T + b_o
            x = output + query
            mu = jnp.mean(x, axis=-1, keepdims=True)
            var = jnp.mean(jnp.square(x - mu), axis=-1, keepdims=True)
            return (x - mu) / jnp.sqrt(var + LN_EPS) * ln_gamma + ln_beta
        return _attention(query, key_value, W_qkv, b_qkv, W_o, b_o, ln_gamma, ln_beta)

    def _L2_xattn_ref(x, encoder_hidden_state, ln1_g, ln1_b, w_qkv, w_prj1, b_prj1, ln2_g, ln2_b, w_q, w_kv, w_prj2, b_prj2, ln3_g, ln3_b, w_fc1, b_fc1, w_fc2, b_fc2):
        import jax, jax.numpy as jnp
        import numpy as np
        DIM = 128
        HEADS = 16
        HEAD_DIM = DIM // HEADS
        HIDDEN = int(DIM * 4.0)
        SCALE = HEAD_DIM ** (-0.5)
        EPS = 1e-05

        def _ln(x, g, b):
            m = jnp.mean(x, axis=-1, keepdims=True)
            v = jnp.mean((x - m) ** 2, axis=-1, keepdims=True)
            return (x - m) * jax.lax.rsqrt(v + EPS) * g + b

        def _split_heads(t, B, N):
            return t.reshape(B, N, HEADS, HEAD_DIM).transpose(0, 2, 1, 3)
        B, Nt, C = x.shape
        Ni = encoder_hidden_state.shape[1]
        h = _ln(x, ln1_g, ln1_b)
        qkv = h @ w_qkv.T
        q, k, v = jnp.split(qkv, 3, axis=-1)
        q, k, v = (_split_heads(q, B, Nt), _split_heads(k, B, Nt), _split_heads(v, B, Nt))
        attn = jnp.einsum('bhqd,bhkd->bhqk', q, k) * SCALE
        causal = jnp.tril(jnp.ones((Nt, Nt), bool))
        attn = jnp.where(causal, attn, -jnp.inf)
        attn = jax.nn.softmax(attn, axis=-1)
        o = jnp.einsum('bhqk,bhkd->bhqd', attn, v).transpose(0, 2, 1, 3).reshape(B, Nt, C)
        x = x + o @ w_prj1.T + b_prj1
        h = _ln(x, ln2_g, ln2_b)
        q = _split_heads(h @ w_q.T, B, Nt)
        kv = encoder_hidden_state @ w_kv.T
        k, v = jnp.split(kv, 2, axis=-1)
        k, v = (_split_heads(k, B, Ni), _split_heads(v, B, Ni))
        attn = jnp.einsum('bhqd,bhkd->bhqk', q, k) * SCALE
        attn = jax.nn.softmax(attn, axis=-1)
        o = jnp.einsum('bhqk,bhkd->bhqd', attn, v).transpose(0, 2, 1, 3).reshape(B, Nt, C)
        x = x + o @ w_prj2.T + b_prj2
        h = _ln(x, ln3_g, ln3_b)
        h = jax.nn.gelu(h @ w_fc1.T + b_fc1, approximate=False)
        x = x + h @ w_fc2.T + b_fc2
        return x

    def _L3_xattn_ref(q, kv, ln_g, ln_b, wq, bq, wkv, bkv, wo, bo):
        import jax, jax.numpy as jnp
        import numpy as np
        B, T, E = (4, 256, 128)
        H, HS = (16, 64)
        EPS = 1e-05

        def _layernorm(x, g, b):
            mu = jnp.mean(x, axis=-1, keepdims=True)
            var = jnp.mean(jnp.square(x - mu), axis=-1, keepdims=True)
            return (x - mu) * jax.lax.rsqrt(var + EPS) * g + b
        oq = q
        qn = _layernorm(q, ln_g, ln_b)
        kvn = _layernorm(kv, ln_g, ln_b)
        b, qT, _ = q.shape
        kvT = kv.shape[1]
        qp = (qn @ wq + bq).reshape(b, qT, H, HS).transpose(0, 2, 1, 3)
        kvp = kvn @ wkv + bkv
        kp, vp = jnp.split(kvp, 2, axis=-1)
        kp = kp.reshape(b, kvT, H, HS).transpose(0, 2, 1, 3)
        vp = vp.reshape(b, kvT, H, HS).transpose(0, 2, 1, 3)
        attn = jnp.einsum('bhqd,bhkd->bhqk', qp, kp) / jnp.sqrt(jnp.float32(HS))
        causal = jnp.tril(jnp.ones((qT, kvT), dtype=bool))
        attn = jnp.where(causal, attn, -jnp.inf)
        attn = jax.nn.softmax(attn, axis=-1)
        ctx = jnp.einsum('bhqk,bhkd->bhqd', attn, vp)
        ctx = ctx.transpose(0, 2, 1, 3).reshape(b, qT, H * HS)
        out = ctx @ wo + bo + oq
        return out
    x = _L0_xattn_ref(x, ctx_1024, itok_BxS2_4_31999, ctxb_2048x64, L0_xattn_A, L0_xattn_Bmat, L0_xattn_Cmat, L0_xattn_W_in, L0_xattn_b_in, L0_xattn_W_qkv, L0_xattn_b_qkv, L0_xattn_W_o, L0_xattn_b_o, L0_xattn_W_prog, L0_xattn_b_prog, L0_xattn_g1, L0_xattn_beta1, L0_xattn_g2, L0_xattn_beta2)
    x = _L1_xattn_ref(x, ctx_1024, L1_xattn_W_qkv, L1_xattn_b_qkv, L1_xattn_W_o, L1_xattn_b_o, L1_xattn_ln_gamma, L1_xattn_ln_beta)
    x = _L2_xattn_ref(x, ctx_1024, L2_xattn_ln1_g, L2_xattn_ln1_b, L2_xattn_w_qkv, L2_xattn_w_prj1, L2_xattn_b_prj1, L2_xattn_ln2_g, L2_xattn_ln2_b, L2_xattn_w_q, L2_xattn_w_kv, L2_xattn_w_prj2, L2_xattn_b_prj2, L2_xattn_ln3_g, L2_xattn_ln3_b, L2_xattn_w_fc1, L2_xattn_b_fc1, L2_xattn_w_fc2, L2_xattn_b_fc2)
    x = _L3_xattn_ref(x, ctx_1024, L3_xattn_ln_g, L3_xattn_ln_b, L3_xattn_wq, L3_xattn_bq, L3_xattn_wkv, L3_xattn_bkv, L3_xattn_wo, L3_xattn_bo)
    return x

_drawn_inputs = setup_inputs


def setup_inputs(seed=0):
    import zlib

    import numpy as np

    out = dict(_drawn_inputs(seed))
    spreads = {'L0_xattn_b_in': (0.0, 0.1),
     'L0_xattn_b_qkv': (0.0, 0.1),
     'L0_xattn_b_o': (0.0, 0.1),
     'L0_xattn_b_prog': (0.0, 0.1),
     'L0_xattn_g1': (1.0, 0.2),
     'L0_xattn_beta1': (0.0, 0.1),
     'L0_xattn_g2': (1.0, 0.2),
     'L0_xattn_beta2': (0.0, 0.1),
     'L1_xattn_ln_gamma': (1.0, 0.2),
     'L1_xattn_ln_beta': (0.0, 0.1),
     'L2_xattn_ln1_g': (1.0, 0.539),
     'L2_xattn_ln1_b': (0.0, 0.1),
     'L2_xattn_b_prj1': (0.0, 0.1),
     'L2_xattn_ln2_g': (1.0, 0.6),
     'L2_xattn_ln2_b': (0.0, 0.8),
     'L2_xattn_b_prj2': (0.0, 0.1),
     'L2_xattn_ln3_g': (1.0, 0.2),
     'L2_xattn_ln3_b': (0.0, 0.495),
     'L2_xattn_b_fc1': (0.0, 0.1),
     'L2_xattn_b_fc2': (0.0, 0.1),
     'L3_xattn_ln_g': (1.0, 0.2),
     'L3_xattn_ln_b': (0.0, 0.281)}
    factors = {'L1_xattn_b_qkv': 8.0,
     'L1_xattn_b_o': 8.0,
     'L2_xattn_w_q': 2.807,
     'L3_xattn_bq': 31.161,
     'L3_xattn_bo': 3.516,
     'L3_xattn_bkv': 2.682}
    for name, (base, spread) in spreads.items():
        noise = np.random.default_rng([zlib.crc32(name.encode()), seed]).standard_normal(out[name].shape)
        drawn = base * np.exp(spread * noise) if base else spread * noise
        out[name] = jnp.asarray(drawn.astype(out[name].dtype))
    for name, factor in factors.items():
        out[name] = (out[name] * factor).astype(out[name].dtype)
    return out
```

```python
from contextlib import ExitStack

import numpy as np

import concourse.bass as bass
from concourse import mybir

F32 = mybir.dt.float32
BF16 = mybir.dt.bfloat16
ACT = mybir.ActivationFunctionType
ALU = mybir.AluOpType
AXX = mybir.AxisListType.X

B, T, D = 4, 512, 128
KV, KP = 154, 160
KL = KV - 128
C = 128
NCH = T // C
TOK = B * C
S = 64
HID = 512
EPS = 1e-5
HS3 = 64
E3 = 1024
BIG = -1.0e38
QPART = (0, 0, 0, 1, 1, 2)
KPART = (0, 1, 2, 0, 1, 0)
NCOMBO = len(QPART)


class Layer:

    def __init__(self, name, heads, hd, own_keys=False, causal=False):
        self.name, self.heads, self.hd = name, heads, hd
        self.own_keys, self.causal = own_keys, causal
        self.packs = heads // 4
        self.wide = hd == HS3
        self.per_tile = 1 if hd == 16 else 2

    def leftover(self, c):
        return not self.own_keys and not (self.causal and c == 0)

    def units(self, c):
        out = [("left", 0, 0)] if self.leftover(c) else []
        blocks = range(c + 1) if self.own_keys else range(1)
        return out + [("full", p, k) for p in range(self.packs) for k in blocks]

    def max_banks(self, c):
        n = self.keys(c)
        per = min(512 // n, self.heads)
        return [(h, min(per, self.heads - h)) for h in range(0, self.heads, per)]

    def keys(self, c):
        if self.own_keys:
            return (c + 1) * C
        return KV if self.leftover(c) else C

    def masked_block(self, c):
        if not self.causal:
            return None
        if self.own_keys:
            return c
        return 0 if c == 0 else None

    def masked_left(self, c):
        return self.causal and not self.own_keys and c == 1


L0 = Layer("L0", 8, 16)
L1 = Layer("L1", 16, 8)
L2S = Layer("L2S", 16, 8, own_keys=True, causal=True)
L2X = Layer("L2X", 16, 8)
L3 = Layer("L3", 16, HS3, causal=True)
ORDER = [L0, L1, L2S, L2X, L3]

PARAMS = [
    [("L0g1", 1), ("L0be1", 1), ("L0bq", 1), ("L0bk", 1),
     ("L0bv", 1), ("L0wq", 128), ("L0wk", 128), ("L0wv", 128), ("L0wo", 128), ("L0bo", 128),
     ("L0g2", 1), ("L0be2", 1), ("L0win", 128), ("L0bin", 1), ("L0bmat", S), ("L0at", S),
     ("L0cp", 128), ("L0bprog", 128)],
    [("ident", 128), ("ctxT", B * KP), ("L1bq", 1), ("L1bk", 1), ("L1bv", 1), ("L1wq", 128), ("L1wk", 128), ("L1wv", 128),
     ("L1wo", 128), ("L1bo", 128), ("L1g", 128), ("L1b", 128),
     ("L2g1", 1), ("L2b1", 1), ("L2g2", 1), ("L2b2", 1), ("L2g3", 1), ("L2b3", 1),
     ("L2Swq", 128), ("L2Swk", 128), ("L2Swv", 128), ("L2Swo", 128), ("L2Sbo", 128),
     ("L2Xwq", 128), ("L2Xwk", 128), ("L2Xwv", 128), ("L2Xwo", 128), ("L2Xbo", 128),
     ("fc1", HID), ("bfc1", HID // 128), ("fc2", HID), ("bfc2", 128)],
    [("L3g", 1), ("L3b", 1), ("L3wq", E3), ("L3bq", E3 // 128), ("L3wk", E3), ("L3bk", E3 // 128),
     ("L3wv", E3), ("L3bv", E3 // 128), ("L3wo", E3), ("L3bo", 128)],
]
EARLY = [("ctx", B * D), ("ctxl", B * D), ("probs", B * KV)]
CONSTS = [("identb", 128), ("maxsel", 16 * 128), ("leftsel", 4 * 128), ("mask", 128), ("maskT", 128), ("maskLT", 128)]


def columns(group):
    at, out = 0, {}
    for name, n in group:
        out[name] = (at, n)
        at += n
    return out, at


class Step:

    def __init__(self, kind, args, g0, g1, mx, u, f, l, o, nm, sp, ld, ln, xd, fi, op):
        self.kind, self.args = kind, args
        self.g0, self.g1, self.mx, self.u, self.f, self.l, self.o = g0, g1, mx, u, f, l, o
        self.nm, self.sp, self.ld, self.ln, self.xd, self.fi, self.op = nm, sp, ld, ln, xd, fi, op


def make_plan():
    count = dict.fromkeys("g0 g1 mx u f l o nm sp ld ln xd fi op".split(), 0)
    plan = []
    ended = {}
    closed = [0]

    def add(kind, *args, **events):
        plan.append(Step(kind, args, **count))
        for k, n in events.items():
            count[k] += n

    def split(layer, what, i):
        add("split", layer, what, i, sp=1, ld=layer.per_tile * NCOMBO)

    def front(layer, i, c):
        def norm():
            if layer is not L1:
                add("ln", "x", c, ln=1)

        def project():
            add("turn", layer, c, g0=1)
            if layer is L3:
                add("project3", c, g1=8)
                return
            add("project", layer, "q", g1=1)
            split(layer, "q", i)
            if layer.own_keys:
                add("project", layer, "k", g1=1)
                split(layer, "k", i)
                add("own_values", c, g0=1)
        return norm, project

    def key_prep(layer):
        if layer in (L0, L3):
            add("operand", layer, op=1)
        if layer is L3:
            add("keys3", g1=16)
        else:
            add("keys", layer, g1=2)
            split(layer, "k", 0)

    def value_prep(layer):
        add("values3" if layer is L3 else "values", layer, g0=12 if layer is L3 else 2)

    def attention(layer, i, c, hooks):
        n_banks = len(layer.max_banks(c))
        units = layer.units(c)

        def maxima(b, at, n):
            lo, hi = n_banks * at // n, n_banks * (at + 1) // n
            for m in range(lo, hi):
                add("max", layer, i, c, b, m, mx=1)

        maxima(0, 0, 1)
        add("negmax", layer, i, 0, nm=1)
        add("negmaxT", layer, 0, g1=1)
        held = None
        for b in range(B):
            for k, unit in enumerate(units):
                full = unit[0] == "full"
                add("score", layer, i, c, b, unit, u=1, f=int(full), l=int(not full))
                scored = plan[-1]
                if held is not None:
                    attend(layer, c, *held)
                if b + 1 < B:
                    maxima(b + 1, k, len(units))
                if not layer.wide:
                    if b and k == 1:
                        add("attended1", layer, b - 1, closed[0], g0=1)
                    if b and k == 2:
                        add("attended2", layer, b - 1, g1=1)
                held = (b, unit, scored)
            if b + 1 < B:
                add("negmax", layer, i, b + 1, nm=1)
                add("negmaxT", layer, b + 1, g1=1)
            for hook in hooks.get(b, []):
                hook()
        attend(layer, c, *held)
        ended[i] = count["f"]
        if not layer.wide:
            add("attended1", layer, B - 1, closed[0], g0=1)
            add("attended2", layer, B - 1, g1=1)

    def attend(layer, c, b, unit, scored):
        if unit[0] == "left":
            return
        _, p, k = unit
        last_block = k == (c if layer.own_keys else 0)
        last_pack = p == layer.packs - 1
        closes = last_block and (layer.wide or last_pack)
        opens = k == 0 and (layer.wide or p == 0)
        add("attend", layer, c, b, p, k, scored, opens, last_block, o=int(closes))
        if closes:
            closed[0] = scored.f + 1
        if layer.wide:
            add("weigh3", c, b, p, closed[0])
            if last_pack:
                for half in range(2):
                    add("turn3", b, half, g0=1)
                add("out3", c, b, g0=1, xd=1)

    def fill(name):
        add("fill", name, fi=1)

    fill("start")
    add("ln", "ctx", 0, ln=1)
    add("ctx_turn", 0, g0=1)
    add("ln", "ctxl", 0, ln=1)
    add("ctx_turn", 1, g0=1)
    key_prep(L0)
    value_prep(L0)

    def state_input(c):
        add("ln", "x", c, ln=1)
        add("turn", "u", c, g0=1)
        add("u1", g1=1)
        add("u2", c, g0=1)

    instances = [(layer, c) for layer in ORDER for c in range(NCH)]
    fronts = [front(layer, i, c) for i, (layer, c) in enumerate(instances)]
    fronts[0][0]()
    fronts[0][1]()
    for i, (layer, c) in enumerate(instances):
        hooks = {}
        ahead = i + 1 < len(instances) and not (layer is L0 and c == NCH - 1) \
            and not (layer is L2X and c == NCH - 1) and layer is not L3
        if ahead:
            hooks[0] = [fronts[i + 1][0]]
            hooks[1] = [fronts[i + 1][1]]
        if layer is L1 and c == 0:
            hooks[3] = [lambda: fill("own keys")]
            hooks[2] = [lambda: add("late_params")]
        if layer is L2S and c == 1:
            hooks[2] = [lambda: key_prep(L2X)]
            hooks[3] = [lambda: value_prep(L2X)]
        if layer is L2X and c == 0:
            hooks[2] = [lambda: fill("layer 3")]
            hooks[3] = [lambda: key_prep(L3)]
        attention(layer, i, c, hooks)
        if layer is not L3:
            add("back", layer, c, g0=1, xd=int(layer is not L1))
        if layer is L1:
            add("ln", "x", c, ln=1)
            add("affine", c, xd=1)
        if layer is L0:
            state_input(c)
        if layer is L0 and c == NCH - 1:
            fill("layer 1")
            key_prep(L1)
            value_prep(L1)
            add("scan")
            for k in range(NCH):
                add("state_out", k, g0=1, xd=1)
            fronts[i + 1][0]()
            fronts[i + 1][1]()
        if layer is L2X and c == NCH - 1:
            fill("layer 3 left")
            value_prep(L3)
            for k in range(NCH):
                add("ln", "x", k, ln=1)
                add("turn", "mlp", k, g0=1)
                add("mlp1", k, g1=4)
                add("mlp2", k, g0=1, xd=1)
            fronts[i + 1][0]()
            fronts[i + 1][1]()
        if layer is L3 and c < NCH - 1:
            fronts[i + 1][0]()
            fronts[i + 1][1]()
    return plan, dict(count), ended


def build(nc, x_dram, early_dram, params_dram, consts_dram, out_dram):
    plan, total, ended = make_plan()
    ctx = ExitStack()

    def sb(name, shape, dt=F32):
        return ctx.enter_context(nc.sbuf_tensor(name, shape, dt))

    def sem(name):
        return ctx.enter_context(nc.semaphore(name))

    with ctx:
        places = [columns(g) for g in PARAMS]
        shared = sb("params_0_and_2", [128, max(places[0][1], places[2][1])])
        par = [shared, sb("params_1", [128, places[1][1]]), shared]
        const_at, n_const = columns(CONSTS)
        con = sb("consts", [128, n_const], BF16)

        def P(name):
            for (at, _), t in zip(places, par):
                if name in at:
                    o, n = at[name]
                    return t[:, o:o + n]
            raise KeyError(name)

        def K(name):
            o, n = const_at[name]
            return con[:, o:o + n]

        X = sb("residual", [128, NCH, B, D])
        Z = sb("normed", [128, B, D])
        XT = sb("normedT", [128, TOK])
        QF = sb("projected", [128, B * KP])
        SPL = sb("parts", [128, 3, B * KP], BF16)
        QS = sb("query_stack", [128, 2, 8, TOK], BF16)
        Q3 = QS[:, :, :, :].rearrange("p a g n -> p (a g n)").bitcast(F32).rearrange("p (g n) -> p g n", g=8)
        KAW = sb("key_stack", [128, 16 * B * KP // 2])
        KA = KAW[:, :].bitcast(BF16).rearrange("p (h n) -> p h n", h=16)
        V3L = KAW[:, 0:B * 4 * 260].rearrange("p (b k n) -> p b k n", b=B, k=4)
        ARENA = sb("own_key_stack", [128, 16 * B * T // 2])
        KS = ARENA[:, :].bitcast(BF16).rearrange("p (c h n) -> p c h n", c=NCH, h=16)
        K3 = ARENA[:, 0:16 * B * KP].rearrange("p (h n) -> p h n", h=16)
        UT = ARENA[:, 0:T * B].rearrange("p (t b) -> p t b", b=B)
        ZT = ARENA[:, T * B:2 * T * B].rearrange("p (t b) -> p t b", b=B)
        SS = ARENA[:, 2 * T * B:3 * T * B].rearrange("p (b t) -> p b t", b=B)
        early_at, n_early = columns(EARLY)
        EA = ARENA[:, 3 * T * B:3 * T * B + n_early]

        def early(name):
            o, n = early_at[name]
            return EA[:, o:o + n].rearrange("p (b n) -> p b n", b=B)

        VW = sb("values", [128, B * 16 * 16 + B * 4 * 128])
        VA = VW[:, 0:B * 16 * 16].rearrange("p (b h n) -> p b h n", b=B, h=16)
        VAL = VW[:, B * 16 * 16:].rearrange("p (b k n) -> p b k n", b=B, k=4)
        CTX3 = VW[:, 0:E3]
        C3T = VW[:, E3:2 * E3].rearrange("p (t n) -> p t n", t=8)
        VAR = sb("values_arena", [128, B * 16 * 65])
        V0 = VAR[:, 0:B * 8 * 32].rearrange("p (b h n) -> p b h n", b=B, h=8)
        V0L = VAR[:, B * 8 * 32:2 * B * 8 * 32].rearrange("p (b k n) -> p b k n", b=B, k=2)
        VS = VAR[:, 0:B * NCH * 256].rearrange("p (b c h n) -> p b c h n", b=B, c=NCH, h=16)
        V3 = VAR[:, 0:B * 16 * 65].rearrange("p (b h n) -> p b h n", b=B, h=16)
        ZC = sb("normed_ctx", [128, B, KP])
        CT0, CT3 = VAR[:, 2 * B * 256:2 * B * 256 + B * KP].rearrange("p (b n) -> p b n", b=B), ZC
        PR = sb("probs", [128, 3, 512])
        PL = sb("probs_left", [128, 2, 512])
        OS = sb("attended", [128, 2, 512])
        CTK = sb("attended_tok", [128, 2, D])
        CXT = sb("attendedT", [128, TOK])
        NMX = sb("negmax", [128, 2, 16])
        NMR = sb("negmax_rest", [128, 16])
        NM3 = sb("negmax_parts", [128, 2, 128], BF16)
        NMT = sb("negmaxT", [128, 2, 128], BF16)
        REC = sb("reciprocals", [128, 16])
        ST = sb("stats", [128, B, 6])
        MV = sb("mean_var", [128, B, 2])
        RS = sb("rstd", [128, 3, B])
        PM = sb("probs_sum", [128, B])
        SB = sb("scaled_bias", [128, 16])
        parts_dram = nc.dram_tensor("parts_dram", [3, 128, B * KP], BF16).ap()

        banks = [ctx.enter_context(nc.psum_tensor(f"bank{i}", [128, 512], F32)) for i in range(8)]
        MB, SBK, OB, G0, G1 = banks[0:2], banks[2:4], banks[4:6], banks[6], banks[7]

        early_in, consts_in, x_in = sem("early_loaded"), sem("consts_loaded"), sem("x_loaded")
        par_in = [sem(f"params_loaded{i}") for i in range(3)]
        stored, stacked, out_done = sem("parts_stored"), sem("stack_loaded"), sem("output_stored")
        g0_full, g0_free = sem("g0_full"), sem("g0_free")
        g1_full, g1_free = sem("g1_full"), sem("g1_free")
        mx_full, mx_free = sem("max_scores_full"), sem("max_scores_free")
        nm_ready = sem("negmax_ready")
        s_full, p_ready, pv_done, o_free = sem("scores_full"), sem("probs_ready"), sem("probs_used"), sem("attended_free")
        dve_step, pool_step = sem("dve_step"), sem("pool_step")
        var_ready, rstd_ready, z_ready = sem("var_ready"), sem("rstd_ready"), sem("z_ready")
        split_ready, operand_ready, fills, x_done = sem("split_ready"), sem("operand_ready"), sem("fills"), sem("x_done")
        bias_ready = sem("scaled_bias_ready")
        au_ready, silu_ready, y_ready, states_ready = sem("au_ready"), sem("silu_ready"), sem("y_ready"), sem("states_ready")

        def wait(eng, s, n):
            if n > 0:
                eng.wait_ge(s, n)

        def group(name):
            return next(i for i, (at, _) in enumerate(places) if name in at)

        def last_use(layer):
            return {L0: 0, L1: ended.get(NCH - 1), L2X: ended.get(2 * NCH - 1)}[layer]

        def q_op(layer, i, h, b):
            t = h // layer.per_tile
            src = Q3[:, h // 2, :] if layer.wide else QS[:, i % 2, t, :]
            return src[:, b * C:(b + 1) * C]

        def k_op(layer, h, b, lo, n):
            if layer.wide:
                return K3[:, h, b * KP + lo:b * KP + lo + n]
            if layer.own_keys:
                return KS[:, lo // C:(lo + n) // C, h, b * C:(b + 1) * C]
            return KA[:, h, b * KP + lo:b * KP + lo + n]

        def v_ops(layer):
            return {L0: (V0, V0L), L1: (VA, VAL), L2X: (VA, VAL), L3: (V3, V3L)}[layer]

        block = ctx.enter_context(nc.Block())

        @block.sync
        def _(sp):
            sp.dma_start(EA[:, :], early_dram[:, :]).then_inc(early_in, 16)
            sp.dma_start(shared[:, 0:places[0][1]], params_dram[0][:, :]).then_inc(par_in[0], 16)
            sp.dma_start(par[1][:, :], params_dram[1][:, :]).then_inc(par_in[1], 16)
            sp.dma_start(con[:, :], consts_dram[:, :]).then_inc(consts_in, 16)
            for c in range(NCH):
                sp.dma_start(X[:, c, :, :], x_dram[:, c * C:(c + 1) * C, :].rearrange("b t f -> t b f")).then_inc(x_in, 16)
            for st in plan:
                if st.kind == "split":
                    layer, what, i = st.args
                    n = TOK if what == "q" or layer.own_keys else B * KP
                    rows = layer.hd
                    sp.wait_ge(split_ready, st.sp + 1)
                    wait(sp, stacked, 16 * st.ld)
                    sp.dma_start(parts_dram[:, :, 0:n].rearrange("s p n -> p s n"), SPL[:, :, 0:n]).then_inc(stored, 16)
                    sp.wait_ge(stored, 16 * (st.sp + 1))
                    wait(sp, fills, st.fi)
                    if what == "q":
                        wait(sp, pv_done, ended.get(i - 2, 0))
                    elif not layer.own_keys:
                        wait(sp, pv_done, last_use(layer))
                    for k in range(NCOMBO):
                        part = parts_dram[(QPART if what == "q" else KPART)[k], :, 0:n]
                        for a in range(layer.per_tile):
                            p0 = 64 * a + rows * k
                            src = part.rearrange("(g a d) n -> a d g n", a=layer.per_tile, d=rows)[a]
                            if what == "q":
                                dst = QS[p0:p0 + rows, i % 2, :, :]
                            elif layer.own_keys:
                                dst = KS[p0:p0 + rows, i % NCH, a::2, :]
                            elif layer.per_tile == 1:
                                dst = KA[p0:p0 + rows, 0:8, :]
                            else:
                                dst = KA[p0:p0 + rows, a::2, :]
                            sp.dma_start(dst, src).then_inc(stacked, 16)
                elif st.kind == "late_params":
                    sp.wait_ge(x_done, st.xd)
                    sp.wait_ge(g0_full, st.g0)
                    sp.wait_ge(g1_free, st.g1)
                    sp.dma_start(shared[:, 0:places[2][1]], params_dram[2][:, :]).then_inc(par_in[2], 16)
                elif st.kind == "out3":
                    c, b = st.args
                    sp.wait_ge(x_done, st.xd + 1)
                    sp.dma_start(out_dram[b, c * C:(c + 1) * C, :], X[:, c, b, :]).then_inc(out_done, 16)
            sp.wait_ge(out_done, 16 * NCH * B)

        @block.gpsimd
        def _(pool):
            steps = [0]

            def link(ins):
                steps[0] += 1
                ins.then_inc(pool_step, 1)
                pool.wait_ge(pool_step, steps[0])

            def put(out, value):
                link(nc.gpsimd.memset(out, value))

            def last_put(out, value, n):
                nc.gpsimd.memset(out, value).then_inc(fills, 1)
                pool.wait_ge(fills, n)

            def ones_left(t, at, width, stride):
                return [t[32 * j:32 * j + KL, :, :, j * stride + at:j * stride + at + width] for j in range(4)]

            for st in plan:
                if st.kind == "fill":
                    name, n = st.args[0], st.fi + 1
                    if name == "start":
                        put(RS[:, 2, :], -0.5)
                        put(NM3[:, :, :], 0.0)
                        put(QS[:, :, :, :].rearrange("p a g n -> p (a g n)").bitcast(F32), 0.0)
                        put(KAW[:, :], 0.0)
                        put(V0L[:, :, :, :], 0.0)
                        for ones in ones_left(V0L, 16, 16, 32):
                            put(ones, 1.0)
                        last_put(V0[:, :, :, 16:32], 1.0, n)
                    elif name == "layer 1":
                        pool.wait_ge(pv_done, st.f)
                        put(KAW[:, :], 0.0)
                        put(VA[:, :, :, :], 1.0)
                        put(VAL[:, :, :, :], 0.0)
                        for ones in ones_left(VAL, 8, 8, 32):
                            put(ones, 1.0)
                        pool.wait_ge(g0_free, st.g0)
                        last_put(ZT[0:S, 0, :], 0.0, n)
                    elif name == "own keys":
                        pool.wait_ge(g0_full, st.g0)
                        pool.wait_ge(x_done, st.xd)
                        pool.wait_ge(pv_done, st.f - 1)
                        put(VS[:, :, :, :, 8:16].rearrange("p b c h n -> p (b c h) n"), 1.0)
                        last_put(ARENA[:, :], 0.0, n)
                    elif name == "layer 3":
                        pool.wait_ge(pv_done, st.f - 3)
                        put(V3[:, :, :, 64:65], 1.0)
                        last_put(ARENA[:, 0:16 * B * KP], 0.0, n)
                    elif name == "layer 3 left":
                        pool.wait_ge(pv_done, st.f)
                        put(V3L[:, :, :, :], 0.0)
                        ones = ones_left(V3L, HS3, 1, 65)
                        for o in ones[:-1]:
                            put(o, 1.0)
                        last_put(ones[-1], 1.0, n)
                elif st.kind == "ln":
                    p = 32 if st.args[0] == "ctxl" else 128
                    if st.ln == 0:
                        pool.wait_ge(fills, 1)
                    pool.wait_ge(var_ready, st.ln + 1)
                    nc.gpsimd.tensor_tensor(RS[0:p, 1, :], RS[0:p, 0, :], RS[0:p, 2, :], ALU.pow).then_inc(rstd_ready, 1)

        @block.tensor
        def _(pe):
            def mm(out, lhsT, rhs, start=True, stop=True):
                return nc.tensor.matmul(out, lhsT, rhs, start=start, stop=stop, skip_group_check=True)

            def parameters(name):
                pe.wait_ge(par_in[group(name)], 16)

            def operand(layer):
                return P("ctxT").rearrange("p (b n) -> p b n", b=B) if layer in (L1, L2X) else CT0

            pe.wait_ge(consts_in, 16)
            parameters("ident")
            for st in plan:
                k = st.kind
                if k == "ctx_turn":
                    pe.wait_ge(z_ready, st.ln)
                    wait(pe, g0_free, st.g0)
                    n = 32 if st.args[0] else 128
                    for b in range(B):
                        ins = nc.tensor.transpose(G0[:, b * n:(b + 1) * n], Z[0:n, b, :], P("ident")[0:n, 0:n])
                    ins.then_inc(g0_full, 1)
                elif k == "turn":
                    what, c = st.args
                    pe.wait_ge(z_ready, st.ln)
                    pe.wait_ge(x_in, 16 * NCH)
                    wait(pe, x_done, st.xd)
                    pe.wait_ge(g0_free, st.g0)
                    for b in range(B):
                        src = X[:, c, b, :] if what is L1 else Z[:, b, :]
                        ins = nc.tensor.transpose(G0[:, b * C:(b + 1) * C], src, P("ident"))
                    ins.then_inc(g0_full, 1)
                elif k == "project":
                    layer, what = st.args
                    pe.wait_ge(g0_free, st.g0)
                    wait(pe, g1_free, st.g1)
                    parameters(f"{layer.name}w{what}")
                    mm(G1[:, :], P(f"{layer.name}w{what}"), XT[:, :]).then_inc(g1_full, 1)
                elif k == "own_values":
                    pe.wait_ge(g0_free, st.g0)
                    for b in range(B):
                        ins = mm(G0[:, b * D:(b + 1) * D], XT[:, b * C:(b + 1) * C], P("L2Swv"))
                    ins.then_inc(g0_full, 1)
                elif k == "project3":
                    pe.wait_ge(g0_free, st.g0)
                    parameters("L3wq")
                    for t in range(8):
                        pe.wait_ge(g1_free, st.g1 + t)
                        mm(G1[:, :], P("L3wq")[:, t * 128:(t + 1) * 128], XT[:, :]).then_inc(g1_full, 1)
                elif k == "keys":
                    layer = st.args[0]
                    wait(pe, operand_ready, st.op)
                    parameters(f"{layer.name}wk")
                    src = operand(layer).rearrange("p b n -> p (b n)")
                    for half in range(2):
                        wait(pe, g1_free, st.g1 + half)
                        mm(G1[:, 0:2 * KP], P(f"{layer.name}wk"), src[:, half * 2 * KP:(half + 1) * 2 * KP]).then_inc(g1_full, 1)
                elif k == "keys3":
                    pe.wait_ge(operand_ready, st.op)
                    parameters("L3wk")
                    src = CT3[:, :, :].rearrange("p b n -> p (b n)")
                    for t in range(8):
                        for half in range(2):
                            pe.wait_ge(g1_free, st.g1 + 2 * t + half)
                            mm(G1[:, 0:2 * KP], P("L3wk")[:, t * 128:(t + 1) * 128],
                               src[:, half * 2 * KP:(half + 1) * 2 * KP]).then_inc(g1_full, 1)
                elif k == "values":
                    layer = st.args[0]
                    src, w = operand(layer), P(f"{layer.name}wv")
                    wait(pe, g0_free, st.g0)
                    for b in range(B):
                        ins = mm(G0[:, b * D:(b + 1) * D], src[:, b, 0:128], w)
                    ins.then_inc(g0_full, 1)
                    pe.wait_ge(g0_free, st.g0 + 1)
                    n = layer.packs * layer.hd
                    for j in range(4):
                        wj = w.rearrange("p (k j d) -> p k j d", j=4, d=layer.hd)[:, :, j, :]
                        for b in range(B):
                            ins = mm(G0[32 * j:32 * j + 32, b * n:(b + 1) * n], src[:, b, 128:KP], wj)
                    ins.then_inc(g0_full, 1)
                elif k == "values3":
                    g = st.g0
                    w = P("L3wv")
                    for b in range(B):
                        for half in range(2):
                            pe.wait_ge(g0_free, g)
                            mm(G0[:, :], CT3[:, b, 0:128], w[:, half * 512:(half + 1) * 512]).then_inc(g0_full, 1)
                            g += 1
                        pe.wait_ge(g0_free, g)
                        for j in range(4):
                            wj = w.rearrange("p (k j d) -> p k j d", j=4, d=HS3)[:, :, j, :]
                            ins = mm(G0[32 * j:32 * j + 32, 0:256], CT3[:, b, 128:KP], wj)
                        ins.then_inc(g0_full, 1)
                        g += 1
                elif k == "max":
                    layer, i, c, b, m = st.args
                    h0, n_h = layer.max_banks(c)[m]
                    n = layer.keys(c)
                    if b == 0 and m == 0:
                        wait(pe, stacked, 16 * st.ld)
                        wait(pe, g1_free, st.g1)
                        wait(pe, fills, st.fi)
                    wait(pe, mx_free, st.mx - 1)
                    bank = MB[st.mx % 2]
                    for h in range(h0, h0 + n_h):
                        o = (h - h0) * n
                        q = q_op(layer, i, h, b)
                        out = bank[:, o:o + n]
                        if layer.own_keys:
                            out = out.rearrange("p (c t) -> p c t", t=C)
                        ins = mm(out, q, k_op(layer, h, b, 0, n))
                        if layer.masked_block(c) is not None:
                            ins = mm(bank[:, o + n - C:o + n], K("identb"), K("mask"), start=False)
                        elif layer.masked_left(c):
                            ins = mm(bank[:, o + C:o + n], K("identb"), K("mask")[:, 0:KL], start=False)
                    ins.then_inc(mx_full, 1)
                elif k == "negmaxT":
                    layer, b = st.args
                    pe.wait_ge(nm_ready, st.nm)
                    pe.wait_ge(g1_free, st.g1)
                    mm(G1[:, 0:C], NM3[:, b % 2, :], K("identb")).then_inc(g1_full, 1)
                elif k == "score":
                    layer, i, c, b, unit = st.args
                    kind, p, kb = unit
                    if unit == layer.units(c)[0]:
                        pe.wait_ge(g1_free, st.g1)
                    wait(pe, p_ready, st.u - 1)
                    bank = SBK[st.u % 2]
                    if kind == "left":
                        for p in range(layer.packs):
                            out = bank[:, p * C:(p + 1) * C]
                            mm(out, K("leftsel")[:, p * 128:(p + 1) * 128], NMT[:, b % 2, :], stop=False)
                            if layer.masked_left(c):
                                mm(out, K("identb"), K("maskLT"), start=False, stop=False)
                            for j in range(4):
                                h = 4 * p + j
                                ins = mm(out[32 * j:32 * j + 32, :], k_op(layer, h, b, 128, 32),
                                         q_op(layer, i, h, b), start=False)
                    else:
                        for j in range(4):
                            h = 4 * p + j
                            out = bank[:, j * C:(j + 1) * C]
                            keys = k_op(layer, h, b, kb * C, C)
                            mm(out, keys[:, 0, :] if layer.own_keys else keys, q_op(layer, i, h, b), stop=False)
                            if layer.masked_block(c) == kb:
                                mm(out, K("identb"), K("maskT"), start=False, stop=False)
                            ins = mm(out, K("maxsel")[:, h * 128:(h + 1) * 128], NMT[:, b % 2, :], start=False)
                    ins.then_inc(s_full, 1)
                elif k == "attend":
                    layer, c, b, p, kb, scored, opens, last = st.args
                    pe.wait_ge(p_ready, scored.u + 1)
                    if opens:
                        wait(pe, o_free, st.o - 1)
                        if b == 0:
                            pe.wait_ge(g0_free, st.g0)
                            wait(pe, fills, st.fi)
                    bank = OB[st.o % 2]
                    left = layer.leftover(c)
                    pr, pl = PR[:, scored.f % 3, :], PL[:, (scored.l - 1) % 2, p * C:(p + 1) * C]
                    if layer.own_keys:
                        v = VS[:, b, kb, :, :]
                    else:
                        v, vl = (t[:, b] for t in v_ops(layer))
                    if layer.wide:
                        if left:
                            mm(bank[:, 0:260], pl, vl[:, p, :], stop=False)
                        for j in range(4):
                            ins = mm(bank[:, 65 * j:65 * j + 65], pr[:, j * C:(j + 1) * C], v[:, 4 * p + j, :],
                                     start=not left)
                    else:
                        w = 2 * layer.hd
                        out = bank[:, p * C:(p + 1) * C]
                        if left:
                            mm(out, vl[:, p, :], pl, stop=False)
                        for j in range(4):
                            ins = mm(out[32 * j:32 * j + w, :], v[:, 4 * p + j, :], pr[:, j * C:(j + 1) * C],
                                     start=not left and kb == 0, stop=last)
                    ins.then_inc(pv_done, 1)
                elif k == "attended1":
                    layer, b, _ = st.args
                    pe.wait_ge(o_free, st.o)
                    pe.wait_ge(g0_free, st.g0)
                    for p in range(layer.packs):
                        ins = nc.tensor.transpose(G0[:, p * 128:(p + 1) * 128],
                                                  OS[:, (st.o - 1) % 2, p * C:(p + 1) * C], P("ident"))
                    ins.then_inc(g0_full, 1)
                elif k == "attended2":
                    layer, b = st.args
                    pe.wait_ge(g0_free, st.g0)
                    pe.wait_ge(g1_free, st.g1)
                    nc.tensor.transpose(G1[:, 0:C], CTK[:, b % 2, :], P("ident")).then_inc(g1_full, 1)
                elif k == "back":
                    layer, c = st.args
                    pe.wait_ge(g1_free, st.g1)
                    pe.wait_ge(g0_free, st.g0)
                    for b in range(B):
                        ins = mm(G0[:, b * D:(b + 1) * D], CXT[:, b * C:(b + 1) * C], P(f"{layer.name}wo"))
                    ins.then_inc(g0_full, 1)
                elif k == "u1":
                    pe.wait_ge(g0_free, st.g0)
                    pe.wait_ge(g1_free, st.g1)
                    mm(G1[:, :], P("L0win"), XT[:, :]).then_inc(g1_full, 1)
                elif k == "u2":
                    pe.wait_ge(g1_free, st.g1)
                    pe.wait_ge(g0_free, st.g0)
                    mm(G0[0:S, :], P("L0bmat"), QF[:, 0:TOK]).then_inc(g0_full, 1)
                elif k == "scan":
                    pe.wait_ge(g0_free, st.g0)
                    pe.wait_ge(mx_free, st.mx)
                    pe.wait_ge(fills, st.fi)

                    def inputs(c):
                        mm(MB[c % 2][0:S, :], P("L0at")[0:S, :],
                           UT[0:S, c * C:(c + 1) * C, :].rearrange("p t b -> p (t b)"), stop=False)

                    inputs(0)
                    for t in range(1, T):
                        c, col = divmod(t - 1, C)
                        if t > 1:
                            pe.wait_ge(silu_ready, t - 1)
                        mm(MB[c % 2][0:S, col * B:(col + 1) * B], P("L0at")[0:S, :], ZT[0:S, t - 1, :],
                           start=False).then_inc(y_ready, 1)
                        if col == C // 2 and c + 1 < NCH:
                            inputs(c + 1)
                elif k == "state_out":
                    c = st.args[0]
                    pe.wait_ge(states_ready, c + 1)
                    pe.wait_ge(g0_free, st.g0)
                    for b in range(B):
                        ins = mm(G0[:, b * D:(b + 1) * D], SS[:, b, c * C:(c + 1) * C], P("L0cp"))
                    ins.then_inc(g0_full, 1)
                elif k == "mlp1":
                    pe.wait_ge(g0_free, st.g0)
                    for j in range(4):
                        pe.wait_ge(g1_free, st.g1 + j)
                        mm(G1[:, :], P("fc1")[:, j * 128:(j + 1) * 128], XT[:, :]).then_inc(g1_full, 1)
                elif k == "mlp2":
                    c = st.args[0]
                    pe.wait_ge(g1_free, st.g1)
                    pe.wait_ge(g0_free, st.g0)
                    for b in range(B):
                        for j in range(4):
                            ins = mm(G0[:, b * D:(b + 1) * D], Q3[:, 4 * (c % 2) + j, b * C:(b + 1) * C],
                                     P("fc2")[:, j * 128:(j + 1) * 128], start=j == 0, stop=j == 3)
                    ins.then_inc(g0_full, 1)
                elif k == "turn3":
                    b, half = st.args
                    pe.wait_ge(o_free, st.o)
                    pe.wait_ge(g0_free, st.g0)
                    for t in range(4):
                        ins = nc.tensor.transpose(G0[:, t * C:(t + 1) * C],
                                                  CTX3[:, (4 * half + t) * 128:(4 * half + t + 1) * 128], P("ident"))
                    ins.then_inc(g0_full, 1)
                elif k == "out3":
                    c, b = st.args
                    pe.wait_ge(g0_free, st.g0)
                    for t in range(8):
                        ins = mm(G0[:, 0:D], C3T[:, t, :], P("L3wo")[:, t * 128:(t + 1) * 128], start=t == 0, stop=t == 7)
                    ins.then_inc(g0_full, 1)

        @block.scalar
        def _(act):
            def affine_copy(out, in_, bias=None, scale=1.0):
                if bias is None:
                    return nc.scalar.activation(out, in_, ACT.Copy, scale=scale)
                return nc.scalar.activation(out, in_, ACT.Identity, bias=bias, scale=scale)

            act.wait_ge(par_in[0], 16)
            act.wait_ge(par_in[1], 16)
            for st in plan:
                k = st.kind
                if k == "project":
                    layer, what = st.args
                    act.wait_ge(g1_full, st.g1 + 1)
                    wait(act, split_ready, st.sp)
                    wait(act, g0_full, st.g0)
                    bias = None
                    if layer is L0:
                        act.wait_ge(bias_ready, 1)
                        bias = SB[:, 0:1]
                    elif layer is L1:
                        act.wait_ge(bias_ready, 1)
                        bias = SB[:, 1:2]
                    affine_copy(QF[:, 0:TOK], G1[:, :], bias, float(layer.hd) ** -0.5 if what == "q" else 1.0)\
                        .then_inc(g1_free, 1)
                elif k == "project3":
                    act.wait_ge(pv_done, st.f)
                    act.wait_ge(g0_full, st.g0)
                    act.wait_ge(bias_ready, 2)
                    for t in range(8):
                        act.wait_ge(g1_full, st.g1 + t + 1)
                        affine_copy(Q3[:, t, :], G1[:, :], SB[:, 2 + t:3 + t], HS3 ** -0.5).then_inc(g1_free, 1)
                elif k == "keys":
                    layer = st.args[0]
                    wait(act, split_ready, st.sp)
                    wait(act, g0_full, st.g0)
                    for half in range(2):
                        act.wait_ge(g1_full, st.g1 + half + 1)
                        affine_copy(QF[:, half * 2 * KP:(half + 1) * 2 * KP], G1[:, 0:2 * KP],
                                    None if layer is L2X else P(f"{layer.name}bk")).then_inc(g1_free, 1)
                elif k == "keys3":
                    act.wait_ge(fills, st.fi)
                    act.wait_ge(par_in[2], 16)
                    for t in range(8):
                        for half in range(2):
                            act.wait_ge(g1_full, st.g1 + 2 * t + half + 1)
                            cols = slice(half * 2 * KP, (half + 1) * 2 * KP)
                            affine_copy(K3[0:64, 2 * t, cols], G1[0:64, 0:2 * KP], P("L3bk")[0:64, t:t + 1])
                            affine_copy(K3[64:128, 2 * t + 1, cols], G1[64:128, 0:2 * KP], P("L3bk")[64:128, t:t + 1])\
                                .then_inc(g1_free, 1)
                elif k == "negmaxT":
                    layer, b = st.args
                    act.wait_ge(g1_full, st.g1 + 1)
                    affine_copy(NMT[:, b % 2, :], G1[:, 0:C]).then_inc(g1_free, 1)
                elif k == "score":
                    layer, i, c, b, unit = st.args
                    act.wait_ge(s_full, st.u + 1)
                    if unit[0] == "left":
                        wait(act, pv_done, st.f - layer.packs)
                        w = layer.packs * C
                        out = PL[:, st.l % 2, 0:w]
                    else:
                        wait(act, pv_done, st.f - 2)
                        w = 512
                        out = PR[:, st.f % 3, :]
                    nc.scalar.activation(out, SBK[st.u % 2][:, 0:w], ACT.Exp).then_inc(p_ready, 1)
                elif k == "attended1":
                    layer, b, closed = st.args
                    act.wait_ge(pv_done, closed)
                    w = layer.packs * C
                    affine_copy(OS[:, (st.o - 1) % 2, 0:w], OB[(st.o - 1) % 2][:, 0:w]).then_inc(o_free, 1)
                elif k == "attended2":
                    layer, b = st.args
                    act.wait_ge(g1_full, st.g1 + 1)
                    bias = P(f"{layer.name}bv") if layer in (L0, L1) else None
                    affine_copy(CXT[:, b * C:(b + 1) * C], G1[:, 0:C], bias).then_inc(g1_free, 1)
                elif k == "u1":
                    act.wait_ge(g1_full, st.g1 + 1)
                    act.wait_ge(split_ready, st.sp)
                    act.wait_ge(g0_full, st.g0)
                    affine_copy(QF[:, 0:TOK], G1[:, :], P("L0bin")).then_inc(g1_free, 1)
                elif k == "scan":
                    for t in range(1, T):
                        c, col = divmod(t - 1, C)
                        act.wait_ge(y_ready, t)
                        nc.scalar.activation(ZT[0:S, t, :], MB[c % 2][0:S, col * B:(col + 1) * B], ACT.Silu)\
                            .then_inc(silu_ready, 1)
                elif k == "mlp1":
                    c = st.args[0]
                    act.wait_ge(pv_done, st.f)
                    act.wait_ge(g0_full, st.g0)
                    for j in range(4):
                        act.wait_ge(g1_full, st.g1 + j + 1)
                        nc.scalar.activation(Q3[:, 4 * (c % 2) + j, :], G1[:, :], ACT.Gelu, bias=P("bfc1")[:, j:j + 1])\
                            .then_inc(g1_free, 1)

        @block.vector
        def _(dve):
            steps = [0]

            def link(ins):
                steps[0] += 1
                ins.then_inc(dve_step, 1)
                dve.wait_ge(dve_step, steps[0])

            def over_batches(row):
                return row.unsqueeze(1).broadcast_to([128, B, D])

            def split3(parts, x, rest):
                link(nc.vector.tensor_copy(parts[0], x))
                link(nc.vector.tensor_tensor(rest, x, parts[0], ALU.subtract))
                link(nc.vector.tensor_copy(parts[1], rest))
                return nc.vector.tensor_tensor(parts[2], rest, parts[1], ALU.subtract)

            dve.wait_ge(early_in, 16)
            dve.wait_ge(par_in[0], 16)
            dve.wait_ge(par_in[1], 16)
            nc.vector.tensor_scalar(SB[:, 1:2], P("L1bq"), L1.hd ** -0.5, None, ALU.mult)
            nc.vector.tensor_scalar(SB[:, 0:1], P("L0bq"), L0.hd ** -0.5, None, ALU.mult).then_inc(bias_ready, 1)
            link(nc.vector.tensor_reduce(PM[S:128, :], early("probs")[S:128, :, :], AXX, ALU.add))
            link(nc.vector.tensor_scalar(SS[S:128, :, :], PM[S:128, :].unsqueeze(2).broadcast_to([S, B, T]),
                                         1.0 / KV, None, ALU.mult))
            for st in plan:
                k = st.kind
                if k == "ln":
                    what, c = st.args
                    p = 32 if what == "ctxl" else 128
                    src = X[:, c, :, :] if what == "x" else early(what)
                    if what == "x":
                        dve.wait_ge(x_in, 16 * NCH)
                        wait(dve, x_done, st.xd)
                    for b in range(B):
                        ins = nc.vector.bn_stats(ST[0:p, b, :], src[0:p, b, :])
                    link(ins)
                    for b in range(B):
                        ins = nc.vector.bn_aggr(MV[0:p, b, :], ST[0:p, b, :])
                    link(ins)
                    nc.vector.tensor_scalar(RS[0:p, 0, :], MV[0:p, :, 1], EPS, None, ALU.add).then_inc(var_ready, 1)
                    dve.wait_ge(rstd_ready, st.ln + 1)
                    wait(dve, g0_full, st.g0)
                    for b in range(B):
                        ins = nc.vector.tensor_scalar(Z[0:p, b, :], src[0:p, b, :], MV[0:p, b, 0:1], RS[0:p, 1, b:b + 1],
                                                      ALU.subtract, ALU.mult)
                    ins.then_inc(z_ready, 1)
                elif k == "ctx_turn":
                    dve.wait_ge(g0_full, st.g0 + 1)
                    n, o = (32, 128) if st.args[0] else (128, 0)
                    nc.vector.tensor_copy(ZC[:, :, o:o + n], G0[:, 0:B * n].rearrange("p (b n) -> p b n", b=B))\
                        .then_inc(g0_free, 1)
                elif k == "operand":
                    layer = st.args[0]
                    g, be = ("L0g1", "L0be1") if layer is L0 else ("L3g", "L3b")
                    dve.wait_ge(g0_free, st.g0)
                    dve.wait_ge(par_in[group(g)], 16)
                    if layer is L3:
                        for t in range(8):
                            ins = nc.vector.tensor_scalar(SB[:, 2 + t:3 + t], P("L3bq")[:, t:t + 1], HS3 ** -0.5, None, ALU.mult)
                        ins.then_inc(bias_ready, 1)
                    nc.vector.tensor_scalar((CT0 if layer is L0 else CT3)[:, :, :], ZC[:, :, :], P(g), P(be), ALU.mult, ALU.add).then_inc(operand_ready, 1)
                elif k == "turn":
                    what, c = st.args
                    dve.wait_ge(g0_full, st.g0 + 1)
                    wait(dve, g1_full, st.g1)
                    if what is L1:
                        nc.vector.tensor_copy(XT[:, :], G0[:, :]).then_inc(g0_free, 1)
                    else:
                        g, be = {L0: ("L0g1", "L0be1"), "u": ("L0g2", "L0be2"), L2S: ("L2g1", "L2b1"),
                                 L2X: ("L2g2", "L2b2"), "mlp": ("L2g3", "L2b3"), L3: ("L3g", "L3b")}[what]
                        nc.vector.tensor_scalar(XT[:, :], G0[:, :], P(g), P(be), ALU.mult, ALU.add).then_inc(g0_free, 1)
                elif k == "split":
                    layer, what, i = st.args
                    n = TOK if what == "q" or layer.own_keys else B * KP
                    dve.wait_ge(g1_free, st.g1)
                    wait(dve, stored, 16 * st.sp)
                    split3([SPL[:, s, 0:n] for s in range(3)], QF[:, 0:n], QF[:, 0:n]).then_inc(split_ready, 1)
                elif k == "own_values":
                    c = st.args[0]
                    dve.wait_ge(g0_full, st.g0 + 1)
                    dve.wait_ge(fills, st.fi)
                    nc.vector.tensor_copy(VS[:, :, c, :, 0:8], G0[:, :].rearrange("p (b h n) -> p b h n", b=B, h=16))\
                        .then_inc(g0_free, 1)
                elif k == "values":
                    layer = st.args[0]
                    v, vl = v_ops(layer)
                    hd, n = layer.hd, layer.packs * layer.hd
                    dve.wait_ge(fills, st.fi)
                    wait(dve, pv_done, last_use(layer))
                    dve.wait_ge(g0_full, st.g0 + 1)
                    nc.vector.tensor_copy(v[:, :, :, 0:hd], G0[:, :].rearrange("p (b h n) -> p b h n", b=B, n=hd))\
                        .then_inc(g0_free, 1)
                    dve.wait_ge(g0_full, st.g0 + 2)
                    for j in range(4):
                        r = slice(32 * j, 32 * j + KL)
                        ins = nc.vector.tensor_copy(vl[r, :, :, 32 * j:32 * j + hd],
                                                    G0[r, 0:B * n].rearrange("p (b k n) -> p b k n", b=B, n=hd))
                    ins.then_inc(g0_free, 1)
                elif k == "values3":
                    g = st.g0
                    dve.wait_ge(fills, st.fi)
                    for b in range(B):
                        for half in range(2):
                            dve.wait_ge(g0_full, g + 1)
                            nc.vector.tensor_copy(V3[:, b, 8 * half:8 * half + 8, 0:HS3],
                                                  G0[:, :].rearrange("p (h n) -> p h n", h=8)).then_inc(g0_free, 1)
                            g += 1
                        dve.wait_ge(g0_full, g + 1)
                        for j in range(4):
                            r = slice(32 * j, 32 * j + KL)
                            ins = nc.vector.tensor_copy(V3L[r, b, :, 65 * j:65 * j + HS3],
                                                        G0[r, 0:256].rearrange("p (k n) -> p k n", k=4))
                        ins.then_inc(g0_free, 1)
                        g += 1
                elif k == "max":
                    layer, i, c, b, m = st.args
                    h0, n_h = layer.max_banks(c)[m]
                    n = layer.keys(c)
                    dve.wait_ge(mx_full, st.mx + 1)
                    nc.vector.tensor_reduce(NMX[:, b % 2, h0:h0 + n_h],
                                            MB[st.mx % 2][:, 0:n_h * n].rearrange("p (h n) -> p h n", h=n_h),
                                            AXX, ALU.max, negate=True).then_inc(mx_free, 1)
                elif k == "negmax":
                    layer, i, b = st.args
                    dve.wait_ge(mx_free, st.mx)
                    wait(dve, fills, 1)
                    n = layer.heads
                    split3([NM3[:, b % 2, 16 * s:16 * s + n] for s in range(3)], NMX[:, b % 2, 0:n], NMR[:, 0:n])\
                        .then_inc(nm_ready, 1)
                elif k == "attended1":
                    layer, b, _ = st.args
                    hd, n = layer.hd, layer.heads
                    dve.wait_ge(g0_full, st.g0 + 1)
                    w = G0[:, 0:n * 32].rearrange("p (h n) -> p h n", n=32)
                    link(nc.vector.reciprocal(REC[:, 0:n], w[:, :, hd]))
                    nc.vector.tensor_tensor(CTK[:, b % 2, :].rearrange("p (h n) -> p h n", n=hd), w[:, :, 0:hd],
                                            REC[:, 0:n].unsqueeze(2).broadcast_to([128, n, hd]), ALU.mult).then_inc(g0_free, 1)
                elif k in ("back", "state_out", "mlp2"):
                    c = st.args[-1]
                    bias = {"state_out": "L0bprog", "mlp2": "bfc2"}.get(k) or f"{st.args[0].name}bo"
                    dve.wait_ge(g0_full, st.g0 + 1)
                    link(nc.vector.tensor_tensor(X[:, c, :, :], G0[:, :].rearrange("p (b n) -> p b n", b=B), X[:, c, :, :], ALU.add))
                    ins = nc.vector.tensor_tensor(X[:, c, :, :], X[:, c, :, :], over_batches(P(bias)), ALU.add)
                    ins.then_inc(g0_free, 1)
                    dve.wait_ge(g0_free, st.g0 + 1)
                    if not (k == "back" and st.args[0] is L1):
                        nc.vector.tensor_copy(REC[:, 0:1], MV[:, 0, 0:1]).then_inc(x_done, 1)
                elif k == "affine":
                    c = st.args[0]
                    dve.wait_ge(z_ready, st.ln)
                    link(nc.vector.tensor_tensor(X[:, c, :, :], Z[:, :, :], over_batches(P("L1g")), ALU.mult))
                    nc.vector.tensor_tensor(X[:, c, :, :], X[:, c, :, :], over_batches(P("L1b")), ALU.add).then_inc(x_done, 1)
                elif k == "u2":
                    c = st.args[0]
                    dve.wait_ge(g0_full, st.g0 + 1)
                    nc.vector.tensor_copy(UT[0:S, c * C:(c + 1) * C, :].rearrange("p t b -> p b t"),
                                          G0[0:S, :].rearrange("p (b t) -> p b t", b=B)).then_inc(g0_free, 1)
                elif k == "scan":
                    dve.wait_ge(g0_free, st.g0)
                    for c in range(NCH):
                        dve.wait_ge(silu_ready, min((c + 1) * C, T) - 1)
                        t = slice(c * C, (c + 1) * C)
                        nc.vector.tensor_tensor(SS[0:S, :, t].rearrange("p b t -> p t b"), ZT[0:S, t, :], UT[0:S, t, :],
                                                ALU.add).then_inc(states_ready, 1)
                elif k == "weigh3":
                    c, b, p, closed = st.args
                    dve.wait_ge(pv_done, closed)
                    if p == 0:
                        dve.wait_ge(g0_full, st.g0)
                    w = OB[(st.o - 1) % 2][:, 0:260].rearrange("p (h n) -> p h n", h=4)
                    wait(dve, o_free, st.o - 2)
                    rec = REC[:, 4 * p:4 * p + 4]
                    link(nc.vector.reciprocal(rec, w[:, :, HS3]))
                    nc.vector.tensor_tensor(CTX3[:, p * 256:(p + 1) * 256].rearrange("p (h n) -> p h n", h=4), w[:, :, 0:HS3],
                                            rec.unsqueeze(2).broadcast_to([128, 4, HS3]), ALU.mult).then_inc(o_free, 1)
                elif k == "turn3":
                    b, half = st.args
                    dve.wait_ge(g0_full, st.g0 + 1)
                    nc.vector.tensor_tensor(C3T[:, 4 * half:4 * half + 4, :], G0[:, :].rearrange("p (t n) -> p t n", t=4),
                                            P("L3bv")[:, 4 * half:4 * half + 4].unsqueeze(2).broadcast_to([128, 4, C]),
                                            ALU.add).then_inc(g0_free, 1)
                elif k == "out3":
                    c, b = st.args
                    dve.wait_ge(g0_full, st.g0 + 1)
                    nc.vector.tensor_tensor(X[:, c, b, :], G0[:, 0:D], X[:, c, b, :], ALU.add).then_inc(g0_free, 1)
                    dve.wait_ge(g0_free, st.g0 + 1)
                    nc.vector.tensor_tensor(X[:, c, b, :], X[:, c, b, :], P("L3bo"), ALU.add).then_inc(x_done, 1)


def kernel(**inputs):
    import concourse.bacc as bacc
    from concourse.bass_utils import run_bass_kernel_spmd

    a = {n: np.asarray(v) for n, v in inputs.items()}
    f32 = np.float32

    def column(v):
        return np.ascontiguousarray(v.reshape(-1, 128).T)

    def row(v):
        return np.broadcast_to(v[None, :], (128, v.shape[0]))

    def cut(w, n):
        return [p.T for p in np.split(w, n, axis=0)]

    def low(v):
        return np.concatenate([v, np.zeros((128 - v.shape[0],) + v.shape[1:], f32)], axis=0)

    ctx = a["ctx_1024"]
    padded = np.concatenate([ctx, np.repeat(ctx[:, -1:], KP - KV, axis=1)], axis=1)
    w = {"ident": np.eye(128, dtype=f32),
         "ctxT": padded.transpose(2, 0, 1).reshape(D, B * KP),
         "ctx": padded[:, 0:128].transpose(1, 0, 2).reshape(128, B * D),
         "ctxl": low(padded[:, 128:].transpose(1, 0, 2).reshape(KP - 128, B * D)),
         "probs": np.concatenate([np.zeros((S, B * KV), f32),
                                  a["ctxb_2048x64"].transpose(2, 0, 1).reshape(S, B * KV)], axis=0)}
    l0 = lambda n: a["L0_xattn_" + n]
    w["L0wq"], w["L0wk"], w["L0wv"] = cut(l0("W_qkv"), 3)
    w["L0bq"], w["L0bk"], w["L0bv"] = (column(v) for v in np.split(l0("b_qkv"), 3))
    w["L0wo"], w["L0bo"] = l0("W_o").T, row(l0("b_o"))
    w["L0g1"], w["L0be1"], w["L0g2"], w["L0be2"] = (column(l0(n)) for n in ("g1", "beta1", "g2", "beta2"))
    w["L0win"], w["L0bin"] = l0("W_in").T, column(l0("b_in"))
    w["L0bmat"], w["L0at"] = l0("Bmat"), low(l0("A").T)
    w["L0cp"] = np.concatenate([l0("Cmat"), l0("W_prog").T], axis=0)
    w["L0bprog"] = row(l0("b_prog"))
    l1 = lambda n: a["L1_xattn_" + n]
    w["L1wq"], w["L1wk"], w["L1wv"] = cut(l1("W_qkv"), 3)
    w["L1bq"], w["L1bk"], w["L1bv"] = (column(v) for v in np.split(l1("b_qkv"), 3))
    w["L1wo"], w["L1bo"] = l1("W_o").T, row(l1("b_o"))
    w["L1g"], w["L1b"] = row(l1("ln_gamma")), row(l1("ln_beta"))
    l2 = lambda n: a["L2_xattn_" + n]
    for n in (1, 2, 3):
        w[f"L2g{n}"], w[f"L2b{n}"] = column(l2(f"ln{n}_g")), column(l2(f"ln{n}_b"))
    w["L2Swq"], w["L2Swk"], w["L2Swv"] = cut(l2("w_qkv"), 3)
    w["L2Swo"], w["L2Sbo"] = l2("w_prj1").T, row(l2("b_prj1"))
    w["L2Xwq"] = l2("w_q").T
    w["L2Xwk"], w["L2Xwv"] = cut(l2("w_kv"), 2)
    w["L2Xwo"], w["L2Xbo"] = l2("w_prj2").T, row(l2("b_prj2"))
    w["fc1"], w["bfc1"] = l2("w_fc1").T, column(l2("b_fc1"))
    w["fc2"] = np.concatenate(np.split(l2("w_fc2").T, HID // 128, axis=0), axis=1)
    w["bfc2"] = row(l2("b_fc2"))
    l3 = lambda n: a["L3_xattn_" + n]
    w["L3g"], w["L3b"] = column(l3("ln_g")), column(l3("ln_b"))
    w["L3wq"], w["L3bq"] = l3("wq"), column(l3("bq"))
    w["L3wk"], w["L3wv"] = np.split(l3("wkv"), 2, axis=1)
    w["L3bk"], w["L3bv"] = (column(v) for v in np.split(l3("bkv"), 2))
    w["L3wo"] = np.concatenate(np.split(l3("wo"), E3 // 128, axis=0), axis=1)
    w["L3bo"] = row(l3("bo"))

    def packed(names):
        for n, cols in names:
            assert w[n].shape == (128, cols), (n, w[n].shape)
        return np.ascontiguousarray(np.concatenate([w[n] for n, _ in names], axis=1))

    import ml_dtypes
    bf16 = ml_dtypes.bfloat16
    q, r = np.arange(128), np.arange(128)
    maxsel = np.zeros((128, 16, 128), f32)
    leftsel = np.zeros((128, 4, 4, 32), f32)
    for h in range(16):
        for part in range(3):
            maxsel[16 * part + h, h] = 1
            leftsel[16 * part + h, h // 4, h % 4] = 1
    later = (r[None, :] > q[:, None])
    left = (r[:, None] % 32 > q[None, :])
    consts = {"identb": np.eye(128), "maxsel": maxsel.reshape(128, -1), "leftsel": leftsel.reshape(128, -1),
              "mask": later * BIG, "maskT": later.T * BIG, "maskLT": left * BIG}
    arrays = {"x": a["x"], "early": packed(EARLY), "consts":
              np.concatenate([np.asarray(consts[n], f32) for n, _ in CONSTS], axis=1).astype(bf16)}
    arrays.update({f"params{i}": packed(g) for i, g in enumerate(PARAMS)})

    nc = bacc.Bacc("TRN2", target_bir_lowering=False, num_devices=1)
    ap = {n: nc.dram_tensor(f"in_{n}", v.shape, mybir.dt.from_np(v.dtype), kind="ExternalInput").ap()
          for n, v in arrays.items()}
    out = nc.dram_tensor("out", (B, T, D), F32, kind="ExternalOutput").ap()
    build(nc, ap["x"], ap["early"], [ap[f"params{i}"] for i in range(3)], ap["consts"], out)
    r = run_bass_kernel_spmd(nc, [{f"in_{n}": v for n, v in arrays.items()}], core_ids=[0])
    return r.results[0]["out"]
```

```python
from contextlib import ExitStack

import numpy as np

import concourse.bass as bass
from concourse import mybir

F32 = mybir.dt.float32
BF16 = mybir.dt.bfloat16
ACT = mybir.ActivationFunctionType
ALU = mybir.AluOpType
AXX = mybir.AxisListType.X

B, T, D = 4, 512, 128
KV, KP = 154, 160
KL = KV - 128
C = 128
NCH = T // C
TOK = B * C
S = 64
HID = 512
EPS = 1e-5
HS3 = 64
E3 = 1024
BIG = -1.0e38
QPART = (0, 0, 0, 1, 1, 2)
KPART = (0, 1, 2, 0, 1, 0)
NCOMBO = len(QPART)
NAHEAD = 2


class Layer:

    def __init__(self, name, heads, hd, own_keys=False, causal=False):
        self.name, self.heads, self.hd = name, heads, hd
        self.own_keys, self.causal = own_keys, causal
        self.packs = heads // 4
        self.wide = hd == HS3
        self.per_tile = 1 if hd == 16 else 2

    def leftover(self, c):
        return not self.own_keys and not (self.causal and c == 0)

    def units(self, c):
        out = [("left", 0, 0)] if self.leftover(c) else []
        blocks = range(c + 1) if self.own_keys else range(1)
        return out + [("full", p, k) for p in range(self.packs) for k in blocks]

    def max_banks(self, c):
        n = self.keys(c)
        per = min(512 // n, self.heads)
        return [(h, min(per, self.heads - h)) for h in range(0, self.heads, per)]

    def keys(self, c):
        if self.own_keys:
            return (c + 1) * C
        return KV if self.leftover(c) else C

    def masked_block(self, c):
        if not self.causal:
            return None
        if self.own_keys:
            return c
        return 0 if c == 0 else None

    def masked_left(self, c):
        return self.causal and not self.own_keys and c == 1


L0 = Layer("L0", 8, 16)
L1 = Layer("L1", 16, 8)
L2S = Layer("L2S", 16, 8, own_keys=True, causal=True)
L2X = Layer("L2X", 16, 8)
L3 = Layer("L3", 16, HS3, causal=True)
ORDER = [L0, L1, L2S, L2X, L3]

PARAMS = [
    [("L1bq", 1), ("L0g1", 1), ("L0be1", 1), ("L0bq", 1), ("L0bk", 1),
     ("L0bv", 1), ("L0wq", 128), ("L0wk", 128), ("L0wv", 128), ("L0wo", 128), ("L0bo", 128),
     ("L0g2", 1), ("L0be2", 1), ("L0win", 128), ("L0bin", 1), ("L0bmat", S), ("L0at", S),
     ("L0cp", 128), ("L0bprog", 128)],
    [("ctxT", B * KP), ("L1bk", 1), ("L1bv", 1), ("L1wq", 128), ("L1wk", 128), ("L1wv", 128),
     ("L1wo", 128), ("L1bo", 128), ("L1g", 128), ("L1b", 128),
     ("L2g1", 1), ("L2b1", 1), ("L2g2", 1), ("L2b2", 1), ("L2g3", 1), ("L2b3", 1),
     ("L2Swq", 128), ("L2Swk", 128), ("L2Swv", 128), ("L2Swo", 128), ("L2Sbo", 128),
     ("L2Xwq", 128), ("L2Xwk", 128), ("L2Xwv", 128), ("L2Xwo", 128), ("L2Xbo", 128),
     ("fc1", HID), ("bfc1", HID // 128), ("fc2", HID), ("bfc2", 128)],
    [("L3g", 1), ("L3b", 1), ("L3wq", E3), ("L3bq", E3 // 128), ("L3wk", E3), ("L3bk", E3 // 128),
     ("L3wv", E3), ("L3bv", E3 // 128), ("L3wo", E3), ("L3bo", 128)],
    [("ident", 128)],
]
EARLY = [("ctx", B * D), ("ctxl", B * D), ("probs", B * KV)]
CONSTS = [("identb", 128), ("maxsel", 16 * 128), ("leftsel", 4 * 128), ("mask", 128), ("maskT", 128), ("maskLT", 128)]


def columns(group):
    at, out = 0, {}
    for name, n in group:
        out[name] = (at, n)
        at += n
    return out, at


class Step:

    def __init__(self, kind, args, g0, g1, mx, u, f, l, o, nm, sp, ld, ln, xd, fi, op):
        self.kind, self.args = kind, args
        self.g0, self.g1, self.mx, self.u, self.f, self.l, self.o = g0, g1, mx, u, f, l, o
        self.nm, self.sp, self.ld, self.ln, self.xd, self.fi, self.op = nm, sp, ld, ln, xd, fi, op


def make_plan():
    count = dict.fromkeys("g0 g1 mx u f l o nm sp ld ln xd fi op".split(), 0)
    plan = []
    ended = {}
    closed = [0]
    needs = {}
    fill_no = {}
    todo, urgent = [], []

    def add(kind, *args, **events):
        plan.append(Step(kind, args, **count))
        for k, n in events.items():
            count[k] += n

    def later(kind, *args, **events):
        return lambda: add(kind, *args, **events)

    def split(layer, what, i, fill):
        add("split", layer, what, i, fill_no[fill], sp=1, ld=layer.per_tile * NCOMBO)

    def norm(what, c):
        return [later("ln", what, c), later("norm", what, c, ln=1)]

    def turn(what, c):
        add("turn", what, c, g0=1)
        needs["turned"] = count["g0"]

    def project(layer, what, i, fill):
        add("project", layer, what, needs["turned"], g1=1)
        split(layer, what, i, fill)
        needs["stack", i] = count["ld"]

    def own_values(i, c):
        add("own_values", c, fill_no["own keys"], needs["turned"], g0=1)
        needs["values", i] = count["g0"]

    def front(i):
        layer, c = instances[i]
        out = [] if layer is L1 else norm("x", c)
        out.append(lambda: turn(layer, c))
        if layer is not L3:
            out.append(lambda: project(layer, "q", i, "start"))
        if layer.own_keys:
            out += [lambda: project(layer, "k", i, "own keys"), lambda: own_values(i, c)]
        return out

    def project3(c, b):
        def half(h):
            add("project3", c, b, h, needs["turned"], g1=1)
            needs["queries", c, b] = count["g1"]
        return [lambda: half(0), lambda: half(1)]

    def key_prep(layer, fill):
        def keys():
            add("keys", layer, g1=2)
            split(layer, "k", 0, fill)
            needs["keys", layer.name] = count["ld"]
        return [keys]

    def value_prep(layer, fill):
        def values():
            add("values", layer, fill_no[fill], g0=2)
            needs["values", layer.name] = count["g0"]
        return [values]

    def keys3(t, half):
        add("keys3", t, half, fill_no["layer 3"], g1=1)
        needs["keys", L3.name] = count["g1"]

    def values3(b, part):
        add("values3", b, part, fill_no["layer 3"], g0=1)
        needs["values", L3.name] = count["g0"]

    def fill(name, pieces=1):
        def piece(k):
            add("fill", name, k, pieces, fi=int(k == pieces - 1))
            fill_no[name] = count["fi"]
        return [lambda k=k: piece(k) for k in range(pieces)]

    def mlp(c):
        return norm("x", c) + [lambda: turn("mlp", c), lambda: add("mlp1", c, needs["turned"], g1=4), later("mlp2", c, g0=1, xd=1)]

    def back(layer, c):
        out = [later("back", layer, c, g0=1, xd=1)]
        if layer is L0:
            out += norm("x", c) + [lambda: turn("u", c), lambda: add("u1", needs["turned"], g1=1), later("u2", c, g0=1)]
        if layer is L1:
            out += norm("x", c) + [later("affine", c, xd=1)]
        if layer is L2X:
            out += mlp(c)
        return out

    def maxima(batch, at, n):
        i, layer, c, b = batch
        n_banks = len(layer.max_banks(c))
        for m in range(n_banks * at // n, n_banks * (at + 1) // n):
            if layer.wide:
                loads, g1 = 0, max(needs["queries", c, b], needs["keys", L3.name])
            else:
                loads, g1 = max(needs["stack", i], 0 if layer.own_keys else needs["keys", layer.name]), 0
            add("max", layer, i, c, b, m, loads, g1, mx=1)

    def negmax(batch):
        add("negmax", batch[1], batch[3], nm=1)

    def negmaxT(batch):
        add("negmaxT", *batch, g1=1)
        needs["negmax", batch[0], batch[3]] = count["g1"]

    def is_ahead(batch):
        return batch[1] is L1 and batch[2] < NAHEAD

    def attend(batch, unit, scored):
        i, layer, c, b = batch
        if unit[0] == "left":
            return
        _, p, k = unit
        last_block = k == (c if layer.own_keys else 0)
        last_pack = p == layer.packs - 1
        closes = last_block and (layer.wide or last_pack)
        opens = k == 0 and (layer.wide or p == 0)
        values = needs["values", i if layer.own_keys else layer.name]
        add("attend", layer, c, b, p, k, scored, opens, last_block, values, o=int(closes))
        if closes:
            closed[0] = scored.f + 1
        if layer.wide:
            add("weigh3", c, b, p, closed[0])
            if p % 2:
                urgent.append(later("turn3", b, p // 2, count["o"], g0=1))
            if last_pack:
                urgent.append(later("out3", c, b, g0=1, xd=1))

    def run(first, end, tasks):
        batches = [(i, *instances[i], b) for i in range(first, end) for b in range(B)]
        if not is_ahead(batches[0]):
            maxima(batches[0], 0, 1)
            negmax(batches[0])
            negmaxT(batches[0])
        held = before = None
        for n, batch in enumerate(batches):
            i, layer, c, b = batch
            following = batches[n + 1] if n + 1 < len(batches) and not is_ahead(batches[n + 1]) else None
            todo.extend(tasks(i, b))
            units = layer.units(c)
            n_units = len(units)
            spread = max(1, n_units - 2)
            turned = needs["negmax", i, b]
            for k, unit in enumerate(units):
                turn_now = following and k == n_units - 1
                if turn_now and n_units > 3:
                    negmaxT(following)
                add("score", layer, i, c, b, unit, turned, u=1, f=int(unit[0] == "full"), l=int(unit[0] == "left"))
                scored = plan[-1]
                if turn_now and n_units <= 3:
                    negmaxT(following)
                if urgent:
                    urgent.pop(0)()
                if held is not None:
                    attend(*held)
                held = (batch, unit, scored)
                if following and k < spread:
                    maxima(following, k, spread)
                    if k == spread - 1:
                        negmax(following)
                if k == 0 and before and not before[1].wide:
                    add("attended0", before[1], closed[0])
                if before and not before[1].wide:
                    if k == 1:
                        add("attended1", before[1], before[3], g0=1)
                    if k == 2:
                        add("attended2", before[1], before[3], g1=1)
                        if before[3] == B - 1:
                            first, *rest = back(before[1], before[2])
                            urgent.append(first)
                            todo.extend(rest)
                slots = (B - b) * n_units - k
                held_up = (b == 0 and k == 0) or (urgent and not layer.wide)
                for _ in range(0 if held_up else min(len(todo), max(1, -(-len(todo) // slots)))):
                    todo.pop(0)()
            if b == B - 1:
                ended[i] = count["f"]
            before = batch
        attend(*held)
        i, layer, c, b = before
        if layer.wide:
            while urgent:
                urgent.pop(0)()
        else:
            add("attended0", layer, closed[0])
            add("attended1", layer, b, g0=1)
            add("attended2", layer, b, g1=1)
            todo.extend(back(layer, c))

    def flush():
        while todo:
            todo.pop(0)()

    instances = [(layer, c) for layer in ORDER for c in range(NCH)]
    at = {layer.name: NCH * n for n, layer in enumerate(ORDER)}
    todo += fill("start")
    for n, what in enumerate(("ctx", "ctxl")):
        todo += norm(what, 0) + [later("ctx_turn", n, g0=1)]
    todo += [later("biases"), later("operand", L0, op=1)]
    todo += key_prep(L0, "start") + front(0) + value_prep(L0, "start")
    flush()

    def tasks0(i, b):
        probs = [later("probs")] if i == 0 and b == 1 else []
        return front(i + 1) if b == 0 and i + 1 < NCH else probs

    run(0, NCH, tasks0)
    todo += fill("layer 1") + key_prep(L1, "layer 1") + value_prep(L1, "layer 1")
    for c in range(NCH):
        if c:
            todo.append(later("states", c - 1))
            todo.append(later("state_out", c - 1, g0=1, xd=1))
        if 0 < c <= NAHEAD:
            i = at["L1"] + c - 1
            todo.append(None)
            for step in front(i):
                todo += [step, None]
            todo += [None] * 8
            for b in range(B):
                batch = (i, L1, c - 1, b)
                banks = len(L1.max_banks(c - 1))
                todo += [lambda batch=batch, m=m, n=banks: maxima(batch, m, n) for m in range(banks)]
                todo += [lambda batch=batch: negmax(batch), None, lambda batch=batch: negmaxT(batch)]
        steps = range(max(1, c * C), (c + 1) * C)
        n_tasks, done = len(todo), 0
        for t in steps:
            add("scan", t)
            while done < n_tasks * (t - steps[0] + 1) // len(steps):
                step = todo.pop(0)
                done += 1
                if step:
                    step()
    add("states", NCH - 1)
    todo.append(later("state_out", NCH - 1, g0=1, xd=1))
    flush()

    steps3 = [lambda t=t, half=half: keys3(t, half) for t in range(8) for half in range(2)] + \
        [lambda b=b, part=part: values3(b, part) for b in range(B) for part in range(3)]

    def tasks1(i, b):
        layer, c = instances[i]
        if i + 1 == at["L3"]:
            return front(i + 1) if b == B - 1 else steps3[(c - 1)::NCH - 1] if b == 0 else []
        if b > 0:
            return []
        out = [] if layer is L1 and c + 1 < NAHEAD else front(i + 1)
        if layer is L1 and c == 0:
            out += [later("late_params")]
        if layer is L1 and c == NAHEAD:
            out = fill("own keys", 6) + out
        if layer is L2S and c == 1:
            out += key_prep(L2X, "layer 1") + value_prep(L2X, "layer 1")
        if layer is L2X and c == 0:
            out += fill("layer 3", 6) + [later("operand", L3, op=1)]
        if layer is L2X and c > 0:
            out += steps3[(c - 1)::NCH - 1]
        return out

    run(at["L1"], at["L3"], tasks1)
    for b in range(B):
        urgent += project3(0, b)
    while urgent:
        urgent.pop(0)()

    def tasks3(i, b):
        c = instances[i][1]
        out = project3(c, B - 1) if b == 0 and c else []
        if c + 1 < NCH:
            out += front(i + 1) if b == 0 else project3(c + 1, b - 1)
        return out

    run(at["L3"], len(instances), tasks3)
    flush()
    return plan, dict(count), ended


def build(nc, x_dram, early_dram, params_dram, consts_dram, out_dram):
    plan, total, ended = make_plan()
    ctx = ExitStack()

    def sb(name, shape, dt=F32):
        return ctx.enter_context(nc.sbuf_tensor(name, shape, dt))

    def sem(name):
        return ctx.enter_context(nc.semaphore(name))

    with ctx:
        places = [columns(g) for g in PARAMS]
        shared = sb("params_0_and_2", [128, max(places[0][1], places[2][1])])
        par = [shared, sb("params_1", [128, places[1][1]]), shared, sb("params_3", [128, places[3][1]])]
        const_at, n_const = columns(CONSTS)
        con = sb("consts", [128, n_const], BF16)

        def P(name):
            for (at, _), t in zip(places, par):
                if name in at:
                    o, n = at[name]
                    return t[:, o:o + n]
            raise KeyError(name)

        def K(name):
            o, n = const_at[name]
            return con[:, o:o + n]

        X = sb("residual", [128, NCH, B, D])
        Z = sb("normed", [128, B, D])
        XT = sb("normedT", [128, TOK])
        QF = sb("projected", [128, B * KP])
        SPL = sb("parts", [128, 3, B * KP], BF16)
        QS = sb("query_stack", [128, 2, 8, TOK], BF16)
        Q3 = QS[:, :, :, :].rearrange("p a g n -> p (a g n)").bitcast(F32).rearrange("p (g n) -> p g n", g=8)
        KAW = sb("key_stack", [128, 16 * B * KP // 2])
        KA = KAW[:, :].bitcast(BF16).rearrange("p (h n) -> p h n", h=16)
        ARENA = sb("own_key_stack", [128, 16 * B * T // 2 + 64])
        KS = ARENA[:, 0:16 * B * T // 2].bitcast(BF16).rearrange("p (c h n) -> p c h n", c=NCH, h=16)
        K3 = ARENA[:, 0:16 * B * KP].rearrange("p (h n) -> p h n", h=16)
        V3L = ARENA[:, 16 * B * KP:16 * (B * KP + 260)].rearrange("p (b k n) -> p b k n", b=B, k=4)
        HT = ARENA[:, 16 * (B * KP + 260):16 * (B * KP + 260) + 4 * TOK].rearrange("p (j n) -> p j n", j=4)
        UT = ARENA[:, 0:T * B].rearrange("p (t b) -> p t b", b=B)
        ZT = ARENA[:, T * B:2 * T * B].rearrange("p (t b) -> p t b", b=B)
        SS = ARENA[:, 2 * T * B:3 * T * B].rearrange("p (b t) -> p b t", b=B)
        early_at, n_early = columns(EARLY)
        EA = ARENA[:, 3 * T * B:3 * T * B + n_early]

        def early(name):
            o, n = early_at[name]
            return EA[:, o:o + n].rearrange("p (b n) -> p b n", b=B)

        VW = sb("values", [128, B * 16 * 16 + B * 4 * 128])
        VA = VW[:, 0:B * 16 * 16].rearrange("p (b h n) -> p b h n", b=B, h=16)
        VAL = VW[:, B * 16 * 16:].rearrange("p (b k n) -> p b k n", b=B, k=4)
        CTX3 = VW[:, 0:E3]
        C3T = VW[:, E3:2 * E3].rearrange("p (t n) -> p t n", t=8)
        VAR = sb("values_arena", [128, B * 16 * 65])
        V0 = VAR[:, 0:B * 8 * 32].rearrange("p (b h n) -> p b h n", b=B, h=8)
        V0L = VAR[:, B * 8 * 32:2 * B * 8 * 32].rearrange("p (b k n) -> p b k n", b=B, k=2)
        VS = VAR[:, 0:B * NCH * 256].rearrange("p (b c h n) -> p b c h n", b=B, c=NCH, h=16)
        V3 = VAR[:, 0:B * 16 * 65].rearrange("p (b h n) -> p b h n", b=B, h=16)
        ZC = sb("normed_ctx", [128, B, KP])
        CT0, CT3 = VAR[:, 2 * B * 256:2 * B * 256 + B * KP].rearrange("p (b n) -> p b n", b=B), ZC
        PR = sb("probs", [128, 3, 512])
        PL = sb("probs_left", [128, 2, 512])
        OS = sb("attended", [128, 2, 512])
        CTK = sb("attended_tok", [128, 2, D])
        CXT = sb("attendedT", [128, TOK])
        NMX = sb("negmax", [128, 2, 16])
        NMR = sb("negmax_rest", [128, 16])
        NM3 = sb("negmax_parts", [128, 2, 128], BF16)
        NMTA = VAR[:, 3072:3072 + NAHEAD * B * C // 2].bitcast(BF16).rearrange("p (k n) -> p k n", n=C)
        NMT = sb("negmaxT", [128, 2, 128], BF16)
        REC = sb("reciprocals", [128, 16])
        ST = sb("stats", [128, B, 6])
        MV = sb("mean_var", [128, B, 2])
        RS = sb("rstd", [128, 3, B])
        PM = sb("probs_sum", [128, B])
        SB = sb("scaled_bias", [128, 16])
        parts_dram = nc.dram_tensor("parts_dram", [3, 128, B * KP], BF16).ap()

        banks = [ctx.enter_context(nc.psum_tensor(f"bank{i}", [128, 512], F32)) for i in range(8)]
        MB, SBK, OB, G0, G1 = banks[0:2], banks[2:4], banks[4:6], banks[6], banks[7]

        early_in = [sem(f"{name}_loaded") for name, _ in EARLY]
        consts_in, x_in = sem("consts_loaded"), [sem(f"x_loaded{c}") for c in range(NCH)]
        par_in = [sem(f"params_loaded{i}") for i in range(len(PARAMS))]
        stored, stacked, out_done = sem("parts_stored"), sem("stack_loaded"), sem("output_stored")
        g0_full, g0_free = sem("g0_full"), sem("g0_free")
        g1_full, g1_free = sem("g1_full"), sem("g1_free")
        mx_full, mx_free = sem("max_scores_full"), sem("max_scores_free")
        nm_ready = sem("negmax_ready")
        s_full, p_ready, pv_done, o_free = sem("scores_full"), sem("probs_ready"), sem("probs_used"), sem("attended_free")
        dve_step, pool_step = sem("dve_step"), sem("pool_step")
        var_ready, rstd_ready, z_ready = sem("var_ready"), sem("rstd_ready"), sem("z_ready")
        split_ready, operand_ready, fills, x_done = sem("split_ready"), sem("operand_ready"), sem("fills"), sem("x_done")
        bias_ready = sem("scaled_bias_ready")
        au_ready, silu_ready, y_ready, states_ready = sem("au_ready"), sem("silu_ready"), sem("y_ready"), sem("states_ready")

        def wait(eng, s, n):
            if n > 0:
                eng.wait_ge(s, n)

        def group(name):
            return next(i for i, (at, _) in enumerate(places) if name in at)

        def last_use(layer):
            return {L0: 0, L1: ended.get(NCH - 1), L2X: ended.get(2 * NCH - 1)}[layer]

        def q_op(layer, i, h, b):
            t = h // layer.per_tile
            src = Q3[:, h // 2, :] if layer.wide else QS[:, i % 2, t, :]
            return src[:, b * C:(b + 1) * C]

        def k_op(layer, h, b, lo, n):
            if layer.wide:
                return K3[:, h, b * KP + lo:b * KP + lo + n]
            if layer.own_keys:
                return KS[:, lo // C:(lo + n) // C, h, b * C:(b + 1) * C]
            return KA[:, h, b * KP + lo:b * KP + lo + n]

        def negmax_turned(layer, c, b):
            return NMTA[:, c * B + b, :] if layer is L1 and c < NAHEAD else NMT[:, b % 2, :]

        def v_ops(layer):
            return {L0: (V0, V0L), L1: (VA, VAL), L2X: (VA, VAL), L3: (V3, V3L)}[layer]

        block = ctx.enter_context(nc.Block())

        @block.sync
        def _(sp):
            def load_x(c):
                sp.dma_start(X[:, c, :, :], x_dram[:, c * C:(c + 1) * C, :].rearrange("b t f -> t b f")).then_inc(x_in[c], 16)

            n = B * D
            sp.dma_start(EA[:, 0:n], early_dram[:, 0:n]).then_inc(early_in[0], 16)
            sp.dma_start(EA[0:32, n:2 * n], early_dram[0:32, n:2 * n]).then_inc(early_in[1], 16)
            sp.dma_start(par[3][:, :], params_dram[3][:, :]).then_inc(par_in[3], 16)
            load_x(0)
            sp.dma_start(shared[:, 0:places[0][1]], params_dram[0][:, :]).then_inc(par_in[0], 16)
            sp.dma_start(con[:, :], consts_dram[:, :]).then_inc(consts_in, 16)
            load_x(1)
            sp.dma_start(EA[S:128, 2 * n:], early_dram[S:128, 2 * n:]).then_inc(early_in[2], 16)
            load_x(2)
            load_x(3)
            sp.dma_start(par[1][:, :], params_dram[1][:, :]).then_inc(par_in[1], 16)
            for st in plan:
                if st.kind == "split":
                    layer, what, i, filled = st.args
                    n = TOK if what == "q" or layer.own_keys else B * KP
                    rows = layer.hd
                    sp.wait_ge(split_ready, st.sp + 1)
                    wait(sp, stacked, 16 * st.ld)
                    sp.dma_start(parts_dram[:, :, 0:n].rearrange("s p n -> p s n"), SPL[:, :, 0:n]).then_inc(stored, 16)
                    sp.wait_ge(stored, 16 * (st.sp + 1))
                    sp.wait_ge(fills, filled)
                    if what == "q":
                        wait(sp, pv_done, ended.get(i - 2, 0))
                    elif not layer.own_keys:
                        wait(sp, pv_done, last_use(layer))
                    for k in range(NCOMBO):
                        part = parts_dram[(QPART if what == "q" else KPART)[k], :, 0:n]
                        for a in range(layer.per_tile):
                            p0 = 64 * a + rows * k
                            src = part.rearrange("(g a d) n -> a d g n", a=layer.per_tile, d=rows)[a]
                            if what == "q":
                                dst = QS[p0:p0 + rows, i % 2, :, :]
                            elif layer.own_keys:
                                dst = KS[p0:p0 + rows, i % NCH, a::2, :]
                            elif layer.per_tile == 1:
                                dst = KA[p0:p0 + rows, 0:8, :]
                            else:
                                dst = KA[p0:p0 + rows, a::2, :]
                            sp.dma_start(dst, src).then_inc(stacked, 16)
                elif st.kind == "late_params":
                    sp.wait_ge(x_done, st.xd)
                    sp.wait_ge(g0_full, st.g0)
                    sp.wait_ge(g1_free, st.g1)
                    sp.dma_start(shared[:, 0:places[2][1]], params_dram[2][:, :]).then_inc(par_in[2], 16)
                elif st.kind == "out3":
                    c, b = st.args
                    sp.wait_ge(x_done, st.xd + 1)
                    sp.dma_start(out_dram[b, c * C:(c + 1) * C, :], X[:, c, b, :]).then_inc(out_done, 16)
            sp.wait_ge(out_done, 16 * NCH * B)

        @block.gpsimd
        def _(pool):
            steps = [0]

            def link(ins):
                steps[0] += 1
                ins.then_inc(pool_step, 1)
                pool.wait_ge(pool_step, steps[0])

            def put(out, value):
                link(nc.gpsimd.memset(out, value))

            def last_put(out, value, n):
                nc.gpsimd.memset(out, value).then_inc(fills, 1)
                pool.wait_ge(fills, n)

            def ones_left(t, at, width, stride):
                return [t[32 * j:32 * j + KL, :, :, j * stride + at:j * stride + at + width] for j in range(4)]

            for st in plan:
                if st.kind == "fill":
                    name, piece, pieces = st.args
                    n = st.fi + 1
                    if name == "start":
                        put(RS[:, 2, :], -0.5)
                        put(NM3[:, :, :], 0.0)
                        put(ZT[0:S, 0, :], 0.0)
                        put(QS[:, :, :, :].rearrange("p a g n -> p (a g n)").bitcast(F32), 0.0)
                        put(KAW[:, :], 0.0)
                        put(V0L[:, :, :, :], 0.0)
                        for ones in ones_left(V0L, 16, 16, 32):
                            put(ones, 1.0)
                        last_put(V0[:, :, :, 16:32], 1.0, n)
                    elif name == "layer 1":
                        pool.wait_ge(pv_done, st.f)
                        put(KAW[:, :], 0.0)
                        put(VA[:, :, :, :], 1.0)
                        put(VAL[:, :, :, :], 0.0)
                        *some, last = ones_left(VAL, 8, 8, 32)
                        for ones in some:
                            put(ones, 1.0)
                        last_put(last, 1.0, n)
                    elif name == "own keys":
                        if piece == 0:
                            pool.wait_ge(g0_full, st.g0)
                            pool.wait_ge(x_done, st.xd)
                            put(VS[:, :, :, :, 8:16].rearrange("p b c h n -> p (b c h) n"), 1.0)
                        w = ARENA.shape[1] // pieces
                        part = ARENA[:, piece * w:ARENA.shape[1] if piece == pieces - 1 else (piece + 1) * w]
                        if piece < pieces - 1:
                            put(part, 0.0)
                        else:
                            last_put(part, 0.0, n)
                    elif name == "layer 3":
                        if piece == 0:
                            pool.wait_ge(pv_done, ended[3 * NCH - 1])
                            put(V3[:, :, :, 64:65], 1.0)
                        w = 16 * (B * KP + 260) // pieces
                        put(ARENA[:, piece * w:16 * (B * KP + 260) if piece == pieces - 1 else (piece + 1) * w], 0.0)
                        if piece == pieces - 1:
                            ones = ones_left(V3L, HS3, 1, 65)
                            for o in ones[:-1]:
                                put(o, 1.0)
                            last_put(ones[-1], 1.0, n)
                elif st.kind == "split":
                    layer, what, i, _ = st.args
                    n = TOK if what == "q" or layer.own_keys else B * KP
                    hi, mid, lo = (SPL[:, s, 0:n] for s in range(3))
                    pool.wait_ge(g1_free, st.g1)
                    wait(pool, stored, 16 * st.sp)
                    link(nc.gpsimd.tensor_copy(hi, QF[:, 0:n]))
                    link(nc.gpsimd.tensor_tensor(QF[:, 0:n], QF[:, 0:n], hi, ALU.subtract))
                    link(nc.gpsimd.tensor_copy(mid, QF[:, 0:n]))
                    nc.gpsimd.tensor_tensor(lo, QF[:, 0:n], mid, ALU.subtract).then_inc(split_ready, 1)
                elif st.kind == "ln":
                    p = 32 if st.args[0] == "ctxl" else 128
                    if st.ln == 0:
                        pool.wait_ge(fills, 1)
                    pool.wait_ge(var_ready, st.ln + 1)
                    nc.gpsimd.tensor_tensor(RS[0:p, 1, :], RS[0:p, 0, :], RS[0:p, 2, :], ALU.pow).then_inc(rstd_ready, 1)

        @block.tensor
        def _(pe):
            def mm(out, lhsT, rhs, start=True, stop=True):
                return nc.tensor.matmul(out, lhsT, rhs, start=start, stop=stop, skip_group_check=True)

            def parameters(name):
                pe.wait_ge(par_in[group(name)], 16)

            def operand(layer):
                return P("ctxT").rearrange("p (b n) -> p b n", b=B) if layer in (L1, L2X) else CT0

            parameters("ident")
            for st in plan:
                k = st.kind
                if k == "ctx_turn":
                    pe.wait_ge(z_ready, st.ln)
                    wait(pe, g0_free, st.g0)
                    n = 32 if st.args[0] else 128
                    for b in range(B):
                        ins = nc.tensor.transpose(G0[:, b * n:(b + 1) * n], Z[0:n, b, :], P("ident")[0:n, 0:n])
                    ins.then_inc(g0_full, 1)
                elif k == "turn":
                    what, c = st.args
                    pe.wait_ge(z_ready, st.ln)
                    pe.wait_ge(x_in[c], 16)
                    wait(pe, x_done, st.xd)
                    pe.wait_ge(g0_free, st.g0)
                    for b in range(B):
                        src = X[:, c, b, :] if what is L1 else Z[:, b, :]
                        ins = nc.tensor.transpose(G0[:, b * C:(b + 1) * C], src, P("ident"))
                    ins.then_inc(g0_full, 1)
                elif k == "project":
                    layer, what, turned = st.args
                    pe.wait_ge(g0_free, turned)
                    wait(pe, g1_free, st.g1)
                    parameters(f"{layer.name}w{what}")
                    mm(G1[:, :], P(f"{layer.name}w{what}"), XT[:, :]).then_inc(g1_full, 1)
                elif k == "own_values":
                    pe.wait_ge(g0_free, st.g0)
                    for b in range(B):
                        ins = mm(G0[:, b * D:(b + 1) * D], XT[:, b * C:(b + 1) * C], P("L2Swv"))
                    ins.then_inc(g0_full, 1)
                elif k == "project3":
                    c, b, half, turned = st.args
                    pe.wait_ge(g0_free, turned)
                    pe.wait_ge(g1_free, st.g1)
                    parameters("L3wq")
                    for t in range(4):
                        w = (4 * half + t) * 128
                        ins = mm(G1[:, t * C:(t + 1) * C], P("L3wq")[:, w:w + 128], XT[:, b * C:(b + 1) * C])
                    ins.then_inc(g1_full, 1)
                elif k == "keys":
                    layer = st.args[0]
                    wait(pe, operand_ready, st.op)
                    parameters(f"{layer.name}wk")
                    src = operand(layer).rearrange("p b n -> p (b n)")
                    for half in range(2):
                        wait(pe, g1_free, st.g1 + half)
                        mm(G1[:, 0:2 * KP], P(f"{layer.name}wk"), src[:, half * 2 * KP:(half + 1) * 2 * KP]).then_inc(g1_full, 1)
                elif k == "keys3":
                    pe.wait_ge(operand_ready, st.op)
                    parameters("L3wk")
                    t, half, _ = st.args
                    src = CT3[:, :, :].rearrange("p b n -> p (b n)")
                    pe.wait_ge(g1_free, st.g1)
                    mm(G1[:, 0:2 * KP], P("L3wk")[:, t * 128:(t + 1) * 128],
                       src[:, half * 2 * KP:(half + 1) * 2 * KP]).then_inc(g1_full, 1)
                elif k == "values":
                    layer, _ = st.args
                    src, w = operand(layer), P(f"{layer.name}wv")
                    wait(pe, g0_free, st.g0)
                    for b in range(B):
                        ins = mm(G0[:, b * D:(b + 1) * D], src[:, b, 0:128], w)
                    ins.then_inc(g0_full, 1)
                    pe.wait_ge(g0_free, st.g0 + 1)
                    n = layer.packs * layer.hd
                    for j in range(4):
                        wj = w.rearrange("p (k j d) -> p k j d", j=4, d=layer.hd)[:, :, j, :]
                        for b in range(B):
                            ins = mm(G0[32 * j:32 * j + 32, b * n:(b + 1) * n], src[:, b, 128:KP], wj)
                    ins.then_inc(g0_full, 1)
                elif k == "values3":
                    b, part, _ = st.args
                    w = P("L3wv")
                    pe.wait_ge(g0_free, st.g0)
                    if part < 2:
                        ins = mm(G0[:, :], CT3[:, b, 0:128], w[:, part * 512:(part + 1) * 512])
                    else:
                        for j in range(4):
                            wj = w.rearrange("p (k j d) -> p k j d", j=4, d=HS3)[:, :, j, :]
                            ins = mm(G0[32 * j:32 * j + 32, 0:256], CT3[:, b, 128:KP], wj)
                    ins.then_inc(g0_full, 1)
                elif k == "max":
                    layer, i, c, b, m, loads, g1 = st.args
                    h0, n_h = layer.max_banks(c)[m]
                    n = layer.keys(c)
                    if m == 0:
                        wait(pe, stacked, 16 * loads)
                        wait(pe, g1_free, g1)
                    wait(pe, mx_free, st.mx - 1)
                    bank = MB[st.mx % 2]
                    for h in range(h0, h0 + n_h):
                        o = (h - h0) * n
                        q = q_op(layer, i, h, b)
                        out = bank[:, o:o + n]
                        if layer.own_keys:
                            out = out.rearrange("p (c t) -> p c t", t=C)
                        ins = mm(out, q, k_op(layer, h, b, 0, n))
                        if layer.masked_block(c) is not None:
                            ins = mm(bank[:, o + n - C:o + n], K("identb"), K("mask"), start=False)
                        elif layer.masked_left(c):
                            ins = mm(bank[:, o + C:o + n], K("identb"), K("mask")[:, 0:KL], start=False)
                    ins.then_inc(mx_full, 1)
                elif k == "negmaxT":
                    i, layer, c, b = st.args
                    pe.wait_ge(consts_in, 16)
                    pe.wait_ge(nm_ready, st.nm)
                    pe.wait_ge(g1_free, st.g1)
                    mm(G1[:, 0:C], NM3[:, b % 2, :], K("identb")).then_inc(g1_full, 1)
                elif k == "score":
                    layer, i, c, b, unit, turned = st.args
                    kind, p, kb = unit
                    if unit == layer.units(c)[0]:
                        pe.wait_ge(g1_free, turned)
                    wait(pe, p_ready, st.u - 1)
                    bank = SBK[st.u % 2]
                    if kind == "left":
                        for p in range(layer.packs):
                            out = bank[:, p * C:(p + 1) * C]
                            mm(out, K("leftsel")[:, p * 128:(p + 1) * 128], negmax_turned(layer, c, b), stop=False)
                            if layer.masked_left(c):
                                mm(out, K("identb"), K("maskLT"), start=False, stop=False)
                            for j in range(4):
                                h = 4 * p + j
                                ins = mm(out[32 * j:32 * j + 32, :], k_op(layer, h, b, 128, 32),
                                         q_op(layer, i, h, b), start=False)
                    else:
                        for j in range(4):
                            h = 4 * p + j
                            out = bank[:, j * C:(j + 1) * C]
                            keys = k_op(layer, h, b, kb * C, C)
                            mm(out, keys[:, 0, :] if layer.own_keys else keys, q_op(layer, i, h, b), stop=False)
                            if layer.masked_block(c) == kb:
                                mm(out, K("identb"), K("maskT"), start=False, stop=False)
                            ins = mm(out, K("maxsel")[:, h * 128:(h + 1) * 128], negmax_turned(layer, c, b), start=False)
                    ins.then_inc(s_full, 1)
                elif k == "attend":
                    layer, c, b, p, kb, scored, opens, last, values = st.args
                    pe.wait_ge(p_ready, scored.u + 1)
                    if opens:
                        wait(pe, o_free, st.o - 1)
                        if b == 0:
                            pe.wait_ge(g0_free, values)
                    bank = OB[st.o % 2]
                    left = layer.leftover(c)
                    pr, pl = PR[:, scored.f % 3, :], PL[:, (scored.l - 1) % 2, p * C:(p + 1) * C]
                    if layer.own_keys:
                        v = VS[:, b, kb, :, :]
                    else:
                        v, vl = (t[:, b] for t in v_ops(layer))
                    if layer.wide:
                        if left:
                            mm(bank[:, 0:260], pl, vl[:, p, :], stop=False)
                        for j in range(4):
                            ins = mm(bank[:, 65 * j:65 * j + 65], pr[:, j * C:(j + 1) * C], v[:, 4 * p + j, :],
                                     start=not left)
                    else:
                        w = 2 * layer.hd
                        out = bank[:, p * C:(p + 1) * C]
                        if left:
                            mm(out, vl[:, p, :], pl, stop=False)
                        for j in range(4):
                            ins = mm(out[32 * j:32 * j + w, :], v[:, 4 * p + j, :], pr[:, j * C:(j + 1) * C],
                                     start=not left and kb == 0, stop=last)
                    ins.then_inc(pv_done, 1)
                elif k == "attended1":
                    layer, b = st.args
                    pe.wait_ge(o_free, st.o)
                    pe.wait_ge(g0_free, st.g0)
                    for p in range(layer.packs):
                        ins = nc.tensor.transpose(G0[:, p * 128:(p + 1) * 128],
                                                  OS[:, (st.o - 1) % 2, p * C:(p + 1) * C], P("ident"))
                    ins.then_inc(g0_full, 1)
                elif k == "attended2":
                    layer, b = st.args
                    pe.wait_ge(g0_free, st.g0)
                    pe.wait_ge(g1_free, st.g1)
                    nc.tensor.transpose(G1[:, 0:C], CTK[:, b % 2, :], P("ident")).then_inc(g1_full, 1)
                elif k == "back":
                    layer, c = st.args
                    pe.wait_ge(g1_free, st.g1)
                    pe.wait_ge(g0_free, st.g0)
                    for b in range(B):
                        ins = mm(G0[:, b * D:(b + 1) * D], CXT[:, b * C:(b + 1) * C], P(f"{layer.name}wo"))
                    ins.then_inc(g0_full, 1)
                elif k == "u1":
                    pe.wait_ge(g0_free, st.args[0])
                    pe.wait_ge(g1_free, st.g1)
                    mm(G1[:, :], P("L0win"), XT[:, :]).then_inc(g1_full, 1)
                elif k == "u2":
                    pe.wait_ge(g1_free, st.g1)
                    pe.wait_ge(g0_free, st.g0)
                    mm(G0[0:S, :], P("L0bmat"), QF[:, 0:TOK]).then_inc(g0_full, 1)
                elif k == "scan":
                    t = st.args[0]
                    c, col = divmod(t - 1, C)
                    for chunk in [0] * (t == 1) + [c + 1] * (col == C // 2 and c + 1 < NCH):
                        pe.wait_ge(p_ready, st.u)
                        pe.wait_ge(g0_free, st.g0)
                        pe.wait_ge(fills, 1)
                        mm(SBK[chunk % 2][0:S, :], P("L0at")[0:S, :],
                           UT[0:S, chunk * C:(chunk + 1) * C, :].rearrange("p t b -> p (t b)"), stop=False)
                    if t > 1:
                        pe.wait_ge(silu_ready, t - 1)
                    mm(SBK[c % 2][0:S, col * B:(col + 1) * B], P("L0at")[0:S, :], ZT[0:S, t - 1, :],
                       start=False).then_inc(y_ready, 1)
                elif k == "state_out":
                    c = st.args[0]
                    pe.wait_ge(states_ready, c + 1)
                    pe.wait_ge(g0_free, st.g0)
                    for b in range(B):
                        ins = mm(G0[:, b * D:(b + 1) * D], SS[:, b, c * C:(c + 1) * C], P("L0cp"))
                    ins.then_inc(g0_full, 1)
                elif k == "mlp1":
                    pe.wait_ge(g0_free, st.args[1])
                    for j in range(4):
                        pe.wait_ge(g1_free, st.g1 + j)
                        mm(G1[:, :], P("fc1")[:, j * 128:(j + 1) * 128], XT[:, :]).then_inc(g1_full, 1)
                elif k == "mlp2":
                    c = st.args[0]
                    pe.wait_ge(g1_free, st.g1)
                    pe.wait_ge(g0_free, st.g0)
                    for b in range(B):
                        for j in range(4):
                            ins = mm(G0[:, b * D:(b + 1) * D], HT[:, j, b * C:(b + 1) * C],
                                     P("fc2")[:, j * 128:(j + 1) * 128], start=j == 0, stop=j == 3)
                    ins.then_inc(g0_full, 1)
                elif k == "turn3":
                    b, half, packs = st.args
                    pe.wait_ge(o_free, packs)
                    pe.wait_ge(g0_free, st.g0)
                    for t in range(4):
                        ins = nc.tensor.transpose(G0[:, t * C:(t + 1) * C],
                                                  CTX3[:, (4 * half + t) * 128:(4 * half + t + 1) * 128], P("ident"))
                    ins.then_inc(g0_full, 1)
                elif k == "out3":
                    c, b = st.args
                    pe.wait_ge(g0_free, st.g0)
                    for t in range(8):
                        ins = mm(G0[:, 0:D], C3T[:, t, :], P("L3wo")[:, t * 128:(t + 1) * 128], start=t == 0, stop=t == 7)
                    ins.then_inc(g0_full, 1)

        @block.scalar
        def _(act):
            def affine_copy(out, in_, bias=None, scale=1.0):
                if bias is None:
                    return nc.scalar.activation(out, in_, ACT.Copy, scale=scale)
                return nc.scalar.activation(out, in_, ACT.Identity, bias=bias, scale=scale)

            act.wait_ge(par_in[0], 16)
            for st in plan:
                k = st.kind
                if k == "project":
                    layer, what, _ = st.args
                    act.wait_ge(g1_full, st.g1 + 1)
                    wait(act, split_ready, st.sp)
                    wait(act, g0_full, st.g0)
                    bias = None
                    if layer is L0:
                        act.wait_ge(bias_ready, 1)
                        bias = SB[:, 0:1]
                    elif layer is L1:
                        act.wait_ge(bias_ready, 1)
                        bias = SB[:, 1:2]
                    affine_copy(QF[:, 0:TOK], G1[:, :], bias, float(layer.hd) ** -0.5 if what == "q" else 1.0)\
                        .then_inc(g1_free, 1)
                elif k == "project3":
                    c, b, half, _ = st.args
                    act.wait_ge(bias_ready, 2)
                    act.wait_ge(g1_full, st.g1 + 1)
                    for t in range(4):
                        u = 4 * half + t
                        ins = affine_copy(Q3[:, u, b * C:(b + 1) * C], G1[:, t * C:(t + 1) * C],
                                          SB[:, 2 + u:3 + u], HS3 ** -0.5)
                    ins.then_inc(g1_free, 1)
                elif k == "keys":
                    layer = st.args[0]
                    wait(act, split_ready, st.sp)
                    wait(act, g0_full, st.g0)
                    for half in range(2):
                        act.wait_ge(g1_full, st.g1 + half + 1)
                        affine_copy(QF[:, half * 2 * KP:(half + 1) * 2 * KP], G1[:, 0:2 * KP],
                                    None if layer is L2X else P(f"{layer.name}bk")).then_inc(g1_free, 1)
                elif k == "keys3":
                    t, half, filled = st.args
                    act.wait_ge(fills, filled)
                    act.wait_ge(par_in[2], 16)
                    act.wait_ge(g1_full, st.g1 + 1)
                    cols = slice(half * 2 * KP, (half + 1) * 2 * KP)
                    affine_copy(K3[0:64, 2 * t, cols], G1[0:64, 0:2 * KP], P("L3bk")[0:64, t:t + 1])
                    affine_copy(K3[64:128, 2 * t + 1, cols], G1[64:128, 0:2 * KP], P("L3bk")[64:128, t:t + 1])\
                        .then_inc(g1_free, 1)
                elif k == "negmaxT":
                    i, layer, c, b = st.args
                    act.wait_ge(g1_full, st.g1 + 1)
                    affine_copy(negmax_turned(layer, c, b), G1[:, 0:C]).then_inc(g1_free, 1)
                elif k == "score":
                    layer, i, c, b, unit, _ = st.args
                    act.wait_ge(s_full, st.u + 1)
                    if unit[0] == "left":
                        wait(act, pv_done, st.f - layer.packs)
                        w = layer.packs * C
                        out = PL[:, st.l % 2, 0:w]
                    else:
                        wait(act, pv_done, st.f - 2)
                        w = 512
                        out = PR[:, st.f % 3, :]
                    nc.scalar.activation(out, SBK[st.u % 2][:, 0:w], ACT.Exp).then_inc(p_ready, 1)
                elif k == "attended0":
                    layer, closed = st.args
                    act.wait_ge(pv_done, closed)
                    w = layer.packs * C
                    affine_copy(OS[:, (st.o - 1) % 2, 0:w], OB[(st.o - 1) % 2][:, 0:w]).then_inc(o_free, 1)
                elif k == "attended2":
                    layer, b = st.args
                    act.wait_ge(g1_full, st.g1 + 1)
                    bias = P(f"{layer.name}bv") if layer in (L0, L1) else None
                    affine_copy(CXT[:, b * C:(b + 1) * C], G1[:, 0:C], bias).then_inc(g1_free, 1)
                elif k == "u1":
                    act.wait_ge(g1_full, st.g1 + 1)
                    act.wait_ge(split_ready, st.sp)
                    act.wait_ge(g0_full, st.g0)
                    affine_copy(QF[:, 0:TOK], G1[:, :], P("L0bin")).then_inc(g1_free, 1)
                elif k == "scan":
                    t = st.args[0]
                    c, col = divmod(t - 1, C)
                    act.wait_ge(y_ready, t)
                    nc.scalar.activation(ZT[0:S, t, :], SBK[c % 2][0:S, col * B:(col + 1) * B], ACT.Silu)\
                        .then_inc(silu_ready, 1)
                elif k == "mlp1":
                    c = st.args[0]
                    act.wait_ge(g0_full, st.g0)
                    for j in range(4):
                        act.wait_ge(g1_full, st.g1 + j + 1)
                        nc.scalar.activation(HT[:, j, :], G1[:, :], ACT.Gelu, bias=P("bfc1")[:, j:j + 1])\
                            .then_inc(g1_free, 1)

        @block.vector
        def _(dve):
            steps = [0]

            def link(ins):
                steps[0] += 1
                ins.then_inc(dve_step, 1)
                dve.wait_ge(dve_step, steps[0])

            def over_batches(row):
                return row.unsqueeze(1).broadcast_to([128, B, D])

            def split3(parts, x, rest):
                link(nc.vector.tensor_copy(parts[0], x))
                link(nc.vector.tensor_tensor(rest, x, parts[0], ALU.subtract))
                link(nc.vector.tensor_copy(parts[1], rest))
                return nc.vector.tensor_tensor(parts[2], rest, parts[1], ALU.subtract)

            for st in plan:
                k = st.kind
                if k == "biases":
                    dve.wait_ge(par_in[0], 16)
                    nc.vector.tensor_scalar(SB[:, 1:2], P("L1bq"), L1.hd ** -0.5, None, ALU.mult)
                    nc.vector.tensor_scalar(SB[:, 0:1], P("L0bq"), L0.hd ** -0.5, None, ALU.mult).then_inc(bias_ready, 1)
                elif k == "probs":
                    dve.wait_ge(early_in[2], 16)
                    link(nc.vector.tensor_reduce(PM[S:128, :], early("probs")[S:128, :, :], AXX, ALU.add))
                    link(nc.vector.tensor_scalar(SS[S:128, :, :], PM[S:128, :].unsqueeze(2).broadcast_to([S, B, T]),
                                                 1.0 / KV, None, ALU.mult))
                elif k == "ln":
                    what, c = st.args
                    p = 32 if what == "ctxl" else 128
                    src = X[:, c, :, :] if what == "x" else early(what)
                    if what == "x":
                        dve.wait_ge(x_in[c], 16)
                        wait(dve, x_done, st.xd)
                    else:
                        dve.wait_ge(early_in[("ctx", "ctxl").index(what)], 16)
                    wait(dve, z_ready, st.ln)
                    for b in range(B):
                        ins = nc.vector.bn_stats(ST[0:p, b, :], src[0:p, b, :])
                    link(ins)
                    for b in range(B):
                        ins = nc.vector.bn_aggr(MV[0:p, b, :], ST[0:p, b, :])
                    link(ins)
                    nc.vector.tensor_scalar(RS[0:p, 0, :], MV[0:p, :, 1], EPS, None, ALU.add).then_inc(var_ready, 1)
                elif k == "norm":
                    what, c = st.args
                    p = 32 if what == "ctxl" else 128
                    src = X[:, c, :, :] if what == "x" else early(what)
                    dve.wait_ge(rstd_ready, st.ln + 1)
                    wait(dve, g0_full, st.g0)
                    for b in range(B):
                        ins = nc.vector.tensor_scalar(Z[0:p, b, :], src[0:p, b, :], MV[0:p, b, 0:1], RS[0:p, 1, b:b + 1],
                                                      ALU.subtract, ALU.mult)
                    ins.then_inc(z_ready, 1)
                elif k == "ctx_turn":
                    dve.wait_ge(g0_full, st.g0 + 1)
                    n, o = (32, 128) if st.args[0] else (128, 0)
                    nc.vector.tensor_copy(ZC[:, :, o:o + n], G0[:, 0:B * n].rearrange("p (b n) -> p b n", b=B))\
                        .then_inc(g0_free, 1)
                elif k == "operand":
                    layer = st.args[0]
                    g, be = ("L0g1", "L0be1") if layer is L0 else ("L3g", "L3b")
                    dve.wait_ge(g0_free, st.g0)
                    dve.wait_ge(par_in[group(g)], 16)
                    if layer is L3:
                        for t in range(8):
                            ins = nc.vector.tensor_scalar(SB[:, 2 + t:3 + t], P("L3bq")[:, t:t + 1], HS3 ** -0.5, None, ALU.mult)
                        ins.then_inc(bias_ready, 1)
                    nc.vector.tensor_scalar((CT0 if layer is L0 else CT3)[:, :, :], ZC[:, :, :], P(g), P(be), ALU.mult, ALU.add).then_inc(operand_ready, 1)
                elif k == "turn":
                    what, c = st.args
                    dve.wait_ge(g0_full, st.g0 + 1)
                    wait(dve, g1_full, st.g1)
                    if what is L1:
                        nc.vector.tensor_copy(XT[:, :], G0[:, :]).then_inc(g0_free, 1)
                    else:
                        g, be = {L0: ("L0g1", "L0be1"), "u": ("L0g2", "L0be2"), L2S: ("L2g1", "L2b1"),
                                 L2X: ("L2g2", "L2b2"), "mlp": ("L2g3", "L2b3"), L3: ("L3g", "L3b")}[what]
                        nc.vector.tensor_scalar(XT[:, :], G0[:, :], P(g), P(be), ALU.mult, ALU.add).then_inc(g0_free, 1)
                elif k == "own_values":
                    c, filled, _ = st.args
                    dve.wait_ge(g0_full, st.g0 + 1)
                    dve.wait_ge(fills, filled)
                    nc.vector.tensor_copy(VS[:, :, c, :, 0:8], G0[:, :].rearrange("p (b h n) -> p b h n", b=B, h=16))\
                        .then_inc(g0_free, 1)
                elif k == "values":
                    layer, filled = st.args
                    v, vl = v_ops(layer)
                    hd, n = layer.hd, layer.packs * layer.hd
                    dve.wait_ge(fills, filled)
                    wait(dve, pv_done, last_use(layer))
                    dve.wait_ge(g0_full, st.g0 + 1)
                    nc.vector.tensor_copy(v[:, :, :, 0:hd], G0[:, :].rearrange("p (b h n) -> p b h n", b=B, n=hd))\
                        .then_inc(g0_free, 1)
                    dve.wait_ge(g0_full, st.g0 + 2)
                    for j in range(4):
                        r = slice(32 * j, 32 * j + KL)
                        ins = nc.vector.tensor_copy(vl[r, :, :, 32 * j:32 * j + hd],
                                                    G0[r, 0:B * n].rearrange("p (b k n) -> p b k n", b=B, n=hd))
                    ins.then_inc(g0_free, 1)
                elif k == "values3":
                    b, part, filled = st.args
                    dve.wait_ge(fills, filled)
                    dve.wait_ge(g0_full, st.g0 + 1)
                    if part < 2:
                        ins = nc.vector.tensor_copy(V3[:, b, 8 * part:8 * part + 8, 0:HS3],
                                                    G0[:, :].rearrange("p (h n) -> p h n", h=8))
                    else:
                        for j in range(4):
                            r = slice(32 * j, 32 * j + KL)
                            ins = nc.vector.tensor_copy(V3L[r, b, :, 65 * j:65 * j + HS3],
                                                        G0[r, 0:256].rearrange("p (k n) -> p k n", k=4))
                    ins.then_inc(g0_free, 1)
                elif k == "max":
                    layer, i, c, b, m, _, _ = st.args
                    h0, n_h = layer.max_banks(c)[m]
                    n = layer.keys(c)
                    dve.wait_ge(mx_full, st.mx + 1)
                    nc.vector.tensor_reduce(NMX[:, b % 2, h0:h0 + n_h],
                                            MB[st.mx % 2][:, 0:n_h * n].rearrange("p (h n) -> p h n", h=n_h),
                                            AXX, ALU.max, negate=True).then_inc(mx_free, 1)
                elif k == "negmax":
                    layer, b = st.args
                    dve.wait_ge(mx_free, st.mx)
                    wait(dve, fills, 1)
                    n = layer.heads
                    split3([NM3[:, b % 2, 16 * s:16 * s + n] for s in range(3)], NMX[:, b % 2, 0:n], NMR[:, 0:n])\
                        .then_inc(nm_ready, 1)
                elif k == "attended1":
                    layer, b = st.args
                    hd, n = layer.hd, layer.heads
                    dve.wait_ge(g0_full, st.g0 + 1)
                    w = G0[:, 0:n * 32].rearrange("p (h n) -> p h n", n=32)
                    link(nc.vector.reciprocal(REC[:, 0:n], w[:, :, hd]))
                    nc.vector.tensor_tensor(CTK[:, b % 2, :].rearrange("p (h n) -> p h n", n=hd), w[:, :, 0:hd],
                                            REC[:, 0:n].unsqueeze(2).broadcast_to([128, n, hd]), ALU.mult).then_inc(g0_free, 1)
                elif k in ("back", "state_out", "mlp2"):
                    c = st.args[-1]
                    bias = {"state_out": "L0bprog", "mlp2": "bfc2"}.get(k) or f"{st.args[0].name}bo"
                    dve.wait_ge(g0_full, st.g0 + 1)
                    nc.vector.tensor_tensor(X[:, c, :, :], G0[:, :].rearrange("p (b n) -> p b n", b=B), X[:, c, :, :], ALU.add)\
                        .then_inc(g0_free, 1)
                    dve.wait_ge(g0_free, st.g0 + 1)
                    nc.vector.tensor_tensor(X[:, c, :, :], X[:, c, :, :], over_batches(P(bias)), ALU.add).then_inc(x_done, 1)
                elif k == "affine":
                    c = st.args[0]
                    dve.wait_ge(z_ready, st.ln)
                    link(nc.vector.tensor_tensor(X[:, c, :, :], Z[:, :, :], over_batches(P("L1g")), ALU.mult))
                    nc.vector.tensor_tensor(X[:, c, :, :], X[:, c, :, :], over_batches(P("L1b")), ALU.add).then_inc(x_done, 1)
                elif k == "u2":
                    c = st.args[0]
                    dve.wait_ge(g0_full, st.g0 + 1)
                    nc.vector.tensor_copy(UT[0:S, c * C:(c + 1) * C, :].rearrange("p t b -> p b t"),
                                          G0[0:S, :].rearrange("p (b t) -> p b t", b=B)).then_inc(g0_free, 1)
                elif k == "states":
                    c = st.args[0]
                    dve.wait_ge(g0_free, st.g0)
                    dve.wait_ge(silu_ready, (c + 1) * C - 1)
                    t = slice(c * C, (c + 1) * C)
                    nc.vector.tensor_tensor(SS[0:S, :, t].rearrange("p b t -> p t b"), ZT[0:S, t, :], UT[0:S, t, :],
                                            ALU.add).then_inc(states_ready, 1)
                elif k == "weigh3":
                    c, b, p, closed = st.args
                    dve.wait_ge(pv_done, closed)
                    if p % 2 == 0:
                        dve.wait_ge(g0_full, st.g0)
                    w = OB[(st.o - 1) % 2][:, 0:260].rearrange("p (h n) -> p h n", h=4)
                    wait(dve, o_free, st.o - 2)
                    rec = REC[:, 4 * p:4 * p + 4]
                    link(nc.vector.reciprocal(rec, w[:, :, HS3]))
                    nc.vector.tensor_tensor(CTX3[:, p * 256:(p + 1) * 256].rearrange("p (h n) -> p h n", h=4), w[:, :, 0:HS3],
                                            rec.unsqueeze(2).broadcast_to([128, 4, HS3]), ALU.mult).then_inc(o_free, 1)
                elif k == "turn3":
                    b, half, _ = st.args
                    dve.wait_ge(g0_full, st.g0 + 1)
                    nc.vector.tensor_tensor(C3T[:, 4 * half:4 * half + 4, :], G0[:, :].rearrange("p (t n) -> p t n", t=4),
                                            P("L3bv")[:, 4 * half:4 * half + 4].unsqueeze(2).broadcast_to([128, 4, C]),
                                            ALU.add).then_inc(g0_free, 1)
                elif k == "out3":
                    c, b = st.args
                    dve.wait_ge(g0_full, st.g0 + 1)
                    nc.vector.tensor_tensor(X[:, c, b, :], G0[:, 0:D], X[:, c, b, :], ALU.add).then_inc(g0_free, 1)
                    dve.wait_ge(g0_free, st.g0 + 1)
                    nc.vector.tensor_tensor(X[:, c, b, :], X[:, c, b, :], P("L3bo"), ALU.add).then_inc(x_done, 1)


def kernel(**inputs):
    import concourse.bacc as bacc
    from concourse.bass_utils import run_bass_kernel_spmd

    a = {n: np.asarray(v) for n, v in inputs.items()}
    f32 = np.float32

    def column(v):
        return np.ascontiguousarray(v.reshape(-1, 128).T)

    def row(v):
        return np.broadcast_to(v[None, :], (128, v.shape[0]))

    def cut(w, n):
        return [p.T for p in np.split(w, n, axis=0)]

    def low(v):
        return np.concatenate([v, np.zeros((128 - v.shape[0],) + v.shape[1:], f32)], axis=0)

    ctx = a["ctx_1024"]
    padded = np.concatenate([ctx, np.repeat(ctx[:, -1:], KP - KV, axis=1)], axis=1)
    w = {"ident": np.eye(128, dtype=f32),
         "ctxT": padded.transpose(2, 0, 1).reshape(D, B * KP),
         "ctx": padded[:, 0:128].transpose(1, 0, 2).reshape(128, B * D),
         "ctxl": low(padded[:, 128:].transpose(1, 0, 2).reshape(KP - 128, B * D)),
         "probs": np.concatenate([np.zeros((S, B * KV), f32),
                                  a["ctxb_2048x64"].transpose(2, 0, 1).reshape(S, B * KV)], axis=0)}
    l0 = lambda n: a["L0_xattn_" + n]
    w["L0wq"], w["L0wk"], w["L0wv"] = cut(l0("W_qkv"), 3)
    w["L0bq"], w["L0bk"], w["L0bv"] = (column(v) for v in np.split(l0("b_qkv"), 3))
    w["L0wo"], w["L0bo"] = l0("W_o").T, row(l0("b_o"))
    w["L0g1"], w["L0be1"], w["L0g2"], w["L0be2"] = (column(l0(n)) for n in ("g1", "beta1", "g2", "beta2"))
    w["L0win"], w["L0bin"] = l0("W_in").T, column(l0("b_in"))
    w["L0bmat"], w["L0at"] = l0("Bmat"), low(l0("A").T)
    w["L0cp"] = np.concatenate([l0("Cmat"), l0("W_prog").T], axis=0)
    w["L0bprog"] = row(l0("b_prog"))
    l1 = lambda n: a["L1_xattn_" + n]
    w["L1wq"], w["L1wk"], w["L1wv"] = cut(l1("W_qkv"), 3)
    w["L1bq"], w["L1bk"], w["L1bv"] = (column(v) for v in np.split(l1("b_qkv"), 3))
    w["L1wo"], w["L1bo"] = l1("W_o").T, row(l1("b_o"))
    w["L1g"], w["L1b"] = row(l1("ln_gamma")), row(l1("ln_beta"))
    l2 = lambda n: a["L2_xattn_" + n]
    for n in (1, 2, 3):
        w[f"L2g{n}"], w[f"L2b{n}"] = column(l2(f"ln{n}_g")), column(l2(f"ln{n}_b"))
    w["L2Swq"], w["L2Swk"], w["L2Swv"] = cut(l2("w_qkv"), 3)
    w["L2Swo"], w["L2Sbo"] = l2("w_prj1").T, row(l2("b_prj1"))
    w["L2Xwq"] = l2("w_q").T
    w["L2Xwk"], w["L2Xwv"] = cut(l2("w_kv"), 2)
    w["L2Xwo"], w["L2Xbo"] = l2("w_prj2").T, row(l2("b_prj2"))
    w["fc1"], w["bfc1"] = l2("w_fc1").T, column(l2("b_fc1"))
    w["fc2"] = np.concatenate(np.split(l2("w_fc2").T, HID // 128, axis=0), axis=1)
    w["bfc2"] = row(l2("b_fc2"))
    l3 = lambda n: a["L3_xattn_" + n]
    w["L3g"], w["L3b"] = column(l3("ln_g")), column(l3("ln_b"))
    w["L3wq"], w["L3bq"] = l3("wq"), column(l3("bq"))
    w["L3wk"], w["L3wv"] = np.split(l3("wkv"), 2, axis=1)
    w["L3bk"], w["L3bv"] = (column(v) for v in np.split(l3("bkv"), 2))
    w["L3wo"] = np.concatenate(np.split(l3("wo"), E3 // 128, axis=0), axis=1)
    w["L3bo"] = row(l3("bo"))

    def packed(names):
        for n, cols in names:
            assert w[n].shape == (128, cols), (n, w[n].shape)
        return np.ascontiguousarray(np.concatenate([w[n] for n, _ in names], axis=1))

    import ml_dtypes
    bf16 = ml_dtypes.bfloat16
    q, r = np.arange(128), np.arange(128)
    maxsel = np.zeros((128, 16, 128), f32)
    leftsel = np.zeros((128, 4, 4, 32), f32)
    for h in range(16):
        for part in range(3):
            maxsel[16 * part + h, h] = 1
            leftsel[16 * part + h, h // 4, h % 4] = 1
    later = (r[None, :] > q[:, None])
    left = (r[:, None] % 32 > q[None, :])
    consts = {"identb": np.eye(128), "maxsel": maxsel.reshape(128, -1), "leftsel": leftsel.reshape(128, -1),
              "mask": later * BIG, "maskT": later.T * BIG, "maskLT": left * BIG}
    arrays = {"x": a["x"], "early": packed(EARLY), "consts":
              np.concatenate([np.asarray(consts[n], f32) for n, _ in CONSTS], axis=1).astype(bf16)}
    arrays.update({f"params{i}": packed(g) for i, g in enumerate(PARAMS)})

    nc = bacc.Bacc("TRN2", target_bir_lowering=False, num_devices=1)
    ap = {n: nc.dram_tensor(f"in_{n}", v.shape, mybir.dt.from_np(v.dtype), kind="ExternalInput").ap()
          for n, v in arrays.items()}
    out = nc.dram_tensor("out", (B, T, D), F32, kind="ExternalOutput").ap()
    build(nc, ap["x"], ap["early"], [ap[f"params{i}"] for i in range(len(PARAMS))], ap["consts"], out)
    r = run_bass_kernel_spmd(nc, [{f"in_{n}": v for n, v in arrays.items()}], core_ids=[0])
    return r.results[0]["out"]
```

```python
from contextlib import ExitStack

import numpy as np

import concourse.bass as bass
from concourse import mybir

F32 = mybir.dt.float32
BF16 = mybir.dt.bfloat16
ACT = mybir.ActivationFunctionType
ALU = mybir.AluOpType
AXX = mybir.AxisListType.X

B, T, D = 4, 512, 128
KV, KP = 154, 160
KL = KV - 128
C = 128
NCH = T // C
TOK = B * C
S = 64
HID = 512
EPS = 1e-5
HS3 = 64
E3 = 1024
BIG = -1.0e38
QPART = (0, 0, 0, 1, 1, 2)
KPART = (0, 1, 2, 0, 1, 0)
RUNS = ((0, 3), (3, 5), (5, 6))
PAUSE = 1
TURN_EARLY = 9
EXTRA_SLOT = NCH + 2
NAHEAD = 3


class Layer:

    def __init__(self, name, heads, hd, own_keys=False, causal=False):
        self.name, self.heads, self.hd = name, heads, hd
        self.own_keys, self.causal = own_keys, causal
        self.packs = heads // 4
        self.wide = hd == HS3
        self.per_tile = 1 if hd == 16 else 2

    def leftover(self, c):
        return not self.own_keys and not (self.causal and c == 0)

    def units(self, c):
        out = [("left", 0, 0)] if self.leftover(c) else []
        blocks = range(c + 1) if self.own_keys else range(1)
        return out + [("full", p, k) for p in range(self.packs) for k in blocks]

    def max_banks(self, c):
        n = self.keys(c)
        per = min(512 // n, self.heads)
        return [(h, min(per, self.heads - h)) for h in range(0, self.heads, per)]

    def keys(self, c):
        if self.own_keys:
            return (c + 1) * C
        return KV if self.leftover(c) else C

    def masked_block(self, c):
        if not self.causal:
            return None
        if self.own_keys:
            return c
        return 0 if c == 0 else None

    def masked_left(self, c):
        return self.causal and not self.own_keys and c == 1


L0 = Layer("L0", 8, 16)
L1 = Layer("L1", 16, 8)
L2S = Layer("L2S", 16, 8, own_keys=True, causal=True)
L2X = Layer("L2X", 16, 8)
L3 = Layer("L3", 16, HS3, causal=True)
ORDER = [L0, L1, L2S, L2X, L3]
SPLIT_ON_VECTOR = (L0, L1, L2S)

PARAMS = [
    [("L1bq", 1), ("L0g1", 1), ("L0be1", 1), ("L0bq", 1), ("L0bk", 1),
     ("L0bv", 1), ("L0wq", 128), ("L0wk", 128), ("L0wv", 128), ("L0wo", 128), ("L0bo", 128),
     ("L0g2", 1), ("L0be2", 1), ("L0win", 128), ("L0bin", 1), ("L0bmat", S), ("L0at", S),
     ("L0cp", 128), ("L0bprog", 128)],
    [("ctxT", B * KP), ("L1bk", 1), ("L1bv", 1), ("L1wq", 128), ("L1wk", 128), ("L1wv", 128),
     ("L1wo", 128), ("L1bo", 128), ("L1g", 128), ("L1b", 128),
     ("L2g1", 1), ("L2b1", 1), ("L2g2", 1), ("L2b2", 1), ("L2g3", 1), ("L2b3", 1),
     ("L2Swq", 128), ("L2Swk", 128), ("L2Swv", 128), ("L2Swo", 128), ("L2Sbo", 128),
     ("L2Xwq", 128), ("L2Xwk", 128), ("L2Xwv", 128), ("L2Xwo", 128), ("L2Xbo", 128),
     ("fc1", HID), ("bfc1", HID // 128), ("fc2", HID), ("bfc2", 128)],
    [("L3g", 1), ("L3b", 1), ("L3wq", E3), ("L3bq", E3 // 128), ("L3wk", E3), ("L3bk", E3 // 128),
     ("L3wv", E3), ("L3bv", E3 // 128), ("L3wo", E3), ("L3bo", 128)],
    [("ident", 128)],
]
EARLY = [("ctx", B * D), ("ctxl", B * D), ("probs", B * KV)]
CONSTS = [("identb", 128), ("maxsel", 16 * 128), ("leftsel", 4 * 128), ("mask", 128), ("maskT", 128), ("maskLT", 128)]


def columns(group):
    at, out = 0, {}
    for name, n in group:
        out[name] = (at, n)
        at += n
    return out, at


class Step:

    def __init__(self, kind, args, g0, g1, mx, u, f, l, o, nm, sp, ld, ln, xd, fi, op):
        self.kind, self.args = kind, args
        self.g0, self.g1, self.mx, self.u, self.f, self.l, self.o = g0, g1, mx, u, f, l, o
        self.nm, self.sp, self.ld, self.ln, self.xd, self.fi, self.op = nm, sp, ld, ln, xd, fi, op


def make_plan():
    count = dict.fromkeys("g0 g1 mx u f l o nm sp ld ln xd fi op".split(), 0)
    plan = []
    ended = {}
    closed = [0]
    needs = {}
    fill_no = {}
    todo, urgent = [], []

    def add(kind, *args, **events):
        plan.append(Step(kind, args, **count))
        for k, n in events.items():
            count[k] += n

    def later(kind, *args, **events):
        return lambda: add(kind, *args, **events)

    def pieces(kind, args, n, **events):
        def piece(k):
            add(kind, *(args() if callable(args) else args), k, n, **(events if k == n - 1 else {}))
        return [lambda k=k: piece(k) for k in range(n)]

    def split(layer, what, i, fill):
        add("split", layer, what, i, fill_no[fill], sp=1, ld=layer.per_tile * len(RUNS))

    def norm(what, c):
        return [later("ln", what, c), later("norm", what, c, ln=1)]

    def turn(what, c):
        add("turn", what, c, g0=1)
        needs["turned"] = count["g0"]

    def project(layer, what, i, fill, n=1):
        def end():
            split(layer, what, i, fill)
            needs["stack", i] = count["ld"]
        *first, last = pieces("project", lambda: (layer, what, needs["turned"]), n, g1=1)
        return first + [lambda: (last(), end())]

    def own_values(i, c):
        add("own_values", c, fill_no["own values"], needs["turned"], g0=1)
        needs["values", i] = count["g0"]

    def front(i, n=1):
        layer, c = instances[i]
        out = [] if layer is L1 else norm("x", c)
        if layer is L0 and c:
            out = [out[0], None, out[1], None]
        out.append(lambda: turn(layer, c))
        if layer is not L3:
            out += project(layer, "q", i, "layer 1" if i == EXTRA_SLOT else "start", n)
        if layer.own_keys:
            pause = [None] * (PAUSE + int(c > 1))
            out += [lambda: own_values(i, c)] + pause + project(layer, "k", i, f"own keys {c}")
        return out

    def project3(c, b):
        def half(h):
            add("project3", c, b, h, needs["turned"], g1=1)
            needs["queries", c, b] = count["g1"]
        return [lambda: half(0), lambda: half(1)]

    def key_prep(layer, fill):
        def keys(half):
            add("keys", layer, half, g1=1)
            if half:
                split(layer, "k", 0, fill)
                needs["keys", layer.name] = count["ld"]
        return [lambda: keys(0), lambda: keys(1)]

    def value_prep(layer, fill):
        def values(left):
            add("values", layer, left, fill_no[fill], g0=1)
            needs["values", layer.name] = count["g0"]
        return [lambda: values(False), lambda: values(True)]

    def keys3(t, half):
        add("keys3", t, half, fill_no["layer 3"], g1=1)
        needs["keys", L3.name] = count["g1"]

    def left3(b):
        add("left3", b, needs["keys", L3.name], fi=1)
        needs["left3"] = count["fi"]

    def values3(b, part):
        add("values3", b, part, fill_no["layer 3"], g0=1)
        needs["values", L3.name] = count["g0"]

    def fill(name, pieces=1):
        def piece(k):
            add("fill", name, k, pieces, fi=int(k == pieces - 1))
            fill_no[name] = count["fi"]
        return [lambda k=k: piece(k) for k in range(pieces)]

    def mlp(c):
        return norm("x", c) + [lambda: turn("mlp", c), lambda: add("mlp1", c, needs["turned"], g0=2, g1=2), later("mlp2", c, g0=1, xd=1)]

    def back(layer, c):
        out = [later("back", layer, c, g0=1, xd=1)]
        if layer is L0 and c == 0:
            out += state_input(c, 1)
        if layer is L1:
            out += norm("x", c) + [later("affine", c, xd=1)]
        if layer is L2X:
            out += mlp(c)
        return out

    def state_input(c, n):
        return norm("x", c) + [lambda: turn("u", c)] + pieces("u1", lambda: (needs["turned"],), n, g1=1) + \
            pieces("u2", (c,), n, g0=1)

    def maxima(batch, at, n):
        i, layer, c, b = batch
        n_banks = len(layer.max_banks(c))
        for m in range(n_banks * at // n, n_banks * (at + 1) // n):
            if layer.wide:
                loads, g1 = 0, max(needs["queries", c, b], needs["keys", L3.name])
            else:
                loads, g1 = max(needs["stack", i], 0 if layer.own_keys else needs["keys", layer.name]), 0
            add("max", layer, i, c, b, m, loads, g1, mx=1)

    def negmax(batch):
        add("negmax", batch[1], batch[3], nm=1)

    def negmaxT(batch):
        add("negmaxT", *batch, g1=1)
        needs["negmax", batch[0], batch[3]] = count["g1"]

    def is_ahead(batch):
        return batch[1] is L1 and batch[2] < NAHEAD

    def attend(batch, unit, scored):
        i, layer, c, b = batch
        if unit[0] == "left":
            return
        _, p, k = unit
        last_block = k == (c if layer.own_keys else 0)
        last_pack = p == layer.packs - 1
        closes = last_block and (layer.wide or last_pack)
        opens = k == 0 and (layer.wide or p == 0)
        values = needs["values", i if layer.own_keys else layer.name]
        add("attend", layer, c, b, p, k, scored, opens, last_block, values, o=int(closes))
        if closes:
            closed[0] = scored.f + 1
        if layer.wide:
            add("weigh3", c, b, p, closed[0])
            if p % 2:
                urgent.append(later("turn3", b, p // 2, count["o"], g0=1))
            if last_pack:
                urgent.append(later("out3", c, b, g0=1, xd=1))

    def run(first, end, tasks):
        batches = [(i, *instances[i], b) for i in range(first, end) for b in range(B)]
        if not is_ahead(batches[0]):
            maxima(batches[0], 0, 1)
            negmax(batches[0])
            negmaxT(batches[0])
        held = before = None
        for n, batch in enumerate(batches):
            i, layer, c, b = batch
            following = batches[n + 1] if n + 1 < len(batches) and not is_ahead(batches[n + 1]) else None
            todo.extend(tasks(i, b))
            units = layer.units(c)
            n_units = len(units)
            spread = max(1, n_units - (3 if n_units > 8 else 2))
            turned = needs["negmax", i, b]
            for k, unit in enumerate(units):
                turn_now = following and k == n_units - 1
                if turn_now and n_units > TURN_EARLY:
                    negmaxT(following)
                add("score", layer, i, c, b, unit, turned, needs["left3"] if layer.wide and c else 0,
                    u=1, f=int(unit[0] == "full"), l=int(unit[0] == "left"))
                scored = plan[-1]
                if turn_now and n_units <= TURN_EARLY:
                    negmaxT(following)
                if urgent:
                    urgent.pop(0)()
                if held is not None:
                    attend(*held)
                held = (batch, unit, scored)
                if following and k < spread:
                    maxima(following, k, spread)
                    if k == spread - 1:
                        negmax(following)
                if k == 0 and before and not before[1].wide:
                    add("attended0", before[1], closed[0])
                if before and not before[1].wide:
                    if k == 1:
                        add("attended1", before[1], before[3], g0=1)
                    if k == 2:
                        add("attended2", before[1], before[3], g1=1)
                        if before[3] == B - 1:
                            first, *rest = back(before[1], before[2])
                            urgent.append(first)
                            todo.extend(rest)
                slots = (B - b) * n_units - k
                held_up = (b == 0 and k == 0) or (urgent and not layer.wide)
                for _ in range(0 if held_up else min(len(todo), max(1, -(-len(todo) // slots)))):
                    step = todo.pop(0)
                    if step:
                        step()
            if b == B - 1:
                ended[i] = count["f"]
            before = batch
        attend(*held)
        i, layer, c, b = before
        if layer.wide:
            while urgent:
                urgent.pop(0)()
        else:
            add("attended0", layer, closed[0])
            add("attended1", layer, b, g0=1)
            add("attended2", layer, b, g1=1)
            todo.extend(back(layer, c))

    def flush():
        while todo:
            step = todo.pop(0)
            if step:
                step()

    instances = [(layer, c) for layer in ORDER for c in range(NCH)]
    at = {layer.name: NCH * n for n, layer in enumerate(ORDER)}
    keys_first, queries_second, the_rest = fill("start", 3)
    todo += [keys_first] + norm("ctx", 0) + [queries_second, later("ctx_turn", 0, g0=1)]
    todo += norm("ctxl", 0) + [later("ctx_turn", 1, g0=1), the_rest, later("biases"), later("operand", L0, op=1)]
    to_stats, *to_operands = front(0)
    todo += [to_stats] + key_prep(L0, "start") + to_operands + value_prep(L0, "start")
    flush()

    def tasks0(i, b):
        probs = [later("probs")] if i == 0 and b == 1 else []
        return front(i + 1) if b == 0 and i + 1 < NCH else probs

    run(0, NCH, tasks0)
    todo += fill("layer 1")
    for c in range(1, NCH):
        todo += state_input(c, 4)
    todo += key_prep(L1, "layer 1") + value_prep(L1, "layer 1")
    for c in range(NCH):
        if c:
            todo.append(later("states", c - 1))
            todo += pieces("state_out", (c - 1,), B, g0=1, xd=1)
        if 0 < c <= NAHEAD:
            i = at["L1"] + c - 1
            todo.append(None)
            for step in front(i, 4):
                todo += [step, None]
            todo += [None] * 8
            for b in range(B):
                batch = (i, L1, c - 1, b)
                banks = len(L1.max_banks(c - 1))
                todo += [lambda batch=batch, m=m, n=banks: maxima(batch, m, n) for m in range(banks)]
                todo += [lambda batch=batch: negmax(batch), None, lambda batch=batch: negmaxT(batch)]
        steps = range(max(1, c * C), (c + 1) * C)
        n_tasks, done = len(todo), 0
        for t in steps:
            add("scan", t)
            while done < n_tasks * (t - steps[0] + 1) // len(steps):
                step = todo.pop(0)
                done += 1
                if step:
                    step()
    add("states", NCH - 1)
    todo += pieces("state_out", (NCH - 1,), 1, g0=1, xd=1)
    flush()

    steps3 = [lambda t=t, half=half: keys3(t, half) for t in range(8) for half in range(2)] + \
        [lambda b=b, part=part: values3(b, part) for b in range(B) for part in range(3)]

    def tasks1(i, b):
        layer, c = instances[i]
        if i + 1 == at["L3"]:
            return front(i + 1) if b == B - 2 else steps3[(c - 1)::NCH - 1] if b == 0 else []
        if b > 0:
            return []
        out = [] if layer is L1 and c + 1 < NAHEAD else front(i + 1)
        if layer is L1 and c == 0:
            out += [later("late_params")]
        if layer is L1 and c == NCH - 2:
            out = sum([fill(f"own keys {k}") for k in range(NCH - 1)], []) + out
        if layer is L1 and c == NCH - 1:
            out = fill("own values") + out + fill(f"own keys {NCH - 1}")
        if layer is L2S and c == 1:
            out += key_prep(L2X, "layer 1") + value_prep(L2X, "layer 1")
        if layer is L2X and c == 0:
            out += fill("layer 3", 6) + [later("operand", L3, op=1)]
        if layer is L2X and c > 0:
            for n, step in enumerate(steps3[(c - 1)::NCH - 1]):
                out.insert(min(2 * n + 1, len(out)), step)
        return out

    run(at["L1"], at["L3"], tasks1)
    to_back, *last_mlp = todo
    urgent += project3(0, 0) + [to_back] + project3(0, 1)
    while urgent:
        urgent.pop(0)()
    todo.clear()

    def tasks3(i, b):
        c = instances[i][1]
        if c == 0:
            if b < 2:
                lefts = [lambda b=b: left3(b) for b in range(B)] if b == 0 else []
                for step in lefts:
                    step()
                return project3(0, b + 2) + (front(i + 1) if b == 1 else [])
            return project3(1, 0) if b == 2 else project3(1, 1) + project3(1, 2)
        out = project3(c, B - 1) if b == 0 else []
        if c == 1 and b == 0:
            out += last_mlp
        if c + 1 < NCH:
            out += front(i + 1) if b == 0 else project3(c + 1, b - 1)
        return out

    run(at["L3"], len(instances), tasks3)
    flush()
    return plan, dict(count), ended


def build(nc, x_dram, early_dram, params_dram, consts_dram, out_dram):
    plan, total, ended = make_plan()
    ctx = ExitStack()

    def sb(name, shape, dt=F32):
        return ctx.enter_context(nc.sbuf_tensor(name, shape, dt))

    def sem(name):
        return ctx.enter_context(nc.semaphore(name))

    with ctx:
        places = [columns(g) for g in PARAMS]
        shared = sb("params_0_and_2", [128, max(places[0][1], places[2][1])])
        par = [shared, sb("params_1", [128, places[1][1]]), shared, sb("params_3", [128, places[3][1]])]
        const_at, n_const = columns(CONSTS)
        con = sb("consts", [128, n_const], BF16)

        def P(name):
            for (at, _), t in zip(places, par):
                if name in at:
                    o, n = at[name]
                    return t[:, o:o + n]
            raise KeyError(name)

        def K(name):
            o, n = const_at[name]
            return con[:, o:o + n]

        X = sb("residual", [128, NCH, B, D])
        Z = sb("normed", [128, B, D])
        XT = sb("normedT", [128, TOK])
        QF = sb("projected", [128, B * KP])
        SPL = sb("parts", [128, 3, B * KP], BF16)
        QS = sb("query_stack", [128, 2, 8, TOK], BF16)
        Q3 = QS[:, :, :, :].rearrange("p a g n -> p (a g n)").bitcast(F32).rearrange("p (g n) -> p g n", g=8)
        KAW = sb("key_stack", [128, 16 * B * KP // 2])
        KA = KAW[:, :].bitcast(BF16).rearrange("p (h n) -> p h n", h=16)
        ARENA = sb("own_key_stack", [128, 16 * B * T // 2 + 64])
        QX = ARENA[:, 3 * 16 * TOK // 2:3 * 16 * TOK // 2 + 8 * TOK // 2].bitcast(BF16)
        KS = ARENA[:, 0:16 * B * T // 2].bitcast(BF16).rearrange("p (c h n) -> p c h n", c=NCH, h=16)
        K3 = ARENA[:, 0:16 * B * KP].rearrange("p (h n) -> p h n", h=16)
        V3L = ARENA[:, 16 * B * KP:16 * (B * KP + 260)].rearrange("p (b k n) -> p b k n", b=B, k=4)
        HT = ARENA[:, 16 * (B * KP + 260):16 * (B * KP + 260) + 4 * TOK].rearrange("p (j n) -> p j n", j=4)
        K3L = KAW[:, 0:B * 8 * 64].rearrange("p (b t n) -> p b t n", b=B, t=8)
        UT = ARENA[:, 0:T * B].rearrange("p (t b) -> p t b", b=B)
        ZT = ARENA[:, T * B:2 * T * B].rearrange("p (t b) -> p t b", b=B)
        SS = ARENA[:, 2 * T * B:3 * T * B].rearrange("p (b t) -> p b t", b=B)
        early_at, n_early = columns(EARLY)
        EA = ARENA[:, 3 * T * B:3 * T * B + n_early]

        def early(name):
            o, n = early_at[name]
            return EA[:, o:o + n].rearrange("p (b n) -> p b n", b=B)

        VW = sb("values", [128, B * 16 * 16 + B * 4 * 128])
        VA = VW[:, 0:B * 16 * 16].rearrange("p (b h n) -> p b h n", b=B, h=16)
        VAL = VW[:, B * 16 * 16:].rearrange("p (b k n) -> p b k n", b=B, k=4)
        CTX3 = VW[:, 0:E3]
        C3T = VW[:, E3:2 * E3].rearrange("p (t n) -> p t n", t=8)
        VAR = sb("values_arena", [128, B * 16 * 65])
        V0 = VAR[:, 0:B * 8 * 32].rearrange("p (b h n) -> p b h n", b=B, h=8)
        V0L = VAR[:, B * 8 * 32:2 * B * 8 * 32].rearrange("p (b k n) -> p b k n", b=B, k=2)
        VS = VAR[:, 0:B * NCH * 256].rearrange("p (b c h n) -> p b c h n", b=B, c=NCH, h=16)
        V3 = VAR[:, 0:B * 16 * 65].rearrange("p (b h n) -> p b h n", b=B, h=16)
        ZC = sb("normed_ctx", [128, B, KP])
        CT0, CT3 = VAR[:, 2 * B * 256:2 * B * 256 + B * KP].rearrange("p (b n) -> p b n", b=B), ZC
        PR = sb("probs", [128, 3, 512])
        PL = sb("probs_left", [128, 2, 512])
        OS = sb("attended", [128, 2, 512])
        CTK = sb("attended_tok", [128, 2, D])
        CXT = sb("attendedT", [128, TOK])
        NMX = sb("negmax", [128, 2, 16])
        NMR = sb("negmax_rest", [128, 16])
        NM3 = sb("negmax_parts", [128, 2, 128], BF16)
        NMTA = VAR[:, 3072:3072 + NAHEAD * B * C // 2].bitcast(BF16).rearrange("p (k n) -> p k n", n=C)
        NMT = sb("negmaxT", [128, 2, 128], BF16)
        REC = sb("reciprocals", [128, 16])
        ST = sb("stats", [128, B, 6])
        MV = sb("mean_var", [128, B, 2])
        RS = sb("rstd", [128, 3, B])
        PM = sb("probs_sum", [128, B])
        SB = sb("scaled_bias", [128, 16])
        parts_dram = nc.dram_tensor("parts_dram", [3, 128, B * KP], BF16).ap()

        banks = [ctx.enter_context(nc.psum_tensor(f"bank{i}", [128, 512], F32)) for i in range(8)]
        MB, SBK, OB, G0, G1 = banks[0:2], banks[2:4], banks[4:6], banks[6], banks[7]

        early_in = [sem(f"{name}_loaded") for name, _ in EARLY]
        consts_in, x_in = sem("consts_loaded"), [sem(f"x_loaded{c}") for c in range(NCH)]
        par_in = [sem(f"params_loaded{i}") for i in range(len(PARAMS))]
        stored, stacked, out_done = sem("parts_stored"), sem("stack_loaded"), sem("output_stored")
        g0_full, g0_free = sem("g0_full"), sem("g0_free")
        g1_full, g1_free = sem("g1_full"), sem("g1_free")
        mx_full, mx_free = sem("max_scores_full"), sem("max_scores_free")
        nm_ready = sem("negmax_ready")
        s_full, p_ready, pv_done, o_free = sem("scores_full"), sem("probs_ready"), sem("probs_used"), sem("attended_free")
        dve_step, pool_step = sem("dve_step"), sem("pool_step")
        var_ready, rstd_ready, z_ready = sem("var_ready"), sem("rstd_ready"), sem("z_ready")
        split_ready, operand_ready, fills, x_done = sem("split_ready"), sem("operand_ready"), sem("fills"), sem("x_done")
        bias_ready = sem("scaled_bias_ready")
        au_ready, silu_ready, y_ready, states_ready = sem("au_ready"), sem("silu_ready"), sem("y_ready"), sem("states_ready")

        def wait(eng, s, n):
            if n > 0:
                eng.wait_ge(s, n)

        def group(name):
            return next(i for i, (at, _) in enumerate(places) if name in at)

        def left_keys(layer, h, b):
            return K3L[:, b, h // 2, :] if layer.wide else k_op(layer, h, b, 128, 32)

        def last_use(layer):
            return {L0: 0, L1: ended.get(NCH - 1), L2X: ended.get(2 * NCH - 1)}[layer]

        def query_slot(i):
            return QX.rearrange("p (g n) -> p g n", g=8) if i == EXTRA_SLOT else QS[:, i % 2, :, :]

        def q_op(layer, i, h, b):
            t = h // layer.per_tile
            src = Q3[:, h // 2, :] if layer.wide else query_slot(i)[:, t, :]
            return src[:, b * C:(b + 1) * C]

        def k_op(layer, h, b, lo, n):
            if layer.wide:
                return K3[:, h, b * KP + lo:b * KP + lo + n]
            if layer.own_keys:
                return KS[:, lo // C:(lo + n) // C, h % 2 * 8 + h // 2, b * C:(b + 1) * C]
            at = h % layer.per_tile * 8 + h // layer.per_tile
            return KA[:, at, b * KP + lo:b * KP + lo + n]

        def splits_on_vector(layer):
            return layer in SPLIT_ON_VECTOR

        def negmax_turned(layer, c, b):
            return NMTA[:, c * B + b, :] if layer is L1 and c < NAHEAD else NMT[:, b % 2, :]

        def v_ops(layer):
            return {L0: (V0, V0L), L1: (VA, VAL), L2X: (VA, VAL), L3: (V3, V3L)}[layer]

        block = ctx.enter_context(nc.Block())

        @block.sync
        def _(sp):
            def load_x(c):
                sp.dma_start(X[:, c, :, :], x_dram[:, c * C:(c + 1) * C, :].rearrange("b t f -> t b f")).then_inc(x_in[c], 16)

            n = B * D
            sp.dma_start(EA[:, 0:n], early_dram[:, 0:n]).then_inc(early_in[0], 16)
            sp.dma_start(EA[0:32, n:2 * n], early_dram[0:32, n:2 * n]).then_inc(early_in[1], 16)
            sp.dma_start(par[3][:, :], params_dram[3][:, :]).then_inc(par_in[3], 16)
            load_x(0)
            sp.dma_start(shared[:, 0:places[0][1]], params_dram[0][:, :]).then_inc(par_in[0], 16)
            sp.dma_start(con[:, :], consts_dram[:, :]).then_inc(consts_in, 16)
            load_x(1)
            sp.dma_start(EA[S:128, 2 * n:], early_dram[S:128, 2 * n:]).then_inc(early_in[2], 16)
            load_x(2)
            load_x(3)
            sp.dma_start(par[1][:, :], params_dram[1][:, :]).then_inc(par_in[1], 16)
            for st in plan:
                if st.kind == "split":
                    layer, what, i, filled = st.args
                    n = TOK if what == "q" or layer.own_keys else B * KP
                    rows = layer.hd
                    sp.wait_ge(split_ready, st.sp + 1)
                    wait(sp, stacked, 16 * st.ld)
                    sp.dma_start(parts_dram[:, :, 0:n].rearrange("s p n -> p s n"), SPL[:, :, 0:n]).then_inc(stored, 16)
                    sp.wait_ge(stored, 16 * (st.sp + 1))
                    sp.wait_ge(fills, filled)
                    if what == "q" and i != EXTRA_SLOT:
                        wait(sp, pv_done, ended.get(i - 2, 0))
                    elif what == "k" and not layer.own_keys:
                        wait(sp, pv_done, last_use(layer))
                    for a in range(layer.per_tile):
                        for lo, hi in RUNS:
                            p = (QPART if what == "q" else KPART)[lo]
                            part = parts_dram[p:p + (1 if what == "q" else hi - lo), :, 0:n]
                            src = part.rearrange("s (a d g) n -> a s d g n", a=layer.per_tile, d=rows)[a]
                            rest = src if what == "k" else src.broadcast_to([hi - lo] + list(src.shape)[1:])
                            p0, p1 = 64 * a + rows * lo, 64 * a + rows * hi
                            if what == "q":
                                dst = query_slot(i)[p0:p1, :, :]
                            elif layer.own_keys:
                                dst = KS[p0:p1, i % NCH, 8 * a:8 * a + 8, :]
                            else:
                                dst = KA[p0:p1, 8 * a:8 * a + 8, :]
                            sp.dma_start(dst, rest).then_inc(stacked, 16)
                elif st.kind == "late_params":
                    sp.wait_ge(x_done, st.xd)
                    sp.wait_ge(g0_full, st.g0)
                    sp.wait_ge(g1_free, st.g1)
                    sp.dma_start(shared[:, 0:places[2][1]], params_dram[2][:, :]).then_inc(par_in[2], 16)
                elif st.kind == "out3":
                    c, b = st.args
                    sp.wait_ge(x_done, st.xd + 1)
                    sp.dma_start(out_dram[b, c * C:(c + 1) * C, :], X[:, c, b, :]).then_inc(out_done, 16)
            sp.wait_ge(out_done, 16 * NCH * B)

        @block.gpsimd
        def _(pool):
            steps = [0]

            def link(ins):
                steps[0] += 1
                ins.then_inc(pool_step, 1)
                pool.wait_ge(pool_step, steps[0])

            def put(out, value):
                link(nc.gpsimd.memset(out, value))

            def last_put(out, value, n):
                nc.gpsimd.memset(out, value).then_inc(fills, 1)
                pool.wait_ge(fills, n)

            def ones_left(t, at, width, stride):
                return [t[32 * j:32 * j + KL, :, :, j * stride + at:j * stride + at + width] for j in range(4)]

            for st in plan:
                if st.kind == "fill":
                    name, piece, pieces = st.args
                    n = st.fi + 1
                    if name == "start":
                        if piece == 0:
                            put(RS[:, 2, :], -0.5)
                            put(KAW[:, :], 0.0)
                        elif piece == 1:
                            put(QS[:, :, :, :].rearrange("p a g n -> p (a g n)").bitcast(F32), 0.0)
                        else:
                            put(NM3[:, :, :], 0.0)
                            put(ZT[0:S, 0, :], 0.0)
                            put(V0L[:, :, :, :], 0.0)
                            for ones in ones_left(V0L, 16, 16, 32):
                                put(ones, 1.0)
                            last_put(V0[:, :, :, 16:32], 1.0, n)
                    elif name == "layer 1":
                        pool.wait_ge(pv_done, st.f)
                        put(KAW[:, :], 0.0)
                        put(QX.bitcast(F32), 0.0)
                        put(VA[:, :, :, :], 1.0)
                        put(VAL[:, :, :, :], 0.0)
                        *some, last = ones_left(VAL, 8, 8, 32)
                        for ones in some:
                            put(ones, 1.0)
                        last_put(last, 1.0, n)
                    elif name == "own values":
                        pool.wait_ge(pv_done, ended[EXTRA_SLOT])
                        last_put(VS[:, :, :, :, 8:16].rearrange("p b c h n -> p (b c h) n"), 1.0, n)
                    elif name.startswith("own keys"):
                        if name == f"own keys {NCH - 1}":
                            pool.wait_ge(pv_done, ended[EXTRA_SLOT])
                        else:
                            pool.wait_ge(g0_full, st.g0)
                            pool.wait_ge(x_done, st.xd)
                        w, c = 16 * TOK // 2, int(name[-1])
                        last_put(ARENA[:, c * w:(c + 1) * w], 0.0, n)
                    elif name == "layer 3":
                        if piece == 0:
                            pool.wait_ge(pv_done, ended[3 * NCH - 1])
                            put(V3[:, :, :, 64:65], 1.0)
                        w = 16 * (B * KP + 260) // pieces
                        put(ARENA[:, piece * w:16 * (B * KP + 260) if piece == pieces - 1 else (piece + 1) * w], 0.0)
                        if piece == pieces - 1:
                            ones = ones_left(V3L, HS3, 1, 65)
                            for o in ones[:-1]:
                                put(o, 1.0)
                            last_put(ones[-1], 1.0, n)
                elif st.kind == "left3":
                    b, keys = st.args
                    pool.wait_ge(pv_done, ended[4 * NCH - 1])
                    pool.wait_ge(g1_free, keys)
                    nc.gpsimd.tensor_copy(K3L[:, b, :, :].rearrange("p t (a n) -> p (t a) n", a=2),
                                          K3[:, :, b * KP + 128:(b + 1) * KP]).then_inc(fills, 1)
                elif st.kind == "split" and not splits_on_vector(st.args[0]):
                    layer, what, i, _ = st.args
                    n = TOK if what == "q" or layer.own_keys else B * KP
                    hi, mid, lo = (SPL[:, s, 0:n] for s in range(3))
                    pool.wait_ge(g1_free, st.g1)
                    wait(pool, stored, 16 * st.sp)
                    link(nc.gpsimd.tensor_copy(hi, QF[:, 0:n]))
                    link(nc.gpsimd.tensor_tensor(QF[:, 0:n], QF[:, 0:n], hi, ALU.subtract))
                    link(nc.gpsimd.tensor_copy(mid, QF[:, 0:n]))
                    nc.gpsimd.tensor_tensor(lo, QF[:, 0:n], mid, ALU.subtract).then_inc(split_ready, 1)
                elif st.kind == "ln":
                    p = 32 if st.args[0] == "ctxl" else 128
                    pool.wait_ge(var_ready, st.ln + 1)
                    nc.gpsimd.tensor_tensor(RS[0:p, 1, :], RS[0:p, 0, :], RS[0:p, 2, :], ALU.pow).then_inc(rstd_ready, 1)

        @block.tensor
        def _(pe):
            def mm(out, lhsT, rhs, start=True, stop=True):
                return nc.tensor.matmul(out, lhsT, rhs, start=start, stop=stop, skip_group_check=True)

            def parameters(name):
                pe.wait_ge(par_in[group(name)], 16)

            def operand(layer):
                return P("ctxT").rearrange("p (b n) -> p b n", b=B) if layer in (L1, L2X) else CT0

            parameters("ident")
            def piece_of(width, piece, n):
                return slice(width * piece // n, width * (piece + 1) // n)

            for st in plan:
                k = st.kind
                if k == "ctx_turn":
                    pe.wait_ge(z_ready, st.ln)
                    wait(pe, g0_free, st.g0)
                    n = 32 if st.args[0] else 128
                    for b in range(B):
                        ins = nc.tensor.transpose(G0[:, b * n:(b + 1) * n], Z[0:n, b, :], P("ident")[0:n, 0:n])
                    ins.then_inc(g0_full, 1)
                elif k == "turn":
                    what, c = st.args
                    pe.wait_ge(z_ready, st.ln)
                    pe.wait_ge(x_in[c], 16)
                    wait(pe, x_done, st.xd)
                    pe.wait_ge(g0_free, st.g0)
                    for b in range(B):
                        src = X[:, c, b, :] if what is L1 else Z[:, b, :]
                        ins = nc.tensor.transpose(G0[:, b * C:(b + 1) * C], src, P("ident"))
                    ins.then_inc(g0_full, 1)
                elif k == "project":
                    layer, what, turned, piece, n = st.args
                    pe.wait_ge(g0_free, turned)
                    wait(pe, g1_free, st.g1)
                    parameters(f"{layer.name}w{what}")
                    cols = piece_of(TOK, piece, n)
                    ins = mm(G1[:, cols], P(f"{layer.name}w{what}"), XT[:, cols])
                    if piece == n - 1:
                        ins.then_inc(g1_full, 1)
                elif k == "own_values":
                    pe.wait_ge(g0_free, st.g0)
                    for b in range(B):
                        ins = mm(G0[:, b * D:(b + 1) * D], XT[:, b * C:(b + 1) * C], P("L2Swv"))
                    ins.then_inc(g0_full, 1)
                elif k == "project3":
                    c, b, half, turned = st.args
                    pe.wait_ge(g0_free, turned)
                    pe.wait_ge(g1_free, st.g1)
                    parameters("L3wq")
                    for t in range(4):
                        w = (4 * half + t) * 128
                        ins = mm(G1[:, t * C:(t + 1) * C], P("L3wq")[:, w:w + 128], XT[:, b * C:(b + 1) * C])
                    ins.then_inc(g1_full, 1)
                elif k == "keys":
                    layer, half = st.args
                    wait(pe, operand_ready, st.op)
                    parameters(f"{layer.name}wk")
                    src = operand(layer).rearrange("p b n -> p (b n)")
                    wait(pe, g1_free, st.g1)
                    mm(G1[:, 0:2 * KP], P(f"{layer.name}wk"), src[:, half * 2 * KP:(half + 1) * 2 * KP]).then_inc(g1_full, 1)
                elif k == "keys3":
                    pe.wait_ge(operand_ready, st.op)
                    parameters("L3wk")
                    t, half, _ = st.args
                    src = CT3[:, :, :].rearrange("p b n -> p (b n)")
                    pe.wait_ge(g1_free, st.g1)
                    mm(G1[:, 0:2 * KP], P("L3wk")[:, t * 128:(t + 1) * 128],
                       src[:, half * 2 * KP:(half + 1) * 2 * KP]).then_inc(g1_full, 1)
                elif k == "values":
                    layer, left, _ = st.args
                    src, w = operand(layer), P(f"{layer.name}wv")
                    wait(pe, g0_free, st.g0)
                    if not left:
                        for b in range(B):
                            ins = mm(G0[:, b * D:(b + 1) * D], src[:, b, 0:128], w)
                    else:
                        n = layer.packs * layer.hd
                        for j in range(4):
                            wj = w.rearrange("p (k j d) -> p k j d", j=4, d=layer.hd)[:, :, j, :]
                            for b in range(B):
                                ins = mm(G0[32 * j:32 * j + 32, b * n:(b + 1) * n], src[:, b, 128:KP], wj)
                    ins.then_inc(g0_full, 1)
                elif k == "values3":
                    b, part, _ = st.args
                    w = P("L3wv")
                    pe.wait_ge(g0_free, st.g0)
                    if part < 2:
                        ins = mm(G0[:, :], CT3[:, b, 0:128], w[:, part * 512:(part + 1) * 512])
                    else:
                        for j in range(4):
                            wj = w.rearrange("p (k j d) -> p k j d", j=4, d=HS3)[:, :, j, :]
                            ins = mm(G0[32 * j:32 * j + 32, 0:256], CT3[:, b, 128:KP], wj)
                    ins.then_inc(g0_full, 1)
                elif k == "max":
                    layer, i, c, b, m, loads, g1 = st.args
                    h0, n_h = layer.max_banks(c)[m]
                    n = layer.keys(c)
                    if m == 0:
                        wait(pe, stacked, 16 * loads)
                        wait(pe, g1_free, g1)
                    wait(pe, mx_free, st.mx - 1)
                    bank = MB[st.mx % 2]
                    for h in range(h0, h0 + n_h):
                        o = (h - h0) * n
                        q = q_op(layer, i, h, b)
                        out = bank[:, o:o + n]
                        if layer.own_keys:
                            out = out.rearrange("p (c t) -> p c t", t=C)
                        ins = mm(out, q, k_op(layer, h, b, 0, n))
                        if layer.masked_block(c) is not None:
                            ins = mm(bank[:, o + n - C:o + n], K("identb"), K("mask"), start=False)
                        elif layer.masked_left(c):
                            ins = mm(bank[:, o + C:o + n], K("identb"), K("mask")[:, 0:KL], start=False)
                    ins.then_inc(mx_full, 1)
                elif k == "negmaxT":
                    i, layer, c, b = st.args
                    pe.wait_ge(consts_in, 16)
                    pe.wait_ge(nm_ready, st.nm)
                    pe.wait_ge(g1_free, st.g1)
                    mm(G1[:, 0:C], NM3[:, b % 2, :], K("identb")).then_inc(g1_full, 1)
                elif k == "score":
                    layer, i, c, b, unit, turned, filled = st.args
                    kind, p, kb = unit
                    if unit == layer.units(c)[0]:
                        pe.wait_ge(g1_free, turned)
                        wait(pe, fills, filled)
                    wait(pe, p_ready, st.u - 1)
                    bank = SBK[st.u % 2]
                    if kind == "left":
                        for p in range(layer.packs):
                            out = bank[:, p * C:(p + 1) * C]
                            mm(out, K("leftsel")[:, p * 128:(p + 1) * 128], negmax_turned(layer, c, b), stop=False)
                            if layer.masked_left(c):
                                mm(out, K("identb"), K("maskLT"), start=False, stop=False)
                            together = 2 if layer.wide else 1
                            for j in range(0, 4, together):
                                h = 4 * p + j
                                ins = mm(out[32 * j:32 * (j + together), :], left_keys(layer, h, b),
                                         q_op(layer, i, h, b), start=False)
                    else:
                        for j in range(4):
                            h = 4 * p + j
                            out = bank[:, j * C:(j + 1) * C]
                            keys = k_op(layer, h, b, kb * C, C)
                            mm(out, keys[:, 0, :] if layer.own_keys else keys, q_op(layer, i, h, b), stop=False)
                            if layer.masked_block(c) == kb:
                                mm(out, K("identb"), K("maskT"), start=False, stop=False)
                            ins = mm(out, K("maxsel")[:, h * 128:(h + 1) * 128], negmax_turned(layer, c, b), start=False)
                    ins.then_inc(s_full, 1)
                elif k == "attend":
                    layer, c, b, p, kb, scored, opens, last, values = st.args
                    pe.wait_ge(p_ready, scored.u + 1)
                    if opens:
                        wait(pe, o_free, st.o - 1)
                        if b == 0:
                            pe.wait_ge(g0_free, values)
                    bank = OB[st.o % 2]
                    left = layer.leftover(c)
                    pr, pl = PR[:, scored.f % 3, :], PL[:, (scored.l - 1) % 2, p * C:(p + 1) * C]
                    if layer.own_keys:
                        v = VS[:, b, kb, :, :]
                    else:
                        v, vl = (t[:, b] for t in v_ops(layer))
                    if layer.wide:
                        if left:
                            mm(bank[:, 0:260], pl, vl[:, p, :], stop=False)
                        for j in range(4):
                            ins = mm(bank[:, 65 * j:65 * j + 65], pr[:, j * C:(j + 1) * C], v[:, 4 * p + j, :],
                                     start=not left)
                    else:
                        w = 2 * layer.hd
                        out = bank[:, p * C:(p + 1) * C]
                        if left:
                            mm(out, vl[:, p, :], pl, stop=False)
                        for j in range(4):
                            ins = mm(out[32 * j:32 * j + w, :], v[:, 4 * p + j, :], pr[:, j * C:(j + 1) * C],
                                     start=not left and kb == 0, stop=last)
                    ins.then_inc(pv_done, 1)
                elif k == "attended1":
                    layer, b = st.args
                    pe.wait_ge(o_free, st.o)
                    pe.wait_ge(g0_free, st.g0)
                    for p in range(layer.packs):
                        ins = nc.tensor.transpose(G0[:, p * 128:(p + 1) * 128],
                                                  OS[:, (st.o - 1) % 2, p * C:(p + 1) * C], P("ident"))
                    ins.then_inc(g0_full, 1)
                elif k == "attended2":
                    layer, b = st.args
                    pe.wait_ge(g0_free, st.g0)
                    pe.wait_ge(g1_free, st.g1)
                    nc.tensor.transpose(G1[:, 0:C], CTK[:, b % 2, :], P("ident")).then_inc(g1_full, 1)
                elif k == "back":
                    layer, c = st.args
                    pe.wait_ge(g1_free, st.g1)
                    pe.wait_ge(g0_free, st.g0)
                    for b in range(B):
                        ins = mm(G0[:, b * D:(b + 1) * D], CXT[:, b * C:(b + 1) * C], P(f"{layer.name}wo"))
                    ins.then_inc(g0_full, 1)
                elif k == "u1":
                    turned, piece, n = st.args
                    pe.wait_ge(g0_free, turned)
                    pe.wait_ge(g1_free, st.g1)
                    cols = piece_of(TOK, piece, n)
                    ins = mm(G1[:, cols], P("L0win"), XT[:, cols])
                    if piece == n - 1:
                        ins.then_inc(g1_full, 1)
                elif k == "u2":
                    c, piece, n = st.args
                    pe.wait_ge(g1_free, st.g1)
                    pe.wait_ge(g0_free, st.g0)
                    cols = piece_of(TOK, piece, n)
                    ins = mm(G0[0:S, cols], P("L0bmat"), QF[:, cols])
                    if piece == n - 1:
                        ins.then_inc(g0_full, 1)
                elif k == "scan":
                    t = st.args[0]
                    c, col = divmod(t - 1, C)
                    for chunk in [0] * (t == 1) + [c + 1] * (col == C // 2 and c + 1 < NCH):
                        pe.wait_ge(p_ready, st.u)
                        pe.wait_ge(g0_free, st.g0)
                        pe.wait_ge(fills, 1)
                        mm(SBK[chunk % 2][0:S, :], P("L0at")[0:S, :],
                           UT[0:S, chunk * C:(chunk + 1) * C, :].rearrange("p t b -> p (t b)"), stop=False)
                    if t > 1:
                        pe.wait_ge(silu_ready, t - 1)
                    mm(SBK[c % 2][0:S, col * B:(col + 1) * B], P("L0at")[0:S, :], ZT[0:S, t - 1, :],
                       start=False).then_inc(y_ready, 1)
                elif k == "state_out":
                    c, piece, n = st.args
                    pe.wait_ge(states_ready, c + 1)
                    pe.wait_ge(g0_free, st.g0)
                    for b in range(B * piece // n, B * (piece + 1) // n):
                        ins = mm(G0[:, b * D:(b + 1) * D], SS[:, b, c * C:(c + 1) * C], P("L0cp"))
                    if piece == n - 1:
                        ins.then_inc(g0_full, 1)
                elif k == "mlp1":
                    pe.wait_ge(g0_free, st.args[1])
                    for j in range(0, 4, 2):
                        pe.wait_ge(g1_free, st.g1 + j // 2)
                        mm(G1[:, :], P("fc1")[:, j * 128:(j + 1) * 128], XT[:, :]).then_inc(g1_full, 1)
                        pe.wait_ge(g0_free, st.g0 + j // 2)
                        mm(G0[:, :], P("fc1")[:, (j + 1) * 128:(j + 2) * 128], XT[:, :]).then_inc(g0_full, 1)
                elif k == "mlp2":
                    c = st.args[0]
                    pe.wait_ge(g1_free, st.g1)
                    pe.wait_ge(g0_free, st.g0)
                    for b in range(B):
                        for j in range(4):
                            ins = mm(G0[:, b * D:(b + 1) * D], HT[:, j, b * C:(b + 1) * C],
                                     P("fc2")[:, j * 128:(j + 1) * 128], start=j == 0, stop=j == 3)
                    ins.then_inc(g0_full, 1)
                elif k == "turn3":
                    b, half, packs = st.args
                    pe.wait_ge(o_free, packs)
                    pe.wait_ge(g0_free, st.g0)
                    for t in range(4):
                        ins = nc.tensor.transpose(G0[:, t * C:(t + 1) * C],
                                                  CTX3[:, (4 * half + t) * 128:(4 * half + t + 1) * 128], P("ident"))
                    ins.then_inc(g0_full, 1)
                elif k == "out3":
                    c, b = st.args
                    pe.wait_ge(g0_free, st.g0)
                    for t in range(8):
                        ins = mm(G0[:, 0:D], C3T[:, t, :], P("L3wo")[:, t * 128:(t + 1) * 128], start=t == 0, stop=t == 7)
                    ins.then_inc(g0_full, 1)

        @block.scalar
        def _(act):
            def affine_copy(out, in_, bias=None, scale=1.0):
                if bias is None:
                    return nc.scalar.activation(out, in_, ACT.Copy, scale=scale)
                return nc.scalar.activation(out, in_, ACT.Identity, bias=bias, scale=scale)

            act.wait_ge(par_in[0], 16)
            for st in plan:
                k = st.kind
                if k in ("project", "u1") and st.args[-2] < st.args[-1] - 1:
                    continue
                if k == "project":
                    layer, what, _, _, _ = st.args
                    act.wait_ge(g1_full, st.g1 + 1)
                    wait(act, split_ready, st.sp)
                    wait(act, g0_full, st.g0)
                    bias = None
                    if layer is L0:
                        act.wait_ge(bias_ready, 1)
                        bias = SB[:, 0:1]
                    elif layer is L1:
                        act.wait_ge(bias_ready, 1)
                        bias = SB[:, 1:2]
                    affine_copy(QF[:, 0:TOK], G1[:, :], bias, float(layer.hd) ** -0.5 if what == "q" else 1.0)\
                        .then_inc(g1_free, 1)
                elif k == "project3":
                    c, b, half, _ = st.args
                    act.wait_ge(bias_ready, 2)
                    act.wait_ge(g1_full, st.g1 + 1)
                    for t in range(4):
                        u = 4 * half + t
                        ins = affine_copy(Q3[:, u, b * C:(b + 1) * C], G1[:, t * C:(t + 1) * C],
                                          SB[:, 2 + u:3 + u], HS3 ** -0.5)
                    ins.then_inc(g1_free, 1)
                elif k == "keys":
                    layer, half = st.args
                    wait(act, split_ready, st.sp)
                    wait(act, g0_full, st.g0)
                    act.wait_ge(g1_full, st.g1 + 1)
                    affine_copy(QF[:, half * 2 * KP:(half + 1) * 2 * KP], G1[:, 0:2 * KP],
                                None if layer is L2X else P(f"{layer.name}bk")).then_inc(g1_free, 1)
                elif k == "keys3":
                    t, half, filled = st.args
                    act.wait_ge(fills, filled)
                    act.wait_ge(par_in[2], 16)
                    act.wait_ge(g1_full, st.g1 + 1)
                    cols = slice(half * 2 * KP, (half + 1) * 2 * KP)
                    affine_copy(K3[0:64, 2 * t, cols], G1[0:64, 0:2 * KP], P("L3bk")[0:64, t:t + 1])
                    affine_copy(K3[64:128, 2 * t + 1, cols], G1[64:128, 0:2 * KP], P("L3bk")[64:128, t:t + 1])\
                        .then_inc(g1_free, 1)
                elif k == "negmaxT":
                    i, layer, c, b = st.args
                    act.wait_ge(g1_full, st.g1 + 1)
                    affine_copy(negmax_turned(layer, c, b), G1[:, 0:C]).then_inc(g1_free, 1)
                elif k == "score":
                    layer, i, c, b, unit, _, _ = st.args
                    act.wait_ge(s_full, st.u + 1)
                    if unit[0] == "left":
                        wait(act, pv_done, st.f - layer.packs)
                        w = layer.packs * C
                        out = PL[:, st.l % 2, 0:w]
                    else:
                        wait(act, pv_done, st.f - 2)
                        w = 512
                        out = PR[:, st.f % 3, :]
                    nc.scalar.activation(out, SBK[st.u % 2][:, 0:w], ACT.Exp).then_inc(p_ready, 1)
                elif k == "attended0":
                    layer, closed = st.args
                    act.wait_ge(pv_done, closed)
                    w = layer.packs * C
                    affine_copy(OS[:, (st.o - 1) % 2, 0:w], OB[(st.o - 1) % 2][:, 0:w]).then_inc(o_free, 1)
                elif k == "attended2":
                    layer, b = st.args
                    act.wait_ge(g1_full, st.g1 + 1)
                    bias = P(f"{layer.name}bv") if layer in (L0, L1) else None
                    affine_copy(CXT[:, b * C:(b + 1) * C], G1[:, 0:C], bias).then_inc(g1_free, 1)
                elif k == "u1":
                    act.wait_ge(g1_full, st.g1 + 1)
                    act.wait_ge(split_ready, st.sp)
                    act.wait_ge(g0_full, st.g0)
                    affine_copy(QF[:, 0:TOK], G1[:, :], P("L0bin")).then_inc(g1_free, 1)
                elif k == "scan":
                    t = st.args[0]
                    c, col = divmod(t - 1, C)
                    act.wait_ge(y_ready, t)
                    nc.scalar.activation(ZT[0:S, t, :], SBK[c % 2][0:S, col * B:(col + 1) * B], ACT.Silu)\
                        .then_inc(silu_ready, 1)
                elif k == "mlp1":
                    c = st.args[0]
                    act.wait_ge(g0_full, st.g0)
                    for j in range(0, 4, 2):
                        act.wait_ge(g1_full, st.g1 + j // 2 + 1)
                        nc.scalar.activation(HT[:, j, :], G1[:, :], ACT.Gelu, bias=P("bfc1")[:, j:j + 1])\
                            .then_inc(g1_free, 1)
                        act.wait_ge(g0_full, st.g0 + j // 2 + 1)
                        nc.scalar.activation(HT[:, j + 1, :], G0[:, :], ACT.Gelu, bias=P("bfc1")[:, j + 1:j + 2])\
                            .then_inc(g0_free, 1)

        @block.vector
        def _(dve):
            steps = [0]

            def link(ins):
                steps[0] += 1
                ins.then_inc(dve_step, 1)
                dve.wait_ge(dve_step, steps[0])

            def over_batches(row):
                return row.unsqueeze(1).broadcast_to([128, B, D])

            def split3(parts, x, rest):
                link(nc.vector.tensor_copy(parts[0], x))
                link(nc.vector.tensor_tensor(rest, x, parts[0], ALU.subtract))
                link(nc.vector.tensor_copy(parts[1], rest))
                return nc.vector.tensor_tensor(parts[2], rest, parts[1], ALU.subtract)

            for st in plan:
                k = st.kind
                if k in ("u2", "state_out") and st.args[-2] < st.args[-1] - 1:
                    continue
                if k == "biases":
                    dve.wait_ge(par_in[0], 16)
                    nc.vector.tensor_scalar(SB[:, 1:2], P("L1bq"), L1.hd ** -0.5, None, ALU.mult)
                    nc.vector.tensor_scalar(SB[:, 0:1], P("L0bq"), L0.hd ** -0.5, None, ALU.mult).then_inc(bias_ready, 1)
                elif k == "probs":
                    dve.wait_ge(early_in[2], 16)
                    link(nc.vector.tensor_reduce(PM[S:128, :], early("probs")[S:128, :, :], AXX, ALU.add))
                    link(nc.vector.tensor_scalar(SS[S:128, :, :], PM[S:128, :].unsqueeze(2).broadcast_to([S, B, T]),
                                                 1.0 / KV, None, ALU.mult))
                elif k == "ln":
                    what, c = st.args
                    p = 32 if what == "ctxl" else 128
                    src = X[:, c, :, :] if what == "x" else early(what)
                    if what == "x":
                        dve.wait_ge(x_in[c], 16)
                        wait(dve, x_done, st.xd)
                    else:
                        dve.wait_ge(early_in[("ctx", "ctxl").index(what)], 16)
                    wait(dve, z_ready, st.ln)
                    for b in range(B):
                        ins = nc.vector.bn_stats(ST[0:p, b, :], src[0:p, b, :])
                    link(ins)
                    for b in range(B):
                        ins = nc.vector.bn_aggr(MV[0:p, b, :], ST[0:p, b, :])
                    link(ins)
                    nc.vector.tensor_scalar(RS[0:p, 0, :], MV[0:p, :, 1], EPS, None, ALU.add).then_inc(var_ready, 1)
                elif k == "norm":
                    what, c = st.args
                    p = 32 if what == "ctxl" else 128
                    src = X[:, c, :, :] if what == "x" else early(what)
                    dve.wait_ge(rstd_ready, st.ln + 1)
                    wait(dve, g0_full, st.g0)
                    for b in range(B):
                        ins = nc.vector.tensor_scalar(Z[0:p, b, :], src[0:p, b, :], MV[0:p, b, 0:1], RS[0:p, 1, b:b + 1],
                                                      ALU.subtract, ALU.mult)
                    ins.then_inc(z_ready, 1)
                elif k == "ctx_turn":
                    dve.wait_ge(g0_full, st.g0 + 1)
                    n, o = (32, 128) if st.args[0] else (128, 0)
                    nc.vector.tensor_copy(ZC[:, :, o:o + n], G0[:, 0:B * n].rearrange("p (b n) -> p b n", b=B))\
                        .then_inc(g0_free, 1)
                elif k == "operand":
                    layer = st.args[0]
                    g, be = ("L0g1", "L0be1") if layer is L0 else ("L3g", "L3b")
                    dve.wait_ge(g0_free, st.g0)
                    dve.wait_ge(par_in[group(g)], 16)
                    if layer is L3:
                        for t in range(8):
                            ins = nc.vector.tensor_scalar(SB[:, 2 + t:3 + t], P("L3bq")[:, t:t + 1], HS3 ** -0.5, None, ALU.mult)
                        ins.then_inc(bias_ready, 1)
                    nc.vector.tensor_scalar((CT0 if layer is L0 else CT3)[:, :, :], ZC[:, :, :], P(g), P(be), ALU.mult, ALU.add).then_inc(operand_ready, 1)
                elif k == "turn":
                    what, c = st.args
                    dve.wait_ge(g0_full, st.g0 + 1)
                    wait(dve, g1_full, st.g1)
                    if what is L1:
                        nc.vector.tensor_copy(XT[:, :], G0[:, :]).then_inc(g0_free, 1)
                    else:
                        g, be = {L0: ("L0g1", "L0be1"), "u": ("L0g2", "L0be2"), L2S: ("L2g1", "L2b1"),
                                 L2X: ("L2g2", "L2b2"), "mlp": ("L2g3", "L2b3"), L3: ("L3g", "L3b")}[what]
                        nc.vector.tensor_scalar(XT[:, :], G0[:, :], P(g), P(be), ALU.mult, ALU.add).then_inc(g0_free, 1)
                elif k == "split" and splits_on_vector(st.args[0]):
                    layer, what, i, _ = st.args
                    n = TOK if what == "q" or layer.own_keys else B * KP
                    dve.wait_ge(g1_free, st.g1)
                    wait(dve, stored, 16 * st.sp)
                    split3([SPL[:, s, 0:n] for s in range(3)], QF[:, 0:n], QF[:, 0:n]).then_inc(split_ready, 1)
                elif k == "own_values":
                    c, filled, _ = st.args
                    dve.wait_ge(g0_full, st.g0 + 1)
                    dve.wait_ge(fills, filled)
                    nc.vector.tensor_copy(VS[:, :, c, :, 0:8], G0[:, :].rearrange("p (b h n) -> p b h n", b=B, h=16))\
                        .then_inc(g0_free, 1)
                elif k == "values":
                    layer, left, filled = st.args
                    v, vl = v_ops(layer)
                    hd, n = layer.hd, layer.packs * layer.hd
                    dve.wait_ge(fills, filled)
                    wait(dve, pv_done, last_use(layer))
                    dve.wait_ge(g0_full, st.g0 + 1)
                    if not left:
                        ins = nc.vector.tensor_copy(v[:, :, :, 0:hd], G0[:, :].rearrange("p (b h n) -> p b h n", b=B, n=hd))
                    else:
                        for j in range(4):
                            r = slice(32 * j, 32 * j + KL)
                            ins = nc.vector.tensor_copy(vl[r, :, :, 32 * j:32 * j + hd],
                                                        G0[r, 0:B * n].rearrange("p (b k n) -> p b k n", b=B, n=hd))
                    ins.then_inc(g0_free, 1)
                elif k == "values3":
                    b, part, filled = st.args
                    dve.wait_ge(fills, filled)
                    dve.wait_ge(g0_full, st.g0 + 1)
                    if part < 2:
                        ins = nc.vector.tensor_copy(V3[:, b, 8 * part:8 * part + 8, 0:HS3],
                                                    G0[:, :].rearrange("p (h n) -> p h n", h=8))
                    else:
                        for j in range(4):
                            r = slice(32 * j, 32 * j + KL)
                            ins = nc.vector.tensor_copy(V3L[r, b, :, 65 * j:65 * j + HS3],
                                                        G0[r, 0:256].rearrange("p (k n) -> p k n", k=4))
                    ins.then_inc(g0_free, 1)
                elif k == "max":
                    layer, i, c, b, m, _, _ = st.args
                    h0, n_h = layer.max_banks(c)[m]
                    n = layer.keys(c)
                    dve.wait_ge(mx_full, st.mx + 1)
                    nc.vector.tensor_reduce(NMX[:, b % 2, h0:h0 + n_h],
                                            MB[st.mx % 2][:, 0:n_h * n].rearrange("p (h n) -> p h n", h=n_h),
                                            AXX, ALU.max, negate=True).then_inc(mx_free, 1)
                elif k == "negmax":
                    layer, b = st.args
                    dve.wait_ge(mx_free, st.mx)
                    wait(dve, fills, 1)
                    n = layer.heads
                    split3([NM3[:, b % 2, 16 * s:16 * s + n] for s in range(3)], NMX[:, b % 2, 0:n], NMR[:, 0:n])\
                        .then_inc(nm_ready, 1)
                elif k == "attended1":
                    layer, b = st.args
                    hd, n = layer.hd, layer.heads
                    dve.wait_ge(g0_full, st.g0 + 1)
                    w = G0[:, 0:n * 32].rearrange("p (h n) -> p h n", n=32)
                    link(nc.vector.reciprocal(REC[:, 0:n], w[:, :, hd]))
                    nc.vector.tensor_tensor(CTK[:, b % 2, :].rearrange("p (h n) -> p h n", n=hd), w[:, :, 0:hd],
                                            REC[:, 0:n].unsqueeze(2).broadcast_to([128, n, hd]), ALU.mult).then_inc(g0_free, 1)
                elif k in ("back", "state_out", "mlp2"):
                    c = st.args[0] if k == "state_out" else st.args[-1]
                    bias = {"state_out": "L0bprog", "mlp2": "bfc2"}.get(k) or f"{st.args[0].name}bo"
                    dve.wait_ge(g0_full, st.g0 + 1)
                    nc.vector.tensor_tensor(X[:, c, :, :], G0[:, :].rearrange("p (b n) -> p b n", b=B), X[:, c, :, :], ALU.add)\
                        .then_inc(g0_free, 1)
                    dve.wait_ge(g0_free, st.g0 + 1)
                    nc.vector.tensor_tensor(X[:, c, :, :], X[:, c, :, :], over_batches(P(bias)), ALU.add).then_inc(x_done, 1)
                elif k == "affine":
                    c = st.args[0]
                    dve.wait_ge(z_ready, st.ln)
                    link(nc.vector.tensor_tensor(X[:, c, :, :], Z[:, :, :], over_batches(P("L1g")), ALU.mult))
                    nc.vector.tensor_tensor(X[:, c, :, :], X[:, c, :, :], over_batches(P("L1b")), ALU.add).then_inc(x_done, 1)
                elif k == "u2":
                    c = st.args[0]
                    dve.wait_ge(g0_full, st.g0 + 1)
                    nc.vector.tensor_copy(UT[0:S, c * C:(c + 1) * C, :].rearrange("p t b -> p b t"),
                                          G0[0:S, :].rearrange("p (b t) -> p b t", b=B)).then_inc(g0_free, 1)
                elif k == "states":
                    c = st.args[0]
                    dve.wait_ge(g0_free, st.g0)
                    dve.wait_ge(silu_ready, (c + 1) * C - 1)
                    t = slice(c * C, (c + 1) * C)
                    nc.vector.tensor_tensor(SS[0:S, :, t].rearrange("p b t -> p t b"), ZT[0:S, t, :], UT[0:S, t, :],
                                            ALU.add).then_inc(states_ready, 1)
                elif k == "weigh3":
                    c, b, p, closed = st.args
                    dve.wait_ge(pv_done, closed)
                    if p % 2 == 0:
                        dve.wait_ge(g0_full, st.g0)
                    w = OB[(st.o - 1) % 2][:, 0:260].rearrange("p (h n) -> p h n", h=4)
                    wait(dve, o_free, st.o - 2)
                    rec = REC[:, 4 * p:4 * p + 4]
                    link(nc.vector.reciprocal(rec, w[:, :, HS3]))
                    nc.vector.tensor_tensor(CTX3[:, p * 256:(p + 1) * 256].rearrange("p (h n) -> p h n", h=4), w[:, :, 0:HS3],
                                            rec.unsqueeze(2).broadcast_to([128, 4, HS3]), ALU.mult).then_inc(o_free, 1)
                elif k == "turn3":
                    b, half, _ = st.args
                    dve.wait_ge(g0_full, st.g0 + 1)
                    nc.vector.tensor_tensor(C3T[:, 4 * half:4 * half + 4, :], G0[:, :].rearrange("p (t n) -> p t n", t=4),
                                            P("L3bv")[:, 4 * half:4 * half + 4].unsqueeze(2).broadcast_to([128, 4, C]),
                                            ALU.add).then_inc(g0_free, 1)
                elif k == "out3":
                    c, b = st.args
                    dve.wait_ge(g0_full, st.g0 + 1)
                    nc.vector.tensor_tensor(X[:, c, b, :], G0[:, 0:D], X[:, c, b, :], ALU.add).then_inc(g0_free, 1)
                    dve.wait_ge(g0_free, st.g0 + 1)
                    nc.vector.tensor_tensor(X[:, c, b, :], X[:, c, b, :], P("L3bo"), ALU.add).then_inc(x_done, 1)


def kernel(**inputs):
    import concourse.bacc as bacc
    from concourse.bass_utils import run_bass_kernel_spmd

    a = {n: np.asarray(v) for n, v in inputs.items()}
    f32 = np.float32

    def column(v):
        return np.ascontiguousarray(v.reshape(-1, 128).T)

    def row(v):
        return np.broadcast_to(v[None, :], (128, v.shape[0]))

    def cut(w, n):
        return [p.T for p in np.split(w, n, axis=0)]

    def by_feature(layer, *operands):
        order = np.arange(128).reshape(8, layer.per_tile, layer.hd).transpose(1, 2, 0).reshape(-1)
        for n in operands:
            w[f"{layer.name}w{n}"] = w[f"{layer.name}w{n}"][:, order]
            if f"{layer.name}b{n}" in w:
                w[f"{layer.name}b{n}"] = w[f"{layer.name}b{n}"][order]

    def low(v):
        return np.concatenate([v, np.zeros((128 - v.shape[0],) + v.shape[1:], f32)], axis=0)

    ctx = a["ctx_1024"]
    padded = np.concatenate([ctx, np.repeat(ctx[:, -1:], KP - KV, axis=1)], axis=1)
    w = {"ident": np.eye(128, dtype=f32),
         "ctxT": padded.transpose(2, 0, 1).reshape(D, B * KP),
         "ctx": padded[:, 0:128].transpose(1, 0, 2).reshape(128, B * D),
         "ctxl": low(padded[:, 128:].transpose(1, 0, 2).reshape(KP - 128, B * D)),
         "probs": np.concatenate([np.zeros((S, B * KV), f32),
                                  a["ctxb_2048x64"].transpose(2, 0, 1).reshape(S, B * KV)], axis=0)}
    l0 = lambda n: a["L0_xattn_" + n]
    w["L0wq"], w["L0wk"], w["L0wv"] = cut(l0("W_qkv"), 3)
    w["L0bq"], w["L0bk"], w["L0bv"] = (column(v) for v in np.split(l0("b_qkv"), 3))
    by_feature(L0, "q", "k")
    w["L0wo"], w["L0bo"] = l0("W_o").T, row(l0("b_o"))
    w["L0g1"], w["L0be1"], w["L0g2"], w["L0be2"] = (column(l0(n)) for n in ("g1", "beta1", "g2", "beta2"))
    w["L0win"], w["L0bin"] = l0("W_in").T, column(l0("b_in"))
    w["L0bmat"], w["L0at"] = l0("Bmat"), low(l0("A").T)
    w["L0cp"] = np.concatenate([l0("Cmat"), l0("W_prog").T], axis=0)
    w["L0bprog"] = row(l0("b_prog"))
    l1 = lambda n: a["L1_xattn_" + n]
    w["L1wq"], w["L1wk"], w["L1wv"] = cut(l1("W_qkv"), 3)
    w["L1bq"], w["L1bk"], w["L1bv"] = (column(v) for v in np.split(l1("b_qkv"), 3))
    by_feature(L1, "q", "k")
    w["L1wo"], w["L1bo"] = l1("W_o").T, row(l1("b_o"))
    w["L1g"], w["L1b"] = row(l1("ln_gamma")), row(l1("ln_beta"))
    l2 = lambda n: a["L2_xattn_" + n]
    for n in (1, 2, 3):
        w[f"L2g{n}"], w[f"L2b{n}"] = column(l2(f"ln{n}_g")), column(l2(f"ln{n}_b"))
    w["L2Swq"], w["L2Swk"], w["L2Swv"] = cut(l2("w_qkv"), 3)
    w["L2Swo"], w["L2Sbo"] = l2("w_prj1").T, row(l2("b_prj1"))
    w["L2Xwq"] = l2("w_q").T
    w["L2Xwk"], w["L2Xwv"] = cut(l2("w_kv"), 2)
    by_feature(L2S, "q", "k")
    by_feature(L2X, "q", "k")
    w["L2Xwo"], w["L2Xbo"] = l2("w_prj2").T, row(l2("b_prj2"))
    w["fc1"], w["bfc1"] = l2("w_fc1").T, column(l2("b_fc1"))
    w["fc2"] = np.concatenate(np.split(l2("w_fc2").T, HID // 128, axis=0), axis=1)
    w["bfc2"] = row(l2("b_fc2"))
    l3 = lambda n: a["L3_xattn_" + n]
    w["L3g"], w["L3b"] = column(l3("ln_g")), column(l3("ln_b"))
    w["L3wq"], w["L3bq"] = l3("wq"), column(l3("bq"))
    w["L3wk"], w["L3wv"] = np.split(l3("wkv"), 2, axis=1)
    w["L3bk"], w["L3bv"] = (column(v) for v in np.split(l3("bkv"), 2))
    w["L3wo"] = np.concatenate(np.split(l3("wo"), E3 // 128, axis=0), axis=1)
    w["L3bo"] = row(l3("bo"))

    def packed(names):
        for n, cols in names:
            assert w[n].shape == (128, cols), (n, w[n].shape)
        return np.ascontiguousarray(np.concatenate([w[n] for n, _ in names], axis=1))

    import ml_dtypes
    bf16 = ml_dtypes.bfloat16
    q, r = np.arange(128), np.arange(128)
    maxsel = np.zeros((128, 16, 128), f32)
    leftsel = np.zeros((128, 4, 4, 32), f32)
    for h in range(16):
        for part in range(3):
            maxsel[16 * part + h, h] = 1
            leftsel[16 * part + h, h // 4, h % 4] = 1
    later = (r[None, :] > q[:, None])
    left = (r[:, None] % 32 > q[None, :])
    consts = {"identb": np.eye(128), "maxsel": maxsel.reshape(128, -1), "leftsel": leftsel.reshape(128, -1),
              "mask": later * BIG, "maskT": later.T * BIG, "maskLT": left * BIG}
    arrays = {"x": a["x"], "early": packed(EARLY), "consts":
              np.concatenate([np.asarray(consts[n], f32) for n, _ in CONSTS], axis=1).astype(bf16)}
    arrays.update({f"params{i}": packed(g) for i, g in enumerate(PARAMS)})

    nc = bacc.Bacc("TRN2", target_bir_lowering=False, num_devices=1)
    ap = {n: nc.dram_tensor(f"in_{n}", v.shape, mybir.dt.from_np(v.dtype), kind="ExternalInput").ap()
          for n, v in arrays.items()}
    out = nc.dram_tensor("out", (B, T, D), F32, kind="ExternalOutput").ap()
    build(nc, ap["x"], ap["early"], [ap[f"params{i}"] for i in range(len(PARAMS))], ap["consts"], out)
    r = run_bass_kernel_spmd(nc, [{f"in_{n}": v for n, v in arrays.items()}], core_ids=[0])
    return r.results[0]["out"]
```
